# Optimizing a Trainium2 kernel written in Bass

```python
import numpy as np
import jax
import jax.numpy as jnp

def _softmax(x, axis=-1):
    return jax.nn.softmax(x, axis=axis)

def _gelu(x):
    return jax.nn.gelu(x, approximate=True)

def _silu(x):
    return jax.nn.silu(x)

def _sigmoid(x):
    return jax.nn.sigmoid(x)

def _layernorm(x, axis=-1, eps=1e-05):
    m = jnp.mean(x, axis=axis, keepdims=True)
    v = jnp.var(x, axis=axis, keepdims=True)
    return (x - m) / jnp.sqrt(v + eps)

def _scatter_add(tgt, idx, src, axis=0):
    return tgt.at[idx].add(src)

def _segment_sum(src, seg, n):
    return jax.ops.segment_sum(src, seg, n)
kernel_name = 'mk_vit_tower_cls_d1_tok_img1024_r4_1972a4'

def setup_inputs(seed: int=0):
    np.random.seed(seed)
    _w = jnp.asarray

    def _rec_inputs():
        import jax
        import jax.numpy as jnp
        _rk = jax.random.key(seed)
        x = 7.22013e-05 + 1.00017 * jax.random.normal(jax.random.fold_in(_rk, 1), (32, 64, 256, 4), jnp.float32)
        cls_tok = 0.02 * jax.random.normal(jax.random.fold_in(_rk, 5), (1, 1, 256), jnp.float32)
        return (x, cls_tok)
    x, cls_tok = _rec_inputs()

    def _L0_tok_setup():
        import jax, jax.numpy as jnp
        import numpy as np
        B, F, L, H, D = (8, 64, 256, 4, 64)
        MODEL = H * F
        WIN = 128

        def _local_mask():
            m = np.ones((L, L), dtype=bool)
            m = np.tril(m, WIN - 1)
            m = np.triu(m, -(WIN - 1))
            return jnp.asarray(m)

        def _flatten(y):
            n = y.shape[0]
            return y.transpose(0, 2, 3, 1).reshape(n, L, -1)
        key = jax.random.key(seed)
        ks = jax.random.split(key, 12)
        s = lambda n: 1.0 / np.sqrt(n)
        xav = np.sqrt(6.0 / (L + L))
        return {'x': jax.random.normal(ks[0], (B, F, L, H), jnp.float32), 'Wq_w': jax.random.normal(ks[1], (D, F), jnp.float32) * s(F), 'Wq_b': jnp.zeros((D,), jnp.float32), 'Wk_w': jax.random.normal(ks[2], (D, F), jnp.float32) * s(F), 'Wk_b': jnp.zeros((D,), jnp.float32), 'Wv_w': jax.random.normal(ks[3], (D, F), jnp.float32) * s(F), 'Wv_b': jnp.zeros((D,), jnp.float32), 'w_bias': jax.random.uniform(ks[4], (L, L), jnp.float32, -xav, xav), 'out_w': jax.random.normal(ks[5], (H * D, MODEL), jnp.float32) * s(H * D), 'out_b': jnp.zeros((MODEL,), jnp.float32), 'ln_g': jnp.ones((MODEL,), jnp.float32), 'ln_b': jnp.zeros((MODEL,), jnp.float32), 'local_mask': _local_mask()}
    _L0_tok_all = _L0_tok_setup()
    _L0_tok_in = {k: v for k, v in _L0_tok_all.items() if k in ('Wq_w', 'Wq_b', 'Wk_w', 'Wk_b', 'Wv_w', 'Wv_b', 'w_bias', 'out_w', 'out_b', 'ln_g', 'ln_b', 'local_mask')}
    del _L0_tok_all

    def _L0_attn_setup():
        import jax, jax.numpy as jnp
        import numpy as np
        HEADS, DK, DV = (16, 16, 64)
        EPS = 1e-12

        def l2norm(t):
            n = jnp.linalg.norm(t, axis=-1, keepdims=True)
            return t / jnp.maximum(n, EPS)

        def tanh_norm(t):
            n = jnp.linalg.norm(t, axis=-1, keepdims=True)
            return jnp.tanh(n) * (t / jnp.maximum(n, EPS))

        def split_heads(x, h):
            b, n, hd = x.shape
            return x.reshape(b, n, h, hd // h).transpose(0, 2, 1, 3)
        key = jax.random.key(seed)
        k1, k2, k3, k4 = jax.random.split(key, 4)
        b, n, dim = (2, 512, 256)
        tokens = jax.random.normal(k1, (b, n, dim), dtype=jnp.float32)
        Wq = jax.random.normal(k2, (dim, DK * HEADS), dtype=jnp.float32) * 0.02
        Wkv = jax.random.normal(k3, (dim, (DK + DV) * HEADS), dtype=jnp.float32) * 0.02
        Wout = jax.random.normal(k4, (DV * HEADS, dim), dtype=jnp.float32) * 0.02
        return {'tokens': tokens, 'Wq': Wq, 'Wkv': Wkv, 'Wout': Wout}
    _L0_attn_all = _L0_attn_setup()
    _L0_attn_in = {k: v for k, v in _L0_attn_all.items() if k in ('Wq', 'Wkv', 'Wout')}
    del _L0_attn_all

    def _L0_ffn_setup():
        import jax, jax.numpy as jnp
        import numpy as np
        EMB = 256
        HEADS = 16
        SEQ = 512
        LATENT = 128
        N_EXP = 8
        TOP_K = 2
        EXP_DIM = 512
        BATCH = 2
        EPS = 1e-06

        def _rmsnorm(x, g):
            return x * jax.lax.rsqrt(jnp.mean(x * x, axis=-1, keepdims=True) + EPS) * g

        def _mla(h, Wq, Wdkv, Wuk, Wuv, Wo):
            B, S, D = h.shape
            hd = D // HEADS
            q = (h @ Wq).reshape(B, S, HEADS, hd)
            c = h @ Wdkv
            k = (c @ Wuk).reshape(B, S, HEADS, hd)
            v = (c @ Wuv).reshape(B, S, HEADS, hd)
            scores = jnp.einsum('bqhd,bkhd->bhqk', q, k) / jnp.sqrt(jnp.asarray(hd, h.dtype))
            causal = jnp.tril(jnp.ones((S, S), bool))
            scores = jnp.where(causal, scores, jnp.asarray(-1000000000.0, h.dtype))
            a = jax.nn.softmax(scores, axis=-1)
            out = jnp.einsum('bhqk,bkhd->bqhd', a, v).reshape(B, S, D)
            return out @ Wo

        def _moe(h, gate_w, w1, w2):
            B, S, D = h.shape
            t = h.reshape(B * S, D)
            logits = t @ gate_w
            top_v, top_i = jax.lax.top_k(logits, TOP_K)
            gates = jax.nn.softmax(top_v, axis=-1)
            T = t.shape[0]
            combine = jnp.zeros((T, N_EXP), t.dtype).at[jnp.arange(T)[:, None], top_i].add(gates)
            hid = jax.nn.silu(jnp.einsum('td,edh->teh', t, w1))
            ye = jnp.einsum('teh,ehd->ted', hid, w2)
            out = jnp.einsum('te,ted->td', combine, ye)
            return out.reshape(B, S, D)
        key = jax.random.key(seed)
        ks = jax.random.split(key, 12)
        s = 0.02
        return {'x': jax.random.normal(ks[0], (BATCH, SEQ, EMB), jnp.float32), 'g1': jnp.ones((EMB,), jnp.float32), 'Wq': jax.random.normal(ks[1], (EMB, EMB), jnp.float32) * s, 'Wdkv': jax.random.normal(ks[2], (EMB, LATENT), jnp.float32) * s, 'Wuk': jax.random.normal(ks[3], (LATENT, EMB), jnp.float32) * s, 'Wuv': jax.random.normal(ks[4], (LATENT, EMB), jnp.float32) * s, 'Wo': jax.random.normal(ks[5], (EMB, EMB), jnp.float32) * s, 'g2': jnp.ones((EMB,), jnp.float32), 'gate_w': jax.random.normal(ks[6], (EMB, N_EXP), jnp.float32) * s, 'w1': jax.random.normal(ks[7], (N_EXP, EMB, EXP_DIM), jnp.float32) * s, 'w2': jax.random.normal(ks[8], (N_EXP, EXP_DIM, EMB), jnp.float32) * s}
    _L0_ffn_all = _L0_ffn_setup()
    _L0_ffn_in = {k: v for k, v in _L0_ffn_all.items() if k in ('g1', 'Wq', 'Wdkv', 'Wuk', 'Wuv', 'Wo', 'g2', 'gate_w', 'w1', 'w2')}
    del _L0_ffn_all
    return {'x': x, 'cls_tok': cls_tok, 'L0_tok_Wq_w': _L0_tok_in['Wq_w'], 'L0_tok_Wq_b': _L0_tok_in['Wq_b'], 'L0_tok_Wk_w': _L0_tok_in['Wk_w'], 'L0_tok_Wk_b': _L0_tok_in['Wk_b'], 'L0_tok_Wv_w': _L0_tok_in['Wv_w'], 'L0_tok_Wv_b': _L0_tok_in['Wv_b'], 'L0_tok_w_bias': _L0_tok_in['w_bias'], 'L0_tok_out_w': _L0_tok_in['out_w'], 'L0_tok_out_b': _L0_tok_in['out_b'], 'L0_tok_ln_g': _L0_tok_in['ln_g'], 'L0_tok_ln_b': _L0_tok_in['ln_b'], 'L0_tok_local_mask': _L0_tok_in['local_mask'], 'L0_attn_Wq': _L0_attn_in['Wq'], 'L0_attn_Wkv': _L0_attn_in['Wkv'], 'L0_attn_Wout': _L0_attn_in['Wout'], 'L0_ffn_g1': _L0_ffn_in['g1'], 'L0_ffn_Wq': _L0_ffn_in['Wq'], 'L0_ffn_Wdkv': _L0_ffn_in['Wdkv'], 'L0_ffn_Wuk': _L0_ffn_in['Wuk'], 'L0_ffn_Wuv': _L0_ffn_in['Wuv'], 'L0_ffn_Wo': _L0_ffn_in['Wo'], 'L0_ffn_g2': _L0_ffn_in['g2'], 'L0_ffn_gate_w': _L0_ffn_in['gate_w'], 'L0_ffn_w1': _L0_ffn_in['w1'], 'L0_ffn_w2': _L0_ffn_in['w2']}

def reference(x, cls_tok, L0_tok_Wq_w, L0_tok_Wq_b, L0_tok_Wk_w, L0_tok_Wk_b, L0_tok_Wv_w, L0_tok_Wv_b, L0_tok_w_bias, L0_tok_out_w, L0_tok_out_b, L0_tok_ln_g, L0_tok_ln_b, L0_tok_local_mask, L0_attn_Wq, L0_attn_Wkv, L0_attn_Wout, L0_ffn_g1, L0_ffn_Wq, L0_ffn_Wdkv, L0_ffn_Wuk, L0_ffn_Wuv, L0_ffn_Wo, L0_ffn_g2, L0_ffn_gate_w, L0_ffn_w1, L0_ffn_w2):
    import jax
    import jax.numpy as jnp

    def _L0_tok_ref(x, Wq_w, Wq_b, Wk_w, Wk_b, Wv_w, Wv_b, w_bias, out_w, out_b, ln_g, ln_b, local_mask):
        import jax, jax.numpy as jnp
        import numpy as np
        B, F, L, H, D = (8, 64, 256, 4, 64)
        MODEL = H * F
        WIN = 128

        def _local_mask():
            m = np.ones((L, L), dtype=bool)
            m = np.tril(m, WIN - 1)
            m = np.triu(m, -(WIN - 1))
            return jnp.asarray(m)

        def _flatten(y):
            n = y.shape[0]
            return y.transpose(0, 2, 3, 1).reshape(n, L, -1)

        def proj(w, b):
            y = jnp.einsum('nclh,dc->ndlh', x, w) + b[None, :, None, None]
            return _flatten(y)
        q = proj(Wq_w, Wq_b)
        k = proj(Wk_w, Wk_b)
        v = proj(Wv_w, Wv_b)
        wb = w_bias * local_mask.astype(w_bias.dtype)
        ew = jnp.exp(wb)
        ek = jnp.exp(k)
        num = jnp.einsum('ts,nsd->ntd', ew, ek * v)
        den = jnp.einsum('ts,nsd->ntd', ew, ek)
        y = jax.nn.sigmoid(q) * num / den
        h = y @ out_w + out_b + _flatten(x)
        mu = jnp.mean(h, axis=-1, keepdims=True)
        var = jnp.mean(jnp.square(h - mu), axis=-1, keepdims=True)
        return (h - mu) * jax.lax.rsqrt(var + 1e-05) * ln_g + ln_b

    def _L0_attn_ref(tokens, Wq, Wkv, Wout):
        import jax, jax.numpy as jnp
        import numpy as np
        HEADS, DK, DV = (16, 16, 64)
        EPS = 1e-12

        def l2norm(t):
            n = jnp.linalg.norm(t, axis=-1, keepdims=True)
            return t / jnp.maximum(n, EPS)

        def tanh_norm(t):
            n = jnp.linalg.norm(t, axis=-1, keepdims=True)
            return jnp.tanh(n) * (t / jnp.maximum(n, EPS))

        def split_heads(x, h):
            b, n, hd = x.shape
            return x.reshape(b, n, h, hd // h).transpose(0, 2, 1, 3)
        q = split_heads(tokens @ Wq, HEADS)
        kv = split_heads(tokens @ Wkv, HEADS)
        k, v = (kv[..., :DK], kv[..., DK:])
        q, k, v = (l2norm(q), l2norm(k), l2norm(v))
        sim = jnp.einsum('bhid,bhjd->bhij', q, k)
        attn = jnp.square(jax.nn.relu(sim))
        out = jnp.einsum('bhij,bhjd->bhid', attn, v)
        out = tanh_norm(out)
        b, h, n, d = out.shape
        out = out.transpose(0, 2, 1, 3).reshape(b, n, h * d)
        return out @ Wout

    def _L0_ffn_ref(x, g1, Wq, Wdkv, Wuk, Wuv, Wo, g2, gate_w, w1, w2):
        import jax, jax.numpy as jnp
        import numpy as np
        EMB = 256
        HEADS = 16
        SEQ = 512
        LATENT = 128
        N_EXP = 8
        TOP_K = 2
        EXP_DIM = 512
        BATCH = 2
        EPS = 1e-06

        def _rmsnorm(x, g):
            return x * jax.lax.rsqrt(jnp.mean(x * x, axis=-1, keepdims=True) + EPS) * g

        def _mla(h, Wq, Wdkv, Wuk, Wuv, Wo):
            B, S, D = h.shape
            hd = D // HEADS
            q = (h @ Wq).reshape(B, S, HEADS, hd)
            c = h @ Wdkv
            k = (c @ Wuk).reshape(B, S, HEADS, hd)
            v = (c @ Wuv).reshape(B, S, HEADS, hd)
            scores = jnp.einsum('bqhd,bkhd->bhqk', q, k) / jnp.sqrt(jnp.asarray(hd, h.dtype))
            causal = jnp.tril(jnp.ones((S, S), bool))
            scores = jnp.where(causal, scores, jnp.asarray(-1000000000.0, h.dtype))
            a = jax.nn.softmax(scores, axis=-1)
            out = jnp.einsum('bhqk,bkhd->bqhd', a, v).reshape(B, S, D)
            return out @ Wo

        def _moe(h, gate_w, w1, w2):
            B, S, D = h.shape
            t = h.reshape(B * S, D)
            logits = t @ gate_w
            top_v, top_i = jax.lax.top_k(logits, TOP_K)
            gates = jax.nn.softmax(top_v, axis=-1)
            T = t.shape[0]
            combine = jnp.zeros((T, N_EXP), t.dtype).at[jnp.arange(T)[:, None], top_i].add(gates)
            hid = jax.nn.silu(jnp.einsum('td,edh->teh', t, w1))
            ye = jnp.einsum('teh,ehd->ted', hid, w2)
            out = jnp.einsum('te,ted->td', combine, ye)
            return out.reshape(B, S, D)
        x = x + _mla(_rmsnorm(x, g1), Wq, Wdkv, Wuk, Wuv, Wo)
        x = x + _moe(_rmsnorm(x, g2), gate_w, w1, w2)
        return x
    h = _L0_tok_ref(x, L0_tok_Wq_w, L0_tok_Wq_b, L0_tok_Wk_w, L0_tok_Wk_b, L0_tok_Wv_w, L0_tok_Wv_b, L0_tok_w_bias, L0_tok_out_w, L0_tok_out_b, L0_tok_ln_g, L0_tok_ln_b, L0_tok_local_mask)
    h = jnp.concatenate([jnp.broadcast_to(cls_tok, (h.shape[0], 1, h.shape[2])), h], axis=1)
    h = h + _L0_attn_ref(_layernorm(h, axis=-1), L0_attn_Wq, L0_attn_Wkv, L0_attn_Wout)
    h = h + _L0_ffn_ref(_layernorm(h, axis=-1), L0_ffn_g1, L0_ffn_Wq, L0_ffn_Wdkv, L0_ffn_Wuk, L0_ffn_Wuv, L0_ffn_Wo, L0_ffn_g2, L0_ffn_gate_w, L0_ffn_w1, L0_ffn_w2)
    return h

_drawn_inputs = setup_inputs


def setup_inputs(seed=0):
    import zlib

    import numpy as np

    out = dict(_drawn_inputs(seed))
    spreads = {'L0_tok_Wq_b': (0.0, 0.8),
     'L0_tok_Wk_b': (0.0, 2.0),
     'L0_tok_Wv_b': (0.0, 0.1),
     'L0_tok_out_b': (0.0, 0.1),
     'L0_tok_ln_g': (1.0, 0.2),
     'L0_tok_ln_b': (0.0, 0.1),
     'L0_ffn_g1': (1.0, 0.6),
     'L0_ffn_g2': (1.0, 0.6)}
    factors = {'L0_tok_w_bias': 8.0,
     'L0_ffn_Wq': 8.0,
     'L0_ffn_Wdkv': 8.0,
     'L0_ffn_Wuk': 8.0,
     'L0_ffn_Wuv': 8.0,
     'L0_ffn_Wo': 8.0,
     'L0_ffn_gate_w': 8.0,
     'L0_ffn_w1': 8.0,
     'L0_ffn_w2': 8.0}
    for name, (base, spread) in spreads.items():
        noise = np.random.default_rng([zlib.crc32(name.encode()), seed]).standard_normal(out[name].shape)
        drawn = base * np.exp(spread * noise) if base else spread * noise
        out[name] = jnp.asarray(drawn.astype(out[name].dtype))
    for name, factor in factors.items():
        out[name] = (out[name] * factor).astype(out[name].dtype)
    return out
```

```python
from contextlib import ExitStack

import numpy as np
import concourse.bass as bass
from concourse import mybir


class Names:
    pass

F32 = mybir.dt.float32
F32R = mybir.dt.float32r
BF16 = mybir.dt.bfloat16
U8 = mybir.dt.uint8
ALU = mybir.AluOpType
ACT = mybir.ActivationFunctionType
AX = mybir.AxisListType

P = 128
F, L, H = 64, 256, 4
MODEL = F * H
KT = MODEL // P
LT = L // P
SEQ = L + 1
HEADS, DK, DV = 16, 16, 64
PAIRS = HEADS // 2
QCOLS = L + 2
NEXP, HID = 8, 512
MT = HID // P
TOKT, TOKW = 4, 121
CHUNK = TOKT * TOKW
LN_EPS, RMS_EPS, L2_EPS = 1e-5, 1e-6, 1e-12
MASKED = -1e30


def sbuf(nc, ctx, name, shape, dt=F32):
    return ctx.enter_context(nc.sbuf_tensor(name, shape, dt))


def release(nc, held):
    nc.clear_and_free_semaphores(held)
    nc.all_engine_barrier()


def sems(nc, ctx, *names):
    held = [nc.alloc_semaphore(n) for n in names]
    ctx.callback(release, nc, held)
    return held


def power(pool, out, x, exponent):
    e = exponent[0:out.shape[0], :]
    while len(e.shape) < len(out.shape):
        e = e.unsqueeze(len(e.shape))
    return pool.tensor_tensor(out, x, e.to_broadcast(list(out.shape)), ALU.pow)


def load_constants(nc, v, a):
    with ExitStack() as ctx:
        wb = sbuf(nc, ctx, "wb", [P, LT, L])
        mask8 = sbuf(nc, ctx, "mask8", [P, LT, L], U8)
        maskf = sbuf(nc, ctx, "maskf", [P, LT, L])
        brow = sbuf(nc, ctx, "brow", [P, 768])
        bpart = sbuf(nc, ctx, "bpart", [P, 3, 768], BF16)
        brest = sbuf(nc, ctx, "brest", [P, 2, 768])
        bq = sbuf(nc, ctx, "bq", [P, 1])
        stats = sbuf(nc, ctx, "c_stats", [1, 6])
        mv = sbuf(nc, ctx, "c_mv", [1, 2])
        rstd = sbuf(nc, ctx, "c_rstd", [1, 2])
        cn = sbuf(nc, ctx, "cn", [1, MODEL])
        cnT = sbuf(nc, ctx, "cnT", [P, KT])
        sq = sbuf(nc, ctx, "c_sq", [1, 1536])
        ss = sbuf(nc, ctx, "c_ss", [1, 48])
        rn = sbuf(nc, ctx, "c_rn", [1, 48])
        qkn = sbuf(nc, ctx, "c_qkn", [1, 512])
        vn = sbuf(nc, ctx, "c_vn", [1, 1024])
        hl = sbuf(nc, ctx, "c_hl", [1, 2 * HEADS, 4, DK], F32R)
        kcol = sbuf(nc, ctx, "kcol", [P, PAIRS])
        kmask = sbuf(nc, ctx, "kmask", [P, PAIRS, HEADS])
        vb = sbuf(nc, ctx, "c_vb", [HEADS, 1024])
        ps = ctx.enter_context(nc.psum_tensor("ps0", [P, 8, 512], F32))
        (zeroed, tables, ld_bd, ld_w, ld_mask, ld_bias, ld_cls, ld_vcls, st_vcls, mask_f, wb_ready, wbT, bias_split,
         cls_stats, cls_norm, cls_T, cls_Tc, cls_proj, cls_sq, cls_ss, cls_rn, cls_unit, cls_hl, cls_hlT,
         cls_col, identr, cls_lift, cls_rstd, powers) = sems(
            nc, ctx, "zeroed", "tables", "ld_bd", "ld_w", "ld_mask", "ld_bias", "ld_cls", "ld_vcls", "st_vcls",
            "mask_f", "wb_ready", "wbT", "bias_split", "cls_stats", "cls_norm", "cls_T", "cls_Tc", "cls_proj",
            "cls_sq", "cls_ss", "cls_rn", "cls_unit", "cls_hl", "cls_hlT", "cls_col", "identr", "cls_lift", "cls_rstd", "powers")
        block = ctx.enter_context(nc.Block())

        @block.sync
        def _(sp):
            sp.dma_start(v.cls_row[:], a.cls_tok).then_inc(ld_cls, 16)
            sp.dma_start(v.wqk[:], a.wqk.rearrange("(k p) n -> p k n", p=P)).then_inc(ld_cls, 16)
            sp.dma_start(v.wv[:], a.wv.rearrange("(k p) n -> p k n", p=P)).then_inc(ld_cls, 16)
            sp.dma_start(wb[:], a.w_bias.rearrange("(t p) s -> p t s", p=P)).then_inc(ld_mask, 16)
            sp.dma_start(mask8[:], a.local_mask.rearrange("(t p) s -> p t s", p=P)).then_inc(ld_mask, 16)
            for n, b in enumerate((a.bk, a.bk, a.bv, a.bv, a.bk, a.bk, a.bv, a.bv)):
                sp.dma_start(brow[:, n * F:(n + 1) * F], b.partition_broadcast(P)).then_inc(ld_bias, 16)
            sp.dma_start(brow[:, 512:768], a.out_b.partition_broadcast(P)).then_inc(ld_bias, 16)
            for hh in range(2):
                sp.dma_start(bq[hh * F:(hh + 1) * F, :], a.bq).then_inc(ld_bias, 16)
            sp.wait_ge(zeroed, 6)
            for hh in range(2):
                rows = slice(hh * F, (hh + 1) * F)
                sp.dma_start(v.wkv_bd[rows, hh * F:(hh + 1) * F], a.wkT).then_inc(ld_bd, 16)
                sp.dma_start(v.wkv_bd[rows, P + hh * F:P + (hh + 1) * F], a.wvT).then_inc(ld_bd, 16)
                sp.dma_start(v.wq_bd[rows, hh * F:(hh + 1) * F], a.wqT).then_inc(ld_bd, 16)
            sp.wait_ge(ld_bd, 96)
            for dst, src in ((v.g_ln, a.ln_g), (v.b_ln, a.ln_b), (v.g1, a.g1)):
                sp.dma_start(dst[:], src.partition_broadcast(P)).then_inc(ld_w, 16)
            sp.dma_start(v.cls32[:], a.cls_tok.partition_broadcast(32)).then_inc(ld_w, 16)
            sp.dma_start(v.outw[:], a.out_w.rearrange("(k p) n -> p k n", p=P)).then_inc(ld_w, 16)
            sp.dma_start(v.wout[:], a.wout.rearrange("(k p) n -> p k n", p=P)).then_inc(ld_w, 16)
            sp.dma_start(v.wq2[:], a.ffn_wq.rearrange("(k p) n -> p k n", p=P)).then_inc(ld_w, 16)
            sp.dma_start(v.wdkv[:], a.wdkv.rearrange("(k p) n -> p k n", p=P)).then_inc(ld_w, 16)
            sp.dma_start(v.wukv[:], a.wukv).then_inc(ld_w, 16)
            sp.dma_start(v.wo[:], a.wo.rearrange("(k p) n -> p k n", p=P)).then_inc(ld_w, 16)
            sp.wait_ge(cls_unit, 2)
            sp.dma_start(a.vcls_attn, vn[:]).then_inc(st_vcls, 16)
            sp.wait_ge(st_vcls, 16)
            sp.dma_start(vb[:], a.vcls_attn.partition_broadcast(HEADS)).then_inc(ld_vcls, 16)
            sp.wait_ge(ld_w, 160)

        @block.gpsimd
        def _(pool):
            pool.memset(v.inv_root[:], -0.5).then_inc(powers, 1)
            pool.memset(v.root[:], 0.5).then_inc(powers, 1)
            pool.memset(v.ident[:], 0.0).then_inc(zeroed, 1)
            pool.memset(v.wkv_bd[:], 0.0).then_inc(zeroed, 1)
            pool.memset(v.wq_bd[:], 0.0).then_inc(zeroed, 1)
            pool.memset(kmask[:], 0.0).then_inc(zeroed, 1)
            pool.memset(v.biasr[:], 0.0).then_inc(zeroed, 1)
            pool.memset(v.bmask[:], 1.0).then_inc(zeroed, 1)
            pool.memset(v.causal[:], 0.0).then_inc(zeroed, 1)
            pool.memset(v.half1[:], 0.0).then_inc(zeroed, 1)
            pool.memset(v.ones_bf[:], 1.0).then_inc(zeroed, 1)
            pool.memset(v.QT[:].bitcast(F32), 0.0).then_inc(zeroed, 1)
            pool.wait_ge(zeroed, 10)
            pool.affine_select(out=v.ident[:], in_=v.ident[:], compare_op=ALU.not_equal, fill=1.0, base=0,
                               pattern=[[-1, P]], channel_multiplier=1).then_inc(tables, 1)
            for hh in range(2):
                rows = slice(64 * hh, 64 * hh + 64)
                pool.wait_ge(tables, 1 + hh)
                pool.affine_select(out=kmask[rows], in_=kmask[rows], compare_op=ALU.not_equal, fill=1.0, base=hh,
                                   pattern=[[2, PAIRS], [-1, HEADS]], channel_multiplier=0).then_inc(tables, 1)
            pool.wait_ge(tables, 3)
            pool.affine_select(out=v.bmask[:], in_=v.bmask[:], compare_op=ALU.is_equal, fill=0.0, base=0,
                               pattern=[[1, HEADS], [0, DV]], channel_multiplier=-1).then_inc(tables, 1)
            pool.wait_ge(tables, 4)
            pool.affine_select(out=v.causal[:], in_=v.causal[:], compare_op=ALU.is_ge, fill=MASKED, base=1,
                               pattern=[[-1, P + 2]], channel_multiplier=1).then_inc(tables, 1)
            for hh in range(2):
                rows = slice(64 * hh, 64 * hh + 64)
                pool.wait_ge(tables, 5 + hh)
                pool.memset(v.half1[rows, 64 * hh:64 * hh + 64], 1.0).then_inc(tables, 1)
            pool.wait_ge(tables, 7)
            pool.tensor_copy(v.ident_r[:], v.ident[:]).then_inc(identr, 1)
            pool.tensor_copy(v.ident_bf[:], v.ident[:]).then_inc(identr, 1)
            pool.wait_ge(powers, 2)
            pool.wait_ge(identr, 2)
            pool.wait_ge(cls_stats, 3)
            power(pool, rstd[:, 0:1], rstd[:, 1:2], v.inv_root).then_inc(cls_rstd, 1)
            pool.wait_ge(cls_rstd, 1)
            pool.wait_ge(cls_lift, 1)
            power(pool, rn[:], ss[:], v.inv_root).then_inc(cls_rn, 1)
            pool.wait_ge(cls_rn, 1)
            pool.wait_ge(ld_vcls, 16)
            pool.tensor_tensor(v.vcls_bd[:], vb[:], v.bmask[:].rearrange("p h d -> p (h d)"),
                               ALU.mult).then_inc(identr, 1)

        @block.scalar
        def _(act):
            act.wait_ge(wbT, 1)
            for s in range(LT):
                act.activation(v.ewT[:, s, :], ps[:, s, 0:L], ACT.Exp)
            act.wait_ge(cls_proj, 1)
            act.activation(sq[:, 0:512], ps[0:1, 3, :], ACT.Square).then_inc(cls_sq, 1)
            act.activation(sq[:, 512:1536], ps[0:1, 4:6, :].rearrange("p a n -> p (a n)"),
                           ACT.Square).then_inc(cls_sq, 1)

        @block.vector
        def _(dve):
            dve.wait_ge(ld_cls, 48)
            dve.bn_stats(stats[:], v.cls_row[:]).then_inc(cls_stats, 1)
            dve.wait_ge(cls_stats, 1)
            dve.bn_aggr(mv[:], stats[:]).then_inc(cls_stats, 1)
            dve.wait_ge(cls_stats, 2)
            dve.tensor_scalar(rstd[:, 1:2], mv[:, 1:2], LN_EPS, None, ALU.add).then_inc(cls_stats, 1)
            dve.wait_ge(cls_rstd, 1)
            dve.tensor_scalar(cn[:], v.cls_row[:], mv[:, 0:1], rstd[:, 0:1], ALU.subtract,
                              ALU.mult).then_inc(cls_norm, 1)
            dve.wait_ge(ld_mask, 32)
            dve.tensor_copy(maskf[:], mask8[:]).then_inc(mask_f, 1)
            dve.wait_ge(mask_f, 1)
            dve.tensor_tensor(wb[:], wb[:], maskf[:], ALU.mult).then_inc(wb_ready, 1)
            dve.wait_ge(ld_bias, 176)
            dve.tensor_copy(bpart[:, 0, :], brow[:]).then_inc(bias_split, 1)
            dve.wait_ge(bias_split, 1)
            dve.tensor_tensor(brest[:, 0, :], brow[:], bpart[:, 0, :], ALU.subtract).then_inc(bias_split, 1)
            dve.wait_ge(bias_split, 2)
            dve.tensor_copy(bpart[:, 1, :], brest[:, 0, :]).then_inc(bias_split, 1)
            dve.wait_ge(bias_split, 3)
            dve.tensor_tensor(brest[:, 1, :], brest[:, 0, :], bpart[:, 1, :], ALU.subtract).then_inc(bias_split, 1)
            dve.wait_ge(bias_split, 4)
            dve.tensor_copy(bpart[:, 2, :], brest[:, 1, :]).then_inc(bias_split, 1)
            dve.wait_ge(bias_split, 5)
            dve.wait_ge(zeroed, 9)
            for n in range(3):
                dve.tensor_copy(v.biasr[32 * n:32 * n + 1, :], bpart[32 * n:32 * n + 1, n, :])
            dve.tensor_scalar(v.nbq[:], bq[:], -1.0, None, ALU.mult)
            dve.wait_ge(ld_w, 160)
            dve.tensor_scalar(v.wq2[:], v.wq2[:], DK ** -0.5, None, ALU.mult)
            dve.wait_ge(cls_T, 1)
            dve.tensor_copy(cnT[:], ps[:, 2, 0:KT]).then_inc(cls_Tc, 1)
            dve.wait_ge(cls_sq, 2)
            dve.tensor_reduce(ss[:, 0:32], sq[:, 0:512].rearrange("p (g d) -> p g d", d=DK), AX.X,
                              ALU.add).then_inc(cls_ss, 1)
            dve.tensor_reduce(ss[:, 32:48], sq[:, 512:1536].rearrange("p (g d) -> p g d", d=DV), AX.X,
                              ALU.add).then_inc(cls_ss, 1)
            dve.wait_ge(cls_ss, 2)
            dve.tensor_scalar(ss[:], ss[:], L2_EPS ** 2, None, ALU.max).then_inc(cls_lift, 1)
            dve.wait_ge(cls_rn, 1)
            dve.tensor_tensor(qkn[:].rearrange("p (g d) -> p g d", d=DK),
                              ps[0:1, 3, :].rearrange("p (g d) -> p g d", d=DK),
                              rn[:, 0:32].unsqueeze(2).to_broadcast([1, 32, DK]), ALU.mult).then_inc(cls_unit, 1)
            dve.tensor_tensor(vn[:].rearrange("p (g d) -> p g d", d=DV),
                              ps[0:1, 4:6, :].rearrange("p a (g d) -> p (a g) d", d=DV),
                              rn[:, 32:48].unsqueeze(2).to_broadcast([1, 16, DV]), ALU.mult).then_inc(cls_unit, 1)
            dve.wait_ge(cls_unit, 2)
            g = qkn[:].rearrange("p (g d) -> p g d", d=DK)
            for q in range(2):
                heads = slice(q * HEADS, (q + 1) * HEADS)
                dve.tensor_copy(blocks(hl[:, heads], q, 0), twice(g[:, heads])).then_inc(cls_hl, 1)
            dve.wait_ge(cls_hl, 2)
            for q in range(2):
                heads = slice(q * HEADS, (q + 1) * HEADS)
                dve.tensor_tensor(blocks(hl[:, heads], q, 1), twice(g[:, heads]),
                                  blocks(hl[:, heads], q, 0).bitcast(F32), ALU.subtract).then_inc(cls_hl, 1)
            dve.wait_ge(cls_hlT, 1)
            dve.wait_ge(zeroed, 10)
            dve.tensor_copy(v.QT[:, :, L], ps[:, 6, 0:PAIRS]).then_inc(cls_col, 1)
            dve.tensor_copy(kcol[:], ps[:, 6, PAIRS:2 * PAIRS]).then_inc(cls_col, 1)
            dve.wait_ge(cls_col, 2)
            dve.wait_ge(tables, 3)
            dve.tensor_tensor(v.kcls_bd[:], kmask[:], kcol[:].unsqueeze(2).to_broadcast([P, PAIRS, HEADS]), ALU.mult)

        @block.tensor
        def _(pe):
            pe.wait_ge(tables, 7)
            pe.wait_ge(wb_ready, 1)
            for s in range(LT):
                for t in range(LT):
                    last = pe.transpose(ps[:, s, t * P:(t + 1) * P], wb[:, t, s * P:(s + 1) * P], v.ident[:])
            last.then_inc(wbT, 1)
            pe.wait_ge(cls_norm, 1)
            for k in range(KT):
                last = pe.transpose(ps[:, 2, k:k + 1], cn[:, k * P:(k + 1) * P], v.ident[0:1, 0:1])
            last.then_inc(cls_T, 1)
            pe.wait_ge(cls_Tc, 1)
            for k in range(KT):
                pe.matmul(ps[0:1, 3, :], cnT[:, k:k + 1], v.wqk[:, k, :], start=k == 0, stop=k == KT - 1)
            for n in range(2):
                for k in range(KT):
                    last = pe.matmul(ps[0:1, 4 + n, :], cnT[:, k:k + 1], v.wv[:, k, n * 512:(n + 1) * 512],
                                     start=k == 0, stop=k == KT - 1)
            last.then_inc(cls_proj, 1)
            pe.wait_ge(cls_hl, 4)
            pe.wait_ge(identr, 1)
            hf = hl[:].bitcast(F32)
            for q in range(2):
                for pr in range(PAIRS):
                    g0 = q * HEADS + 2 * pr
                    last = pe.transpose(ps[:, 6, q * PAIRS + pr:q * PAIRS + pr + 1],
                                        hf[:, g0:g0 + 2].rearrange("p g a d -> p (g a d)"), v.ident[0:1, 0:1])
            last.then_inc(cls_hlT, 1)


def blocks(hl, is_key, low):
    if is_key:
        return hl.rearrange("p g (a b) d -> p g a b d", b=2)[:, :, :, int(low), :]
    return hl[:, :, 2 * low:2 * low + 2, :]


def twice(x):
    r, g, d = x.shape
    return x.unsqueeze(2).to_broadcast([r, g, 2, d])


def mixer_and_attention(nc, v, a, nb):
    with ExitStack() as ctx:
        idle = sbuf(nc, ctx, "idle", [1, 1])
        xraw = sbuf(nc, ctx, "xraw", [P, L * H + 8])
        x2 = sbuf(nc, ctx, "x2", [P, 2, L])
        ekv = sbuf(nc, ctx, "ekv", [P, LT, 2, 2, P])
        eq = sbuf(nc, ctx, "eq", [P, 2, L])
        den = sbuf(nc, ctx, "den", [P, 2, L])
        rden = sbuf(nc, ctx, "rden", [P, 2, L])
        yT = sbuf(nc, ctx, "yT", [P, 2, L])
        stats = sbuf(nc, ctx, "stats", [P, LT, 6])
        mv = sbuf(nc, ctx, "mv", [P, LT, 2])
        rstd = sbuf(nc, ctx, "rstd", [P, 2, LT])
        ln = sbuf(nc, ctx, "ln", [P, LT, MODEL])
        lng = sbuf(nc, ctx, "lng", [P, LT, MODEL])
        h1 = sbuf(nc, ctx, "h1", [P, LT, MODEL])
        stats2 = sbuf(nc, ctx, "stats2", [P, LT, 6])
        mv2 = sbuf(nc, ctx, "mv2", [P, LT, 2])
        rstd2 = sbuf(nc, ctx, "rstd2", [P, 2, LT])
        xn = sbuf(nc, ctx, "xn", [P, LT, MODEL])
        xT = sbuf(nc, ctx, "xT", [P, KT, L])
        sq = sbuf(nc, ctx, "sq", [P, LT, 1536])
        ss = sbuf(nc, ctx, "ss", [P, LT, 48])
        ssm = sbuf(nc, ctx, "ssm", [P, LT, 48])
        rn = sbuf(nc, ctx, "rn", [P, LT, 48])
        qkn = sbuf(nc, ctx, "qkn", [P, LT, 512])
        hl = sbuf(nc, ctx, "hl", [P, LT, 2 * HEADS, 4, DK], F32R)
        V = sbuf(nc, ctx, "V", [P, LT, HEADS * DV])
        KTr = sbuf(nc, ctx, "KTr", [P, PAIRS, L], F32R)
        R = sbuf(nc, ctx, "R", [P, 2, LT, QCOLS])
        PR = sbuf(nc, ctx, "PR", [P, 3, LT, QCOLS])
        rcl = sbuf(nc, ctx, "rcl", [HEADS, QCOLS])
        pcl = sbuf(nc, ctx, "pcl", [HEADS, QCOLS])
        osq = sbuf(nc, ctx, "osq", [P, 2, LT, 512])
        oss = sbuf(nc, ctx, "oss", [P, 2, LT * 8])
        osm = sbuf(nc, ctx, "osm", [P, 2, LT * 8])
        orn = sbuf(nc, ctx, "orn", [P, 2, LT * 8])
        onm = sbuf(nc, ctx, "onm", [P, 2, LT * 8])
        oth = sbuf(nc, ctx, "oth", [P, 2, LT * 8])
        osc = sbuf(nc, ctx, "osc", [P, 2, LT * 8])
        on = sbuf(nc, ctx, "on", [P, 2, LT, 512])
        OT = sbuf(nc, ctx, "OT", [P, PAIRS, L])
        h2 = sbuf(nc, ctx, "h2", [P, LT * MODEL])
        ps = ctx.enter_context(nc.psum_tensor("psA", [P, 8, 512], F32))
        (x_loaded, x2_ready, kvq_done, ek_done, eq_done, ev_done, num_done, den_t, den_r, y_done, hpre_done,
         ln_stats, ln_done, ln_scaled, h1_done, ln2_stats, xn_done, xn_T, xT_done, qk_done, v_done, qk_sq, v_sq, qk_ss,
         qk_rn, qk_unit, v_unit, qk_hi, qk_lo, qkT_done, qkT_copied, pcl_sim, pcl_relu, pcl_done, sim_done, relu_done,
         prob_done, av_done, o_sq, o_ss, o_norms, o_tanh, o_scale, o_unit, ocl_copied, oT_done, oT_copied,
         out_done, h2_done, h2_stored, ln_rooted, ln2_rooted, qk_lift, o_lift) = sems(
            nc, ctx, "x_loaded", "x2_ready", "kvq_done", "ek_done", "eq_done", "ev_done", "num_done", "den_t",
            "den_r", "y_done", "hpre_done", "ln_stats", "ln_done", "ln_scaled", "h1_done", "ln2_stats", "xn_done",
            "xn_T", "xT_done", "qk_done", "v_done", "qk_sq", "v_sq", "qk_ss", "qk_rn", "qk_unit", "v_unit", "qk_hi",
            "qk_lo", "qkT_done", "qkT_copied", "pcl_sim", "pcl_relu", "pcl_done", "sim_done", "relu_done",
            "prob_done", "av_done", "o_sq", "o_ss", "o_norms", "o_tanh", "o_scale", "o_unit", "ocl_copied",
            "oT_done", "oT_copied", "out_done", "h2_done", "h2_stored", "ln_rooted", "ln2_rooted",
            "qk_lift", "o_lift")
        block = ctx.enter_context(nc.Block())
        x_flat = a.x.rearrange("n c l h -> n c (l h)")

        def load_x(sp, i):
            src = x_flat[bass.ds(i, 1)].rearrange("n c m -> c (n m)")
            sp.dma_start(xraw[0:F, 4:4 + L * H], src).then_inc(x_loaded, 16)
            sp.dma_start(xraw[F:P, 3:3 + L * H], src).then_inc(x_loaded, 16)

        @block.sync
        def _(sp):
            load_x(sp, 0)
            with sp.Fori(1, nb) as i:
                at, prev = sp.snap(i), sp.snap(i - 1)
                sp.wait_ge(x2_ready, i)
                load_x(sp, at)
                sp.wait_ge(h2_done, i)
                sp.dma_start(a.hs[bass.ds(prev, 1)].rearrange("n p m -> p (n m)"), h2[:]).then_inc(h2_stored, 16)
            sp.wait_ge(h2_done, nb)
            sp.dma_start(a.hs[nb - 1], h2[:]).then_inc(h2_stored, 16)
            sp.wait_ge(h2_stored, 16 * nb + 1)

        @block.gpsimd
        def _(pool):
            with pool.Fori(0, nb) as i:
                pool.wait_ge(ln_stats, 5 * i + 5)
                power(pool, rstd[:, 1], rstd[:, 0], v.inv_root).then_inc(ln_rooted, 1)
                pool.wait_ge(ln_done, 2 * i + 2)
                gb = v.g_ln[:].unsqueeze(1).to_broadcast([P, LT, MODEL])
                bb = v.b_ln[:].unsqueeze(1).to_broadcast([P, LT, MODEL])
                pool.tensor_tensor(lng[:], ln[:], gb, ALU.mult).then_inc(ln_scaled, 1)
                pool.wait_ge(ln_scaled, i + 1)
                pool.tensor_tensor(h1[:], lng[:], bb, ALU.add).then_inc(h1_done, 1)
                pool.wait_ge(ln2_stats, 5 * i + 5)
                power(pool, rstd2[:, 1], rstd2[:, 0], v.inv_root).then_inc(ln2_rooted, 1)
                pool.wait_ge(qk_lift, i + 1)
                power(pool, rn[:].rearrange("p t g -> p (t g)"), ssm[:].rearrange("p t g -> p (t g)"),
                      v.inv_root).then_inc(qk_rn, 1)
                for t in range(LT):
                    for q in range(2):
                        pool.wait_ge(qk_hi, 4 * i + 2 * t + q + 1)
                        src = qkn[:, t, q * 256:(q + 1) * 256].rearrange("p (g d) -> p g d", d=DK)
                        heads = slice(q * HEADS, (q + 1) * HEADS)
                        pool.tensor_tensor(blocks(hl[:, t, heads], q, 1), twice(src),
                                           blocks(hl[:, t, heads], q, 0).bitcast(F32), ALU.subtract)\
                            .then_inc(qk_lo, 1)
                for g in range(2):
                    pool.wait_ge(o_lift, 2 * i + g + 1)
                    power(pool, onm[:, g], oss[:, g], v.root).then_inc(o_norms, 1)
                    power(pool, orn[:, g], osm[:, g], v.inv_root).then_inc(o_norms, 1)

        @block.scalar
        def _(act):
            with act.Fori(0, nb) as i:
                act.wait_ge(kvq_done, i + 1)
                for t in range(LT):
                    act.activation(ekv[:, t, 0], ps[:, t, :].rearrange("p (a n) -> p a n", a=2)[:, :, 0:P],
                                   ACT.Exp).then_inc(ek_done, 1)
                act.activation(eq[:], ps[:, 2, :].rearrange("p (a n) -> p a n", a=2), ACT.Exp, bias=v.nbq[:],
                               scale=-1.0).then_inc(eq_done, 1)
                act.wait_ge(xn_T, i + 1)
                act.activation(xT[:], ps[:, 7, :].rearrange("p (k n) -> p k n", k=KT), ACT.Copy).then_inc(xT_done, 1)
                act.wait_ge(qk_done, i + 1)
                act.activation(sq[:, :, 0:512], ps[:, 0:2, :], ACT.Square).then_inc(qk_sq, 1)
                for t in range(LT):
                    act.wait_ge(v_done, LT * i + t + 1)
                    act.activation(sq[:, t, 512:1536].rearrange("p (a n) -> p a n", a=2),
                                   ps[:, 2 + 2 * t:4 + 2 * t, :], ACT.Square).then_inc(v_sq, 1)
                act.wait_ge(qk_unit, i + 1)
                for t in range(LT):
                    for q in range(2):
                        src = qkn[:, t, q * 256:(q + 1) * 256].rearrange("p (g d) -> p g d", d=DK)
                        act.activation(blocks(hl[:, t, q * HEADS:(q + 1) * HEADS], q, 0), twice(src),
                                       ACT.Copy).then_inc(qk_hi, 1)
                for n in range(0, 8, 2):
                    act.wait_ge(qkT_done, 8 * i + n + 1)
                    dst = (v.QT if n < 4 else KTr)[:, 2 * (n % 4):2 * (n % 4) + 2, 0:L]
                    act.activation(dst, ps[:, n % 4, :].rearrange("p (a n) -> p a n", a=2),
                                   ACT.Copy).then_inc(qkT_copied, 1)
                act.wait_ge(pcl_sim, i + 1)
                act.activation(rcl[:], ps[0:HEADS, 7, 0:QCOLS], ACT.Relu).then_inc(pcl_relu, 1)
                for g in range(2):
                    for h in range(8 * g, 8 * g + 8):
                        act.wait_ge(sim_done, HEADS * i + h + 1)
                        act.wait_ge(prob_done, HEADS * i + h + 1)
                        b = 2 * (h % 2)
                        act.activation(R[:, h % 2], ps[:, b:b + 2, 0:QCOLS], ACT.Relu).then_inc(relu_done, 1)
                    act.wait_ge(av_done, 2 * i + g + 1)
                    act.activation(osq[:, g], ps[:, 4:6, :], ACT.Square).then_inc(o_sq, 1)
                    act.wait_ge(o_norms, 4 * i + 2 * g + 2)
                    act.activation(oth[:, g], onm[:, g], ACT.Tanh).then_inc(o_tanh, 1)
                for g in range(2):
                    for t in range(LT):
                        act.wait_ge(oT_done, 4 * i + 2 * g + t + 1)
                        act.activation(OT[:, 4 * g:4 * g + 4, t * P:(t + 1) * P],
                                       ps[:, 6 + t, :].rearrange("p (a n) -> p a n", a=4),
                                       ACT.Copy).then_inc(oT_copied, 1)

        @block.vector
        def _(dve):
            dve.memset(PR[:], 0.0).then_inc(prob_done, 1)
            dve.memset(R[:], 0.0).then_inc(prob_done, 1)
            dve.sem_inc(h2_stored, 1)

            def layer_norm(i, src, st, mvt, rs, dst, sem, rooted, done):
                for t in range(LT):
                    dve.bn_stats(st[:, t], src[t]).then_inc(sem, 1)
                dve.wait_ge(sem, 5 * i + 2)
                dve.memset(idle[:], 0.0)
                for t in range(LT):
                    dve.bn_aggr(mvt[:, t], st[:, t]).then_inc(sem, 1)
                dve.wait_ge(sem, 5 * i + 4)
                dve.tensor_scalar(rs[:, 0], mvt[:, :, 1], LN_EPS, None, ALU.add).then_inc(sem, 1)
                dve.wait_ge(rooted, i + 1)
                for t in range(LT):
                    dve.tensor_scalar(dst[:, t], src[t], mvt[:, t, 0:1], rs[:, 1, t:t + 1], ALU.subtract,
                                      ALU.mult).then_inc(done, 1)

            with dve.Fori(0, nb) as i:
                dve.wait_ge(x_loaded, 32 * i + 32)
                raw = xraw[:, 4:4 + L * H].rearrange("p (l a b) -> p a l b", a=2, b=2)[:, :, :, 0]
                dve.tensor_copy(x2[:], raw).then_inc(x2_ready, 1)
                for t in range(LT):
                    dve.wait_ge(ek_done, LT * i + t + 1)
                    dve.tensor_tensor(ekv[:, t, 1], ps[:, t, :].rearrange("p (a n) -> p a n", a=2)[:, :, P:2 * P],
                                      ekv[:, t, 0], ALU.mult).then_inc(ev_done, 1)
                dve.wait_ge(num_done, i + 1)
                dve.wait_ge(eq_done, i + 1)
                dve.scalar_tensor_tensor(den[:], eq[:], 1.0, ps[:, 4, :].rearrange("p (a n) -> p a n", a=2),
                                         ALU.add, ALU.mult).then_inc(den_t, 1)
                dve.wait_ge(den_t, i + 1)
                dve.reciprocal(rden[:], den[:]).then_inc(den_r, 1)
                dve.wait_ge(den_r, i + 1)
                dve.tensor_tensor(yT[:], ps[:, 3, :].rearrange("p (a n) -> p a n", a=2), rden[:],
                                  ALU.mult).then_inc(y_done, 1)
                dve.wait_ge(hpre_done, i + 1)
                layer_norm(i, [ps[:, 5, t * MODEL:(t + 1) * MODEL] for t in range(LT)], stats, mv, rstd, ln,
                           ln_stats, ln_rooted, ln_done)
                dve.wait_ge(h1_done, i + 1)
                layer_norm(i, [h1[:, t] for t in range(LT)], stats2, mv2, rstd2, xn, ln2_stats,
                           ln2_rooted, xn_done)
                dve.wait_ge(qk_sq, i + 1)
                dve.tensor_reduce(ss[:, :, 0:32], sq[:, :, 0:512].rearrange("p t (g d) -> p t g d", d=DK), AX.X,
                                  ALU.add).then_inc(qk_ss, 1)
                dve.wait_ge(v_sq, LT * i + LT)
                dve.tensor_reduce(ss[:, :, 32:48], sq[:, :, 512:1536].rearrange("p t (g d) -> p t g d", d=DV), AX.X,
                                  ALU.add).then_inc(qk_ss, 1)
                dve.wait_ge(qk_ss, 2 * i + 2)
                dve.tensor_scalar(ssm[:], ss[:], L2_EPS ** 2, None, ALU.max).then_inc(qk_lift, 1)
                dve.wait_ge(qk_rn, i + 1)
                dve.tensor_tensor(qkn[:].rearrange("p t (g d) -> p t g d", d=DK),
                                  ps[:, 0:2, :].rearrange("p t (g d) -> p t g d", d=DK),
                                  rn[:, :, 0:32].unsqueeze(3).to_broadcast([P, LT, 32, DK]),
                                  ALU.mult).then_inc(qk_unit, 1)
                for t in range(LT):
                    dve.tensor_tensor(V[:, t].rearrange("p (g d) -> p g d", d=DV),
                                      ps[:, 2 + 2 * t:4 + 2 * t, :].rearrange("p a (g d) -> p (a g) d", d=DV),
                                      rn[:, t, 32:48].unsqueeze(2).to_broadcast([P, HEADS, DV]),
                                      ALU.mult).then_inc(v_unit, 1)
                for n in range(1, 8, 2):
                    dve.wait_ge(qkT_done, 8 * i + n + 1)
                    dst = (v.QT if n < 4 else KTr)[:, 2 * (n % 4):2 * (n % 4) + 2, 0:L]
                    dve.tensor_copy(dst, ps[:, n % 4, :].rearrange("p (a n) -> p a n", a=2)).then_inc(qkT_copied, 1)
                dve.wait_ge(pcl_relu, i + 1)
                dve.tensor_tensor(pcl[:], ps[0:HEADS, 7, 0:QCOLS], rcl[:], ALU.mult).then_inc(pcl_done, 1)
                for g in range(2):
                    for h in range(8 * g, 8 * g + 8):
                        dve.wait_ge(relu_done, HEADS * i + h + 1)
                        b = 2 * (h % 2)
                        dve.tensor_tensor(PR[:, h % 3], ps[:, b:b + 2, 0:QCOLS], R[:, h % 2],
                                          ALU.mult).then_inc(prob_done, 1)
                    dve.wait_ge(o_sq, 2 * i + g + 1)
                    dve.tensor_reduce(oss[:, g], osq[:, g].rearrange("p t (h d) -> p (t h) d", d=DV), AX.X,
                                      ALU.add).then_inc(o_ss, 1)
                    dve.wait_ge(o_ss, 2 * i + g + 1)
                    dve.tensor_scalar(osm[:, g], oss[:, g], L2_EPS ** 2, None, ALU.max).then_inc(o_lift, 1)
                    dve.wait_ge(o_tanh, 2 * i + g + 1)
                    dve.wait_ge(o_norms, 4 * i + 2 * g + 2)
                    dve.tensor_tensor(osc[:, g], oth[:, g], orn[:, g], ALU.mult).then_inc(o_scale, 1)
                    dve.wait_ge(o_scale, 2 * i + g + 1)
                    dve.tensor_tensor(on[:, g].rearrange("p t (h d) -> p (t h) d", d=DV),
                                      ps[:, 4:6, :].rearrange("p t (h d) -> p (t h) d", d=DV),
                                      osc[:, g].unsqueeze(2).to_broadcast([P, LT * 8, DV]),
                                      ALU.mult).then_inc(o_unit, 1)
                dve.tensor_copy(v.oclsT[:, :, bass.ds(i, 1)].rearrange("p a b -> p (a b)"),
                                ps[:, 6, 0:PAIRS]).then_inc(ocl_copied, 1)
                dve.wait_ge(out_done, i + 1)
                dve.wait_ge(h2_stored, 16 * i + 1)
                dve.tensor_tensor(h2[:], ps[:, 5, :], h1[:].rearrange("p t n -> p (t n)"), ALU.add).then_inc(h2_done, 1)

        @block.tensor
        def _(pe):
            with pe.Fori(0, nb) as i:
                pe.wait_ge(x2_ready, i + 1)
                for t in range(LT):
                    pe.matmul(ps[:, t, :], v.ones_bf[0:96, :], v.biasr[0:96, 0:512], start=True, stop=False,
                              skip_group_check=True)
                    for hp in range(2):
                        pe.matmul(ps[:, t, hp * 256:hp * 256 + 256], x2[:, hp, t * P:(t + 1) * P], v.wkv_bd[:],
                                  start=False, stop=True, skip_group_check=True)
                for hp in range(2):
                    last = pe.matmul(ps[:, 2, hp * 256:hp * 256 + 256], v.wq_bd[:], x2[:, hp, :], start=True,
                                     stop=True)
                last.then_inc(kvq_done, 1)
                pe.wait_ge(ev_done, LT * i + LT)
                for n, kv in ((3, 1), (4, 0)):
                    for hp in range(2):
                        for t in range(LT):
                            last = pe.matmul(ps[:, n, hp * L:(hp + 1) * L], ekv[:, t, kv, hp, :], v.ewT[:, t, :],
                                             start=t == 0, stop=t == LT - 1)
                last.then_inc(num_done, 1)
                for t in range(LT):
                    pe.matmul(ps[:, 5, t * MODEL:(t + 1) * MODEL], v.ones_bf[0:96, :], v.biasr[0:96, 512:768],
                              start=t == 0, stop=False, skip_group_check=True)
                for t in range(LT):
                    for hp in range(2):
                        pe.matmul(ps[:, 5, t * MODEL + hp * P:t * MODEL + hp * P + P], x2[:, hp, t * P:(t + 1) * P],
                                  v.ident[:], start=False, stop=False, skip_group_check=True)
                pe.wait_ge(y_done, i + 1)
                for t in range(LT):
                    for hp in range(2):
                        last = pe.matmul(ps[:, 5, t * MODEL:(t + 1) * MODEL], yT[:, hp, t * P:(t + 1) * P],
                                         v.outw[:, hp, :], start=False, stop=True, skip_group_check=True)
                last.then_inc(hpre_done, 1)
                pe.wait_ge(xn_done, LT * i + LT)
                for k in range(KT):
                    for t in range(LT):
                        last = pe.transpose(ps[:, 7, k * L + t * P:k * L + (t + 1) * P],
                                            xn[:, t, k * P:(k + 1) * P], v.ident[:])
                last.then_inc(xn_T, 1)
                pe.wait_ge(xT_done, i + 1)
                for t in range(LT):
                    for k in range(KT):
                        last = pe.matmul(ps[:, t, :], xT[:, k, t * P:(t + 1) * P], v.wqk[:, k, :], start=k == 0,
                                         stop=k == KT - 1)
                last.then_inc(qk_done, 1)
                for t in range(LT):
                    for n in range(2):
                        for k in range(KT):
                            last = pe.matmul(ps[:, 2 + 2 * t + n, :], xT[:, k, t * P:(t + 1) * P],
                                             v.wv[:, k, n * 512:(n + 1) * 512], start=k == 0, stop=k == KT - 1)
                    last.then_inc(v_done, 1)
                pe.wait_ge(qk_lo, 4 * i + 4)
                pe.wait_ge(v_unit, LT * i + LT)
                hf = hl[:].bitcast(F32)
                for n in range(8):
                    if n >= 4:
                        pe.wait_ge(qkT_copied, 8 * i + n)
                    for j in range(2):
                        for t in range(LT):
                            g0 = HEADS * (n // 4) + 2 * (2 * (n % 4) + j)
                            last = pe.transpose(ps[:, n % 4, j * L + t * P:j * L + (t + 1) * P],
                                                hf[:, t, g0:g0 + 2].rearrange("p g a d -> p (g a d)"), v.ident[:])
                    last.then_inc(qkT_done, 1)
                pe.wait_ge(qkT_copied, 8 * i + 8)
                for pr in range(PAIRS):
                    last = pe.matmul(ps[0:HEADS, 7, 0:QCOLS], v.kcls_bd[:, pr, :], v.QT[:, pr, :], start=pr == 0,
                                     stop=pr == PAIRS - 1)
                last.then_inc(pcl_sim, 1)

                def sim(h):
                    rows = slice(64 * (h % 2), 64 * (h % 2) + 64)
                    if h >= 2:
                        pe.wait_ge(prob_done, HEADS * i + h + 1)
                    for t in range(LT):
                        last = pe.matmul(ps[:, 2 * (h % 2) + t, 0:QCOLS], KTr[rows, h // 2, t * P:(t + 1) * P],
                                         v.QT[rows, h // 2, :], start=True, stop=True)
                    last.then_inc(sim_done, 1)

                def values(h):
                    pe.wait_ge(prob_done, HEADS * i + h + 3)
                    c = (h % 8) * DV
                    for it in range(LT):
                        for jt in range(LT):
                            pe.matmul(ps[:, 4 + it, c:c + DV], PR[:, h % 3, jt, it * P:(it + 1) * P],
                                      V[:, jt, h * DV:(h + 1) * DV], start=False, stop=True, skip_group_check=True)
                    rows = slice(64 * (h % 2), 64 * (h % 2) + 64)
                    for jt in range(LT):
                        last = pe.matmul(ps[rows, 6, h // 2:h // 2 + 1], V[:, jt, h * DV:(h + 1) * DV],
                                         PR[:, h % 3, jt, L:L + 1], start=False, stop=True, skip_group_check=True)
                    return last

                sim(0)
                sim(1)
                pe.wait_ge(pcl_done, i + 1)
                for g in range(2):
                    if g == 1:
                        pe.wait_ge(o_unit, 2 * i + 1)
                    for it in range(LT):
                        pe.matmul(ps[:, 4 + it, :], pcl[:, it * P:(it + 1) * P], v.vcls_bd[:, g * 512:(g + 1) * 512],
                                  start=True, stop=False, skip_group_check=True)
                    if g == 0:
                        for pr in range(PAIRS):
                            pe.matmul(ps[:, 6, pr:pr + 1], v.vcls_bd[:, pr * P:(pr + 1) * P], pcl[:, L:L + 1],
                                      start=pr == 0, stop=False, skip_group_check=True)
                    for h in range(8 * g, 8 * g + 8):
                        last = values(h)
                        if h + 2 < HEADS:
                            sim(h + 2)
                    last.then_inc(av_done, 1)
                for g in range(2):
                    pe.wait_ge(o_unit, 2 * i + g + 1)
                    for t in range(LT):
                        if g == 0 and t == 0:
                            pe.wait_ge(ocl_copied, i + 1)
                        if g == 1:
                            pe.wait_ge(oT_copied, 4 * i + t + 1)
                        for pr in range(4):
                            last = pe.transpose(ps[:, 6 + t, pr * P:(pr + 1) * P],
                                                on[:, g, t, pr * P:(pr + 1) * P], v.ident[:])
                        last.then_inc(oT_done, 1)
                pe.wait_ge(oT_copied, 4 * i + 4)
                for t in range(LT):
                    for pr in range(PAIRS):
                        last = pe.matmul(ps[:, 5, t * MODEL:(t + 1) * MODEL], OT[:, pr, t * P:(t + 1) * P],
                                         v.wout[:, pr, :], start=pr == 0, stop=pr == PAIRS - 1)
                last.then_inc(out_done, 1)


def class_tokens(nc, v, a, nb):
    NP = PAIRS * nb
    with ExitStack() as ctx:
        sq = sbuf(nc, ctx, "b_sq", [P, NP])
        ssum = sbuf(nc, ctx, "b_ssum", [P, NP])
        ssm = sbuf(nc, ctx, "b_ssm", [P, NP])
        nrm = sbuf(nc, ctx, "b_nrm", [P, NP])
        rnm = sbuf(nc, ctx, "b_rnm", [P, NP])
        th = sbuf(nc, ctx, "b_th", [P, NP])
        sc = sbuf(nc, ctx, "b_sc", [P, NP])
        on = sbuf(nc, ctx, "b_on", [P, PAIRS, nb])
        h2c = sbuf(nc, ctx, "b_h2", [nb, MODEL])
        stats = sbuf(nc, ctx, "b_stats", [nb, 6])
        mv = sbuf(nc, ctx, "b_mv", [nb, 2])
        rstd = sbuf(nc, ctx, "b_rstd", [nb, 5])
        y = sbuf(nc, ctx, "b_y", [nb, MODEL])
        ysq = sbuf(nc, ctx, "b_ysq", [nb, MODEL])
        hn = sbuf(nc, ctx, "b_hn", [nb, MODEL])
        hT = sbuf(nc, ctx, "b_hT", [P, KT, nb])
        cT = sbuf(nc, ctx, "b_cT", [P, nb])
        hl = sbuf(nc, ctx, "b_hl", [nb, HEADS, 4, DK], F32R)
        vrow = sbuf(nc, ctx, "b_v", [nb, MODEL])
        vT = sbuf(nc, ctx, "b_vT", [P, KT, nb])
        x = sbuf(nc, ctx, "b_x", [nb, MODEL])
        base = sbuf(nc, ctx, "b_base", [nb, MODEL])
        ps = ctx.enter_context(nc.psum_tensor("psB", [P, 8, 512], F32))
        (squared, norms_sum, norms, tanhed, scaled, unit, attn_out, h2_done, stat, y_done, ysq_done, rms, hn_done,
         hn_T, hT_done, c_done, cT_done, kv_done, k_hi, k_lo, v_copied, kT_done, k_copied, vT_done, v_turned,
         o_done, x_done, stored, lifted, rooted) = sems(
            nc, ctx, "b_squared", "b_norms_sum", "b_norms", "b_tanhed", "b_scaled", "b_unit", "b_attn_out",
            "b_h2_done", "b_stat", "b_y_done", "b_ysq_done", "b_rms", "b_hn_done", "b_hn_T", "b_hT_done", "b_c_done",
            "b_cT_done", "b_kv_done", "b_k_hi", "b_k_lo", "b_v_copied", "b_kT_done", "b_k_copied", "b_vT_done",
            "b_v_turned", "b_o_done", "b_x_done", "b_stored",
            "b_lifted", "b_rooted")
        block = ctx.enter_context(nc.Block())
        oc = v.oclsT[:].rearrange("p a b -> p (a b)")

        @block.sync
        def _(sp):
            sp.wait_ge(v_copied, 1)
            sp.dma_start(a.vcls_mla[0:nb], vrow[:]).then_inc(stored, 16)
            sp.wait_ge(x_done, 2)
            rows = a.xs[0:nb * SEQ].rearrange("(n s) d -> n s d", s=SEQ)[:, 0, :]
            sp.dma_start(rows, x[:]).then_inc(stored, 16)
            rows = a.bs[0:nb * SEQ].rearrange("(n s) d -> n s d", s=SEQ)[:, 0, :]
            sp.dma_start(rows, base[:]).then_inc(stored, 16)
            sp.wait_ge(stored, 48)

        @block.gpsimd
        def _(pool):
            pool.wait_ge(lifted, 2)
            power(pool, nrm[:], ssum[:], v.root).then_inc(norms, 1)
            power(pool, rnm[:], ssm[:], v.inv_root).then_inc(norms, 1)
            pool.wait_ge(stat, 3)
            power(pool, rstd[:, 0:1], rstd[:, 4:5], v.inv_root).then_inc(rooted, 1)
            pool.wait_ge(rms, 2)
            power(pool, rstd[:, 3:4], rstd[:, 2:3], v.inv_root).then_inc(rooted, 1)

        @block.scalar
        def _(act):
            act.activation(sq[:], oc, ACT.Square).then_inc(squared, 1)
            act.wait_ge(norms, 1)
            act.activation(th[:], nrm[:], ACT.Tanh).then_inc(tanhed, 1)
            act.wait_ge(y_done, 1)
            act.activation(ysq[:], y[:], ACT.Square).then_inc(ysq_done, 1)

        @block.vector
        def _(dve):
            dve.wait_ge(norms_sum, 1)
            dve.tensor_copy(ssum[:], ps[:, 0, 0:NP]).then_inc(lifted, 1)
            dve.tensor_scalar(ssm[:], ps[:, 0, 0:NP], L2_EPS ** 2, None, ALU.max).then_inc(lifted, 1)
            dve.wait_ge(tanhed, 1)
            dve.wait_ge(norms, 2)
            dve.tensor_tensor(sc[:], th[:], rnm[:], ALU.mult).then_inc(scaled, 1)
            dve.wait_ge(scaled, 1)
            dve.tensor_tensor(on[:].rearrange("p a b -> p (a b)"), oc, sc[:], ALU.mult).then_inc(unit, 1)
            dve.wait_ge(attn_out, 1)
            dve.tensor_tensor(h2c[:], ps[0:nb, 1, 0:MODEL], v.cls32[0:nb, :], ALU.add).then_inc(h2_done, 1)
            dve.wait_ge(h2_done, 1)
            dve.bn_stats(stats[:], h2c[:]).then_inc(stat, 1)
            dve.wait_ge(stat, 1)
            dve.bn_aggr(mv[:], stats[:]).then_inc(stat, 1)
            dve.wait_ge(stat, 2)
            dve.tensor_scalar(rstd[:, 4:5], mv[:, 1:2], LN_EPS, None, ALU.add).then_inc(stat, 1)
            dve.wait_ge(rooted, 1)
            dve.tensor_scalar(y[:], h2c[:], mv[:, 0:1], rstd[:, 0:1], ALU.subtract, ALU.mult).then_inc(y_done, 1)
            dve.wait_ge(ysq_done, 1)
            dve.tensor_reduce(rstd[:, 1:2], ysq[:], AX.X, ALU.add).then_inc(rms, 1)
            dve.wait_ge(rms, 1)
            dve.tensor_scalar(rstd[:, 2:3], rstd[:, 1:2], 1.0 / MODEL, RMS_EPS, ALU.mult, ALU.add).then_inc(rms, 1)
            dve.wait_ge(rms, 2)
            dve.wait_ge(rooted, 2)
            dve.scalar_tensor_tensor(hn[:], y[:], rstd[:, 3:4], v.g1[0:nb, :], ALU.mult, ALU.mult).then_inc(hn_done, 1)
            dve.wait_ge(hn_T, 1)
            dve.tensor_copy(hT[:], ps[:, 2, 0:KT * nb].rearrange("p (k n) -> p k n", k=KT)).then_inc(hT_done, 1)
            dve.wait_ge(c_done, 1)
            dve.tensor_copy(cT[:], ps[:, 3, 0:nb]).then_inc(cT_done, 1)
            dve.wait_ge(kv_done, 1)
            k = ps[0:nb, 4, 0:MODEL].rearrange("p (g d) -> p g d", d=DK)
            dve.tensor_copy(blocks(hl[:], 1, 0), twice(k)).then_inc(k_hi, 1)
            dve.tensor_copy(vrow[:], ps[0:nb, 4, MODEL:2 * MODEL]).then_inc(v_copied, 1)
            dve.wait_ge(k_hi, 1)
            dve.tensor_tensor(blocks(hl[:], 1, 1), twice(k), blocks(hl[:], 1, 0).bitcast(F32),
                              ALU.subtract).then_inc(k_lo, 1)
            dve.wait_ge(vT_done, 1)
            dve.tensor_copy(vT[:], ps[:, 5, 0:KT * nb].rearrange("p (k n) -> p k n", k=KT)).then_inc(v_turned, 1)
            dve.wait_ge(kT_done, 1)
            dve.tensor_copy(v.kclsT[:], ps[:, 6, 0:NP].rearrange("p (a b) -> p a b", a=PAIRS)).then_inc(k_copied, 1)
            dve.wait_ge(o_done, 1)
            dve.tensor_tensor(x[:], ps[0:nb, 7, 0:MODEL], y[:], ALU.add).then_inc(x_done, 1)
            dve.wait_ge(x_done, 1)
            dve.tensor_tensor(base[:], x[:], h2c[:], ALU.add).then_inc(x_done, 1)

        @block.tensor
        def _(pe):
            pe.wait_ge(squared, 1)
            pe.matmul(ps[:, 0, 0:NP], v.half1[:], sq[:], start=True, stop=True).then_inc(norms_sum, 1)
            pe.wait_ge(unit, 1)
            for pr in range(PAIRS):
                last = pe.matmul(ps[0:nb, 1, 0:MODEL], on[:, pr, :], v.wout[:, pr, :], start=pr == 0,
                                 stop=pr == PAIRS - 1)
            last.then_inc(attn_out, 1)
            pe.wait_ge(hn_done, 1)
            for k in range(KT):
                last = pe.transpose(ps[:, 2, k * nb:(k + 1) * nb], hn[:, k * P:(k + 1) * P], v.ident[0:nb, 0:nb])
            last.then_inc(hn_T, 1)
            pe.wait_ge(hT_done, 1)
            for k in range(KT):
                last = pe.matmul(ps[:, 3, 0:nb], v.wdkv[:, k, :], hT[:, k, :], start=k == 0, stop=k == KT - 1)
            last.then_inc(c_done, 1)
            pe.wait_ge(cT_done, 1)
            pe.matmul(ps[0:nb, 4, :], cT[:], v.wukv[:], start=True, stop=True).then_inc(kv_done, 1)
            pe.wait_ge(v_copied, 1)
            for k in range(KT):
                last = pe.transpose(ps[:, 5, k * nb:(k + 1) * nb], vrow[:, k * P:(k + 1) * P], v.ident[0:nb, 0:nb])
            last.then_inc(vT_done, 1)
            pe.wait_ge(k_lo, 1)
            hf = hl[:].bitcast(F32)
            for pr in range(PAIRS):
                last = pe.transpose(ps[:, 6, pr * nb:(pr + 1) * nb], hf[:, 2 * pr:2 * pr + 2].rearrange("p g a d -> p (g a d)"),
                                    v.ident[0:nb, 0:nb])
            last.then_inc(kT_done, 1)
            pe.wait_ge(v_turned, 1)
            for k in range(KT):
                last = pe.matmul(ps[0:nb, 7, 0:MODEL], vT[:, k, :], v.wo[:, k, :], start=k == 0, stop=k == KT - 1)
            last.then_inc(o_done, 1)


def latent_attention(nc, v, a, nb):
    with ExitStack() as ctx:
        stats = sbuf(nc, ctx, "m_stats", [P, LT, 6])
        idle = sbuf(nc, ctx, "m_idle", [1, 1])
        h2 = sbuf(nc, ctx, "m_h2", [P, LT, MODEL])
        hy = sbuf(nc, ctx, "m_hy", [P, LT, MODEL])
        mv = sbuf(nc, ctx, "m_mv", [P, LT, 2])
        rstd = sbuf(nc, ctx, "m_rstd", [P, 2, LT])
        y = sbuf(nc, ctx, "m_y", [P, LT, MODEL])
        ysq = sbuf(nc, ctx, "m_ysq", [P, LT, MODEL])
        ms = sbuf(nc, ctx, "m_ms", [P, 3, LT])
        hn = sbuf(nc, ctx, "m_hn", [P, LT, MODEL])
        hT = sbuf(nc, ctx, "m_hT", [P, KT, L])
        cT = sbuf(nc, ctx, "m_cT", [P, L])
        hl = sbuf(nc, ctx, "m_hl", [P, LT, 2 * HEADS, 4, DK], F32R)
        V = sbuf(nc, ctx, "m_V", [P, LT, MODEL])
        KTr = sbuf(nc, ctx, "m_KT", [P, PAIRS, QCOLS], F32R)
        nmax = sbuf(nc, ctx, "m_nmax", [P, LT, HEADS])
        esum = sbuf(nc, ctx, "m_esum", [P, LT, HEADS])
        PM = sbuf(nc, ctx, "m_P", [P, 2, 2, QCOLS])
        pc = sbuf(nc, ctx, "m_pc", [P, LT, HEADS])
        pcT = sbuf(nc, ctx, "m_pcT", [HEADS, L])
        PT = sbuf(nc, ctx, "m_PT", [P, 2, 512])
        vb = sbuf(nc, ctx, "m_vb", [HEADS, MODEL])
        vcb = sbuf(nc, ctx, "m_vcb", [HEADS, MODEL])
        resum = sbuf(nc, ctx, "m_resum", [P, LT, HEADS])
        on = sbuf(nc, ctx, "m_on", [P, LT, MODEL])
        oT = sbuf(nc, ctx, "m_oT", [P, KT, L])
        x = sbuf(nc, ctx, "m_x", [P, LT, MODEL])
        base = sbuf(nc, ctx, "m_base", [P, LT, MODEL])
        pad = a.xs.shape[0] - nb * SEQ
        zparts = max(n for n in range(1, P + 1) if pad % n == 0)
        zrow = sbuf(nc, ctx, "m_zrow", [zparts, pad // zparts * MODEL])
        ps = ctx.enter_context(nc.psum_tensor("psC", [P, 8, 512], F32))
        (v_loaded, vcb_done, ln_stats, y_done, ysq_done, rms, hn_done, hn_T, hT_done, cq_done, cT_done, kv_done,
         qk_hi, qk_lo, v_copied, qkT_done, qkT_copied, kcls_done, s_done, max_done, exp_done, pc_done, pT_done,
         pT_copied, o_done, pcT_done, pcT_copied, resum_done, on_done, oT_done, oT_copied, wo_done, x_done,
         base_done, stored, pad_done, rooted, h2_loaded, hy_done) = sems(
            nc, ctx, "m_v_loaded", "m_vcb_done", "m_ln_stats", "m_y_done", "m_ysq_done", "m_rms", "m_hn_done",
            "m_hn_T", "m_hT_done", "m_cq_done", "m_cT_done", "m_kv_done", "m_qk_hi", "m_qk_lo", "m_v_copied",
            "m_qkT_done", "m_qkT_copied", "m_kcls_done", "m_s_done", "m_max_done", "m_exp_done", "m_pc_done",
            "m_pT_done", "m_pT_copied", "m_o_done", "m_pcT_done", "m_pcT_copied", "m_resum_done", "m_on_done",
            "m_oT_done", "m_oT_copied", "m_wo_done", "m_x_done", "m_base_done", "m_stored", "m_pad_done", "m_rooted",
            "m_h2_loaded", "m_hy_done")
        block = ctx.enter_context(nc.Block())
        UNITS = [(hp, t) for hp in range(PAIRS) for t in range(LT)]
        KEYS = [P + 2, QCOLS]
        NU = len(UNITS)

        def q_psum(t):
            return ps[:, 0, t * MODEL:(t + 1) * MODEL].rearrange("p (g d) -> p g d", d=DK)

        def k_psum(t):
            return ps[:, 1 + t, 0:MODEL].rearrange("p (g d) -> p g d", d=DK)

        xs_rows = a.xs[0:nb * SEQ].rearrange("(n s) d -> n s d", s=SEQ)[:, 1:SEQ, :]
        bs_rows = a.bs[0:nb * SEQ].rearrange("(n s) d -> n s d", s=SEQ)[:, 1:SEQ, :]

        @block.sync
        def _(sp):
            sp.wait_ge(pad_done, 2)
            sp.dma_start(a.xs[nb * SEQ:nb * SEQ + pad].rearrange("(p r) d -> p (r d)", p=zparts), zrow[:]).then_inc(stored, 16)
            sp.dma_start(a.bs[nb * SEQ:nb * SEQ + pad].rearrange("(p r) d -> p (r d)", p=zparts), zrow[:]).then_inc(stored, 16)
            sp.dma_start(h2[:].rearrange("p t n -> p (t n)"), a.hs[0]).then_inc(h2_loaded, 16)

            def value_and_results(i):
                sp.wait_ge(vcb_done, i + 1)
                sp.dma_start(vb[:], a.vcls_mla[bass.ds(i, 1)].partition_broadcast(HEADS)).then_inc(v_loaded, 16)
                out_x = xs_rows[bass.ds(i, 1)].rearrange("n (t p) d -> p (n t) d", p=P)
                out_b = bs_rows[bass.ds(i, 1)].rearrange("n (t p) d -> p (n t) d", p=P)
                sp.wait_ge(x_done, i + 1)
                sp.dma_start(out_x, x[:]).then_inc(stored, 16)
                sp.wait_ge(base_done, i + 1)
                sp.dma_start(out_b, base[:]).then_inc(stored, 16)

            with sp.Fori(0, nb - 1) as i:
                at, nxt = sp.snap(i), sp.snap(i + 1)
                sp.wait_ge(hy_done, i + 1)
                sp.dma_start(h2[:].rearrange("p t n -> p (t n)"),
                             a.hs[bass.ds(nxt, 1)].rearrange("n p m -> p (n m)")).then_inc(h2_loaded, 16)
                value_and_results(at)
            value_and_results(nb - 1)
            sp.wait_ge(h2_loaded, 16 * nb)
            sp.wait_ge(stored, 32 * nb + 32)

        @block.gpsimd
        def _(pool):
            pool.memset(KTr[:].bitcast(F32), 0.0).then_inc(pad_done, 1)
            pool.memset(zrow[:], 0.0).then_inc(pad_done, 1)
            pool.memset(vcb[:], 0.0).then_inc(vcb_done, 1)
            with pool.Fori(0, nb) as i:
                pool.wait_ge(ln_stats, 5 * i + 5)
                power(pool, rstd[:, 1], rstd[:, 0], v.inv_root).then_inc(rooted, 1)
                pool.wait_ge(y_done, LT * i + LT)
                pool.tensor_tensor(hy[:], h2[:], y[:], ALU.add).then_inc(hy_done, 1)
                pool.wait_ge(rms, i + 1)
                power(pool, ms[:, 2], ms[:, 1], v.inv_root).then_inc(rooted, 1)
                pool.wait_ge(kv_done, i + 1)
                pool.wait_ge(v_loaded, 16 * i + 16)
                pool.tensor_tensor(vcb[:].rearrange("p (h d) -> p h d", d=DK),
                                   vb[:].rearrange("p (h d) -> p h d", d=DK), v.bmask[:, :, 0:DK],
                                   ALU.mult).then_inc(vcb_done, 1)

        @block.scalar
        def _(act):
            with act.Fori(0, nb) as i:
                for t in range(LT):
                    act.wait_ge(y_done, LT * i + t + 1)
                    act.activation(ysq[:, t], y[:, t], ACT.Square, accum_out=ms[:, 0, t:t + 1]).then_inc(ysq_done, 1)
                act.wait_ge(hn_T, i + 1)
                act.activation(hT[:], ps[:, 6, :].rearrange("p (k n) -> p k n", k=KT), ACT.Copy).then_inc(hT_done, 1)
                act.wait_ge(cq_done, i + 1)
                act.activation(cT[:], ps[:, 7, 0:L], ACT.Copy).then_inc(cT_done, 1)
                for t in range(LT):
                    act.activation(blocks(hl[:, t, 0:HEADS], 0, 0), twice(q_psum(t)),
                                   ACT.Copy).then_inc(qk_hi, 1)
                act.wait_ge(kv_done, i + 1)
                for t in range(LT):
                    act.activation(blocks(hl[:, t, HEADS:2 * HEADS], 1, 0), twice(k_psum(t)),
                                   ACT.Copy).then_inc(qk_hi, 1)
                act.activation(V[:], ps[:, 1:3, MODEL:2 * MODEL], ACT.Copy).then_inc(v_copied, 1)
                for n in range(0, 8, 2):
                    act.wait_ge(qkT_done, 8 * i + n + 1)
                    j = 2 * (n % 4)
                    dst = v.QT[:, j:j + 2, 0:L] if n < 4 else KTr[:, j:j + 2, 1:1 + L]
                    act.activation(dst, ps[:, n % 4, :].rearrange("p (a n) -> p a n", a=2),
                                   ACT.Copy).then_inc(qkT_copied, 1)
                for u, (hp, t) in enumerate(UNITS):
                    act.wait_ge(max_done, NU * i + u + 1)
                    act.wait_ge(pT_done, NU * i + u + 1)
                    if u >= 2:
                        act.wait_ge(pc_done, NU * i + u - 1)
                    N = KEYS[t]
                    b = 2 * (u % 2)
                    for hh in range(2):
                        h = 2 * hp + hh
                        act.activation(PM[:, u % 2, hh, 0:N - 1], ps[:, b + hh, 0:N - 1], ACT.Exp,
                                       bias=nmax[:, t, h:h + 1], accum_out=esum[:, t, h:h + 1]).then_inc(exp_done, 1)
                act.wait_ge(pcT_done, i + 1)
                act.activation(pcT[:], ps[0:HEADS, 7, 0:L], ACT.Copy).then_inc(pcT_copied, 1)
                act.wait_ge(oT_done, i + 1)
                act.activation(oT[:], ps[:, 7, :].rearrange("p (k n) -> p k n", k=KT), ACT.Copy).then_inc(oT_copied, 1)

        @block.vector
        def _(dve):
            with dve.Fori(0, nb) as i:
                src = [h2[:, t] for t in range(LT)]
                dve.wait_ge(h2_loaded, 16 * i + 16)
                for t in range(LT):
                    dve.bn_stats(stats[:, t], src[t]).then_inc(ln_stats, 1)
                dve.wait_ge(ln_stats, 5 * i + 2)
                dve.memset(idle[:], 0.0)
                for t in range(LT):
                    dve.bn_aggr(mv[:, t], stats[:, t]).then_inc(ln_stats, 1)
                dve.wait_ge(ln_stats, 5 * i + 4)
                dve.tensor_scalar(rstd[:, 0], mv[:, :, 1], LN_EPS, None, ALU.add).then_inc(ln_stats, 1)
                dve.wait_ge(rooted, 2 * i + 1)
                for t in range(LT):
                    dve.tensor_scalar(y[:, t], src[t], mv[:, t, 0:1], rstd[:, 1, t:t + 1], ALU.subtract,
                                      ALU.mult).then_inc(y_done, 1)
                dve.wait_ge(ysq_done, LT * i + LT)
                dve.tensor_scalar(ms[:, 1], ms[:, 0], 1.0 / MODEL, RMS_EPS, ALU.mult, ALU.add).then_inc(rms, 1)
                dve.wait_ge(rooted, 2 * i + 2)
                for t in range(LT):
                    dve.scalar_tensor_tensor(hn[:, t], y[:, t], ms[:, 2, t:t + 1], v.g1[:], ALU.mult,
                                             ALU.mult).then_inc(hn_done, 1)
                dve.wait_ge(qk_hi, 4 * i + LT)
                for t in range(LT):
                    dve.tensor_tensor(blocks(hl[:, t, 0:HEADS], 0, 1), twice(q_psum(t)),
                                      blocks(hl[:, t, 0:HEADS], 0, 0).bitcast(F32), ALU.subtract).then_inc(qk_lo, 1)
                dve.wait_ge(v_copied, i + 1)
                for t in range(LT):
                    dve.tensor_tensor(blocks(hl[:, t, HEADS:2 * HEADS], 1, 1), twice(k_psum(t)),
                                      blocks(hl[:, t, HEADS:2 * HEADS], 1, 0).bitcast(F32),
                                      ALU.subtract).then_inc(qk_lo, 1)
                dve.tensor_copy(KTr[:, :, 0], v.kclsT[:, :, bass.ds(i, 1)].rearrange("p a b -> p (a b)"))\
                    .then_inc(kcls_done, 1)
                for n in range(1, 8, 2):
                    dve.wait_ge(qkT_done, 8 * i + n + 1)
                    j = 2 * (n % 4)
                    dst = v.QT[:, j:j + 2, 0:L] if n < 4 else KTr[:, j:j + 2, 1:1 + L]
                    dve.tensor_copy(dst, ps[:, n % 4, :].rearrange("p (a n) -> p a n", a=2)).then_inc(qkT_copied, 1)

                def copy_back(u):
                    t = UNITS[u][1]
                    dve.wait_ge(pT_done, NU * i + u + 3)
                    n = 256 * (t + 1)
                    dve.tensor_copy(PT[:, u % 2, 0:n], ps[:, 4 + u % 2, 0:n]).then_inc(pT_copied, 1)
                    dve.tensor_copy(pc[:, t, 2 * UNITS[u][0]:2 * UNITS[u][0] + 2],
                                    PM[:, u % 2, :, 0]).then_inc(pc_done, 1)

                for u, (hp, t) in enumerate(UNITS):
                    dve.wait_ge(s_done, NU * i + u + 1)
                    b = 2 * (u % 2)
                    dve.tensor_reduce(nmax[:, t, 2 * hp:2 * hp + 2], ps[:, b:b + 2, 0:KEYS[t] - 1], AX.X, ALU.max,
                                      negate=True).then_inc(max_done, 1)
                    if u:
                        copy_back(u - 1)
                copy_back(NU - 1)
                dve.wait_ge(exp_done, 2 * NU * (i + 1))
                dve.reciprocal(resum[:], esum[:]).then_inc(resum_done, 1)
                dve.wait_ge(resum_done, i + 1)
                dve.wait_ge(o_done, i + 1)
                dve.tensor_tensor(on[:].rearrange("p t (h d) -> p (t h) d", d=DK),
                                  ps[:, 6, :].rearrange("p (g d) -> p g d", d=DK),
                                  resum[:].rearrange("p t h -> p (t h)").unsqueeze(2).to_broadcast(
                                      [P, LT * HEADS, DK]), ALU.mult).then_inc(on_done, 1)
                dve.wait_ge(wo_done, i + 1)
                dve.wait_ge(stored, 32 * i + 32)
                dve.tensor_tensor(x[:], ps[:, 3, :].rearrange("p (t n) -> p t n", t=LT), y[:],
                                  ALU.add).then_inc(x_done, 1)
                dve.tensor_tensor(base[:], ps[:, 3, :].rearrange("p (t n) -> p t n", t=LT), hy[:],
                                  ALU.add).then_inc(base_done, 1)

        @block.tensor
        def _(pe):
            pe.sem_inc(pT_done, 2)
            with pe.Fori(0, nb) as i:
                pe.wait_ge(hn_done, LT * i + LT)
                for k in range(KT):
                    for t in range(LT):
                        last = pe.transpose(ps[:, 6, k * L + t * P:k * L + (t + 1) * P],
                                            hn[:, t, k * P:(k + 1) * P], v.ident[:])
                last.then_inc(hn_T, 1)
                pe.wait_ge(hT_done, i + 1)
                for k in range(KT):
                    pe.matmul(ps[:, 7, 0:L], v.wdkv[:, k, :], hT[:, k, :], start=k == 0, stop=k == KT - 1)
                for t in range(LT):
                    for k in range(KT):
                        last = pe.matmul(ps[:, 0, t * MODEL:(t + 1) * MODEL], hT[:, k, t * P:(t + 1) * P],
                                         v.wq2[:, k, :], start=k == 0, stop=k == KT - 1)
                last.then_inc(cq_done, 1)
                pe.wait_ge(cT_done, i + 1)
                for t in range(LT):
                    last = pe.matmul(ps[:, 1 + t, :], cT[:, t * P:(t + 1) * P], v.wukv[:], start=True, stop=True)
                last.then_inc(kv_done, 1)
                pe.wait_ge(v_copied, i + 1)
                pe.wait_ge(qk_lo, 4 * i + 4)
                hf = hl[:].bitcast(F32)
                for n in range(8):
                    if n >= 4:
                        pe.wait_ge(qkT_copied, 8 * i + n)
                    for j in range(2):
                        for t in range(LT):
                            g0 = HEADS * (n // 4) + 2 * (2 * (n % 4) + j)
                            last = pe.transpose(ps[:, n % 4, j * L + t * P:j * L + (t + 1) * P],
                                                hf[:, t, g0:g0 + 2].rearrange("p g a d -> p (g a d)"), v.ident[:])
                    last.then_inc(qkT_done, 1)
                pe.wait_ge(qkT_copied, 8 * i + 8)
                pe.wait_ge(kcls_done, i + 1)

                def scores(u):
                    hp, t = UNITS[u]
                    if u >= 2:
                        pe.wait_ge(exp_done, 2 * NU * i + 2 * (u - 1))
                    for hh in range(2):
                        b = 2 * (u % 2) + hh
                        rows = slice(64 * hh, 64 * hh + 64)
                        pe.matmul(ps[:, b, 0:KEYS[t]], v.QT[rows, hp, t * P:(t + 1) * P], KTr[rows, hp, 0:KEYS[t]],
                                  start=True, stop=False, skip_group_check=True)
                        last = pe.matmul(ps[:, b, t * P:t * P + P + 2], v.ident_bf[:], v.causal[:], start=False,
                                         stop=True, skip_group_check=True)
                    last.then_inc(s_done, 1)

                def turn(u):
                    hp, t = UNITS[u]
                    pe.wait_ge(exp_done, 2 * NU * i + 2 * (u + 1))
                    if u >= 2:
                        pe.wait_ge(pT_copied, NU * i + u - 1)
                    for hh in range(2):
                        for jt in range(t + 1):
                            c = (hh * (t + 1) + jt) * P
                            last = pe.transpose(ps[:, 4 + u % 2, c:c + P],
                                                PM[:, u % 2, hh, 1 + jt * P:1 + (jt + 1) * P], v.ident[:])
                    last.then_inc(pT_done, 1)

                def values(u):
                    hp, t = UNITS[u]
                    pe.wait_ge(pT_copied, NU * i + u + 1)
                    for hh in range(2):
                        for jt in range(t + 1):
                            c = (hh * (t + 1) + jt) * P
                            h = 2 * hp + hh
                            pe.matmul(ps[:, 6, t * MODEL + h * DK:t * MODEL + (h + 1) * DK],
                                      PT[:, u % 2, c:c + P], V[:, jt, h * DK:(h + 1) * DK],
                                      start=u == 0 and hh == 0 and jt == 0, stop=True, skip_group_check=True)

                scores(0)
                scores(1)
                for u in range(NU):
                    turn(u)
                    if u + 2 < NU:
                        scores(u + 2)
                    if u:
                        values(u - 1)
                values(NU - 1)
                pe.wait_ge(pc_done, NU * (i + 1))
                for t in range(LT):
                    last = pe.transpose(ps[0:HEADS, 7, t * P:(t + 1) * P], pc[:, t, :], v.ident[:])
                last.then_inc(pcT_done, 1)
                pe.wait_ge(pcT_copied, i + 1)
                pe.wait_ge(vcb_done, i + 2)
                for t in range(LT):
                    last = pe.matmul(ps[:, 6, t * MODEL:(t + 1) * MODEL], pcT[:, t * P:(t + 1) * P], vcb[:],
                                     start=False, stop=True, skip_group_check=True)
                last.then_inc(o_done, 1)
                pe.wait_ge(on_done, i + 1)
                for k in range(KT):
                    for t in range(LT):
                        last = pe.transpose(ps[:, 7, k * L + t * P:k * L + (t + 1) * P],
                                            on[:, t, k * P:(k + 1) * P], v.ident[:])
                last.then_inc(oT_done, 1)
                pe.wait_ge(oT_copied, i + 1)
                for t in range(LT):
                    for k in range(KT):
                        last = pe.matmul(ps[:, 3, t * MODEL:(t + 1) * MODEL], oT[:, k, t * P:(t + 1) * P],
                                         v.wo[:, k, :], start=k == 0, stop=k == KT - 1)
                last.then_inc(wo_done, 1)


def load_experts(nc, v, a):
    with ExitStack() as ctx:
        NST = 4
        stage = sbuf(nc, ctx, "w_stage", [P, NST, KT * HID])
        gstage = sbuf(nc, ctx, "g_stage", [P, KT, NEXP])
        w_loaded = sems(nc, ctx, *[f"w_loaded{n}" for n in range(NST)])
        hi_done, lo_done, g_loaded, g_hi, misc = sems(nc, ctx, "w_hi", "w_lo", "g_loaded", "g_hi", "d_misc")
        block = ctx.enter_context(nc.Block())
        parts = [(v.w1h, v.w1l, e) for e in range(NEXP)] + [(v.w2h, v.w2l, e) for e in range(NEXP)]

        @block.sync
        def _(sp):
            sp.dma_start(v.g2[:], a.g2.partition_broadcast(TOKW)).then_inc(g_loaded, 16)
            sp.dma_start(gstage[:], a.gate_w.rearrange("(k p) e -> p k e", p=P)).then_inc(g_loaded, 16)
            for n, (h, _, e) in enumerate(parts):
                if n >= NST:
                    sp.wait_ge(lo_done, n - NST + 1)
                if h is v.w1h:
                    src = a.w1[e].rearrange("(k p) n -> p k n", p=P)
                    dst = stage[:, n % NST].rearrange("p (k n) -> p k n", k=KT)
                else:
                    src = a.w2[e].rearrange("(m p) d -> p m d", p=P)
                    dst = stage[:, n % NST].rearrange("p (m d) -> p m d", m=MT)
                sp.dma_start(dst, src).then_inc(w_loaded[n % NST], 16)
            sp.wait_ge(g_loaded, 32)

        @block.scalar
        def _(act):
            for n, (h, _, e) in enumerate(parts):
                act.wait_ge(w_loaded[n % NST], 16 * (n // NST + 1))
                act.activation(h[:, e], stage[:, n % NST], ACT.Copy).then_inc(hi_done, 1)

        @block.gpsimd
        def _(pool):
            pool.memset(v.lower[:], 1.0).then_inc(misc, 1)
            pool.memset(v.inv_root_d[:], -0.5)
            pool.memset(v.identd[:], 0.0).then_inc(misc, 1)
            pool.wait_ge(misc, 2)
            for t in range(TOKT):
                pool.affine_select(out=v.lower[:, t], in_=v.lower[:, t], compare_op=ALU.is_gt, fill=0.0, base=0,
                                   pattern=[[1, NEXP], [-1, NEXP]], channel_multiplier=0)
            pool.affine_select(out=v.identd[:], in_=v.identd[:], compare_op=ALU.not_equal, fill=1.0, base=0,
                               pattern=[[-1, P]], channel_multiplier=1)

        @block.vector
        def _(dve):
            dve.wait_ge(g_loaded, 32)
            dve.tensor_copy(v.gateh[:], gstage[:]).then_inc(g_hi, 1)
            dve.wait_ge(g_hi, 1)
            dve.tensor_tensor(v.gatel[:], gstage[:], v.gateh[:].bitcast(F32), ALU.subtract)
            for n, (h, l, e) in enumerate(parts):
                dve.wait_ge(hi_done, n + 1)
                dve.tensor_tensor(l[:, e], stage[:, n % NST], h[:, e].bitcast(F32), ALU.subtract).then_inc(lo_done, 1)


def experts(nc, v, a, out, chunks):
    with ExitStack() as ctx:
        x = sbuf(nc, ctx, "d_x", [TOKW, TOKT, MODEL])
        acc = sbuf(nc, ctx, "d_acc", [TOKW, TOKT, MODEL])
        xsq = sbuf(nc, ctx, "d_xsq", [TOKW, TOKT, MODEL])
        ms = sbuf(nc, ctx, "d_ms", [TOKW, 3, TOKT])
        tn = sbuf(nc, ctx, "d_tn", [TOKW, TOKT, MODEL])
        tTh = sbuf(nc, ctx, "d_tTh", [P, KT, CHUNK], F32R)
        tTl = sbuf(nc, ctx, "d_tTl", [P, KT, CHUNK], F32R)
        lg = sbuf(nc, ctx, "d_lg", [TOKW, TOKT, NEXP])
        gt = sbuf(nc, ctx, "d_gt", [TOKW, TOKT, NEXP, NEXP])
        eqm = sbuf(nc, ctx, "d_eqm", [TOKW, TOKT, NEXP, NEXP])
        rank = sbuf(nc, ctx, "d_rank", [TOKW, TOKT, NEXP])
        sel = sbuf(nc, ctx, "d_sel", [TOKW, TOKT, NEXP])
        mx = sbuf(nc, ctx, "d_mx", [TOKW, TOKT])
        ex = sbuf(nc, ctx, "d_ex", [TOKW, TOKT, NEXP])
        exs = sbuf(nc, ctx, "d_exs", [TOKW, TOKT, NEXP])
        es = sbuf(nc, ctx, "d_es", [TOKW, 2, TOKT])
        cg = sbuf(nc, ctx, "d_cg", [TOKW, TOKT, NEXP])
        S = sbuf(nc, ctx, "d_S", [P, 3, CHUNK])
        Sh = sbuf(nc, ctx, "d_Sh", [P, 3, CHUNK], F32R)
        Sl = sbuf(nc, ctx, "d_Sl", [P, 3, CHUNK], F32R)
        ps = ctx.enter_context(nc.psum_tensor("psD", [P, 8, 512], F32))
        (x_loaded, b_loaded, x_sq, rms, tn_done, t_T, t_hi, t_lo, lg_done, gate, ex_done, hid_done, silu_done,
         s_hi, s_lo, y_done, acc_done, stored, rooted) = sems(
            nc, ctx, "d_x_loaded", "d_b_loaded", "d_x_sq", "d_rms", "d_tn_done", "d_t_T", "d_t_hi", "d_t_lo",
            "d_lg_done", "d_gate", "d_ex_done", "d_hid_done", "d_silu_done", "d_s_hi", "d_s_lo", "d_y_done",
            "d_acc_done", "d_stored", "d_rooted")
        block = ctx.enter_context(nc.Block())
        NB = NEXP * MT
        xs = a.xs.rearrange("(c t p) d -> c p t d", t=TOKT, p=TOKW)
        bs = a.bs.rearrange("(c t p) d -> c p t d", t=TOKT, p=TOKW)
        outc = out.rearrange("(c t p) d -> c p t d", t=TOKT, p=TOKW)

        def one(view, i):
            return view[bass.ds(i, 1)].rearrange("c p t d -> p (c t) d")

        @block.sync
        def _(sp):
            sp.dma_start(x[:], one(xs, 0)).then_inc(x_loaded, 16)
            sp.dma_start(acc[:], one(bs, 0)).then_inc(b_loaded, 16)
            with sp.Fori(1, chunks) as i:
                at = sp.snap(i)
                prev = sp.snap(i - 1)
                nx, nb_, no = one(xs, at), one(bs, at), one(outc, prev)
                sp.wait_ge(tn_done, TOKT * i)
                sp.dma_start(x[:], nx).then_inc(x_loaded, 16)
                sp.wait_ge(acc_done, NEXP * TOKT * i)
                sp.dma_start(no, acc[:]).then_inc(stored, 16)
                sp.wait_ge(stored, 16 * i)
                sp.dma_start(acc[:], nb_).then_inc(b_loaded, 16)
            sp.wait_ge(acc_done, NEXP * TOKT * chunks)
            sp.dma_start(one(outc, chunks - 1), acc[:]).then_inc(stored, 16)
            sp.wait_ge(stored, 16 * chunks)

        @block.gpsimd
        def _(pool):
            with pool.Fori(0, chunks) as i:
                pool.wait_ge(rms, i + 1)
                power(pool, ms[:, 2], ms[:, 1], v.inv_root_d).then_inc(rooted, 1)
                for b in range(NB):
                    pool.wait_ge(s_hi, NB * i + b + 1)
                    pool.tensor_tensor(Sl[:, b % 3], S[:, b % 3], Sh[:, b % 3].bitcast(F32),
                                       ALU.subtract).then_inc(s_lo, 1)

        @block.scalar
        def _(act):
            with act.Fori(0, chunks) as i:
                act.wait_ge(x_loaded, 16 * i + 16)
                for t in range(TOKT):
                    act.activation(xsq[:, t], x[:, t], ACT.Square, accum_out=ms[:, 0, t:t + 1]).then_inc(x_sq, 1)
                act.wait_ge(t_T, i + 1)
                act.activation(tTh[:], ps[:, 0:2, 0:CHUNK], ACT.Copy).then_inc(t_hi, 1)
                act.wait_ge(gate, GATE_STEPS * i + 4)
                act.activation(ex[:], exs[:], ACT.Exp).then_inc(ex_done, 1)
                for b in range(NB):
                    act.wait_ge(hid_done, NB * i + b + 1)
                    act.activation(S[:, b % 3], ps[:, b % 3, 0:CHUNK], ACT.Silu).then_inc(silu_done, 1)

        @block.vector
        def _(dve):
            with dve.Fori(0, chunks) as i:
                dve.wait_ge(x_sq, TOKT * i + TOKT)
                dve.tensor_scalar(ms[:, 1], ms[:, 0], 1.0 / MODEL, RMS_EPS, ALU.mult, ALU.add).then_inc(rms, 1)
                dve.wait_ge(rooted, i + 1)
                for t in range(TOKT):
                    dve.scalar_tensor_tensor(tn[:, t], x[:, t], ms[:, 2, t:t + 1], v.g2[:], ALU.mult,
                                             ALU.mult).then_inc(tn_done, 1)
                dve.wait_ge(t_hi, i + 1)
                dve.tensor_tensor(tTl[:], ps[:, 0:2, 0:CHUNK], tTh[:].bitcast(F32), ALU.subtract).then_inc(t_lo, 1)
                g = GATE_STEPS * i
                dve.wait_ge(lg_done, i + 1)
                dve.tensor_copy(lg[:], ps[0:TOKW, 2, 0:TOKT * NEXP].rearrange("p (t e) -> p t e", t=TOKT))\
                    .then_inc(gate, 1)
                dve.wait_ge(gate, g + 1)
                one_e = lg[:].unsqueeze(3).to_broadcast([TOKW, TOKT, NEXP, NEXP])
                other = lg[:].unsqueeze(2).to_broadcast([TOKW, TOKT, NEXP, NEXP])
                dve.tensor_reduce(mx[:], lg[:], AX.X, ALU.max).then_inc(gate, 1)
                dve.tensor_tensor(gt[:], other, one_e, ALU.is_gt).then_inc(gate, 1)
                dve.wait_ge(gate, g + 2)
                dve.tensor_tensor(exs[:], lg[:], mx[:].unsqueeze(2).to_broadcast([TOKW, TOKT, NEXP]),
                                  ALU.subtract).then_inc(gate, 1)
                dve.tensor_tensor(eqm[:], other, one_e, ALU.is_equal).then_inc(gate, 1)
                dve.wait_ge(gate, g + 5)
                dve.tensor_tensor(eqm[:], eqm[:], v.lower[:], ALU.mult).then_inc(gate, 1)
                dve.wait_ge(gate, g + 6)
                dve.tensor_tensor(gt[:], gt[:], eqm[:], ALU.add).then_inc(gate, 1)
                dve.wait_ge(gate, g + 7)
                dve.tensor_reduce(rank[:], gt[:], AX.X, ALU.add).then_inc(gate, 1)
                dve.wait_ge(gate, g + 8)
                dve.tensor_scalar(sel[:], rank[:], 2.0, None, ALU.is_lt).then_inc(gate, 1)
                dve.wait_ge(gate, g + 9)
                dve.wait_ge(ex_done, i + 1)
                dve.tensor_tensor(exs[:], ex[:], sel[:], ALU.mult).then_inc(gate, 1)
                dve.wait_ge(gate, g + 10)
                dve.tensor_reduce(es[:, 0], exs[:], AX.X, ALU.add).then_inc(gate, 1)
                dve.wait_ge(gate, g + 11)
                dve.reciprocal(es[:, 1], es[:, 0]).then_inc(gate, 1)
                dve.wait_ge(gate, g + 12)
                dve.tensor_tensor(cg[:], exs[:], es[:, 1].unsqueeze(2).to_broadcast([TOKW, TOKT, NEXP]),
                                  ALU.mult).then_inc(gate, 1)

                def add_expert(e):
                    dve.wait_ge(y_done, NEXP * i + e + 1)
                    if e:
                        dve.wait_ge(acc_done, NEXP * TOKT * i + TOKT * e)
                    for t in range(TOKT):
                        bank = 4 + 2 * (e % 2) + t // 2
                        dve.scalar_tensor_tensor(acc[:, t], ps[0:TOKW, bank, (t % 2) * MODEL:(t % 2 + 1) * MODEL],
                                                 cg[:, t, e:e + 1], acc[:, t], ALU.mult, ALU.add).then_inc(acc_done, 1)

                dve.wait_ge(gate, g + 13)
                dve.wait_ge(b_loaded, 16 * i + 16)
                for b in range(NB):
                    dve.wait_ge(silu_done, NB * i + b + 1)
                    dve.tensor_copy(Sh[:, b % 3], S[:, b % 3]).then_inc(s_hi, 1)
                    if b % MT == 1 and b >= MT:
                        add_expert(b // MT - 1)
                add_expert(NEXP - 1)

        @block.tensor
        def _(pe):
            def mm3(out, lh, ll, rh, rl, start, stop, lone=True):
                pe.matmul(out, lh, rh, start=start, stop=False, skip_group_check=not lone)
                pe.matmul(out, ll, rh, start=False, stop=False, skip_group_check=not lone)
                return pe.matmul(out, lh, rl, start=False, stop=stop, skip_group_check=not lone)

            with pe.Fori(0, chunks) as i:
                pe.wait_ge(tn_done, TOKT * i + TOKT)
                for k in range(KT):
                    for t in range(TOKT):
                        last = pe.transpose(ps[:, k, t * TOKW:(t + 1) * TOKW], tn[:, t, k * P:(k + 1) * P],
                                            v.identd[0:TOKW, 0:TOKW])
                last.then_inc(t_T, 1)
                pe.wait_ge(t_lo, i + 1)
                for t in range(TOKT):
                    c = slice(t * TOKW, (t + 1) * TOKW)
                    for k in range(KT):
                        last = mm3(ps[0:TOKW, 2, t * NEXP:(t + 1) * NEXP], tTh[:, k, c], tTl[:, k, c],
                                   v.gateh[:, k, :], v.gatel[:, k, :], k == 0, k == KT - 1)
                last.then_inc(lg_done, 1)
                pe.wait_ge(gate, GATE_STEPS * i + 1)

                def hidden(b):
                    e, m = divmod(b, MT)
                    if b >= 3:
                        pe.wait_ge(silu_done, NB * i + b - 2)
                    for k in range(KT):
                        c = slice(k * HID + m * P, k * HID + (m + 1) * P)
                        last = mm3(ps[:, b % 3, 0:CHUNK], v.w1h[:, e, c], v.w1l[:, e, c], tTh[:, k, :], tTl[:, k, :],
                                   k == 0, k == KT - 1)
                    last.then_inc(hid_done, 1)

                def output(b):
                    e, m = divmod(b, MT)
                    pe.wait_ge(s_lo, NB * i + b + 1)
                    if m == 0 and e >= 2:
                        pe.wait_ge(acc_done, NEXP * TOKT * i + TOKT * (e - 1))
                    w = slice(m * MODEL, (m + 1) * MODEL)
                    for t in range(TOKT):
                        c = slice(t * TOKW, (t + 1) * TOKW)
                        bank = 4 + 2 * (e % 2) + t // 2
                        last = mm3(ps[0:TOKW, bank, (t % 2) * MODEL:(t % 2 + 1) * MODEL], Sh[:, b % 3, c],
                                   Sl[:, b % 3, c], v.w2h[:, e, w], v.w2l[:, e, w], m == 0 and t % 2 == 0,
                                   m == MT - 1, lone=False)
                    if m == MT - 1:
                        last.then_inc(y_done, 1)

                hidden(0)
                hidden(1)
                for b in range(NB):
                    if b + 2 < NB:
                        hidden(b + 2)
                    output(b)


GATE_STEPS = 13


def build(nc, a, out):
    nb = a.x.shape[0]
    v = Names()
    with ExitStack() as ctx:
        v.cls_row = sbuf(nc, ctx, "cls_row", [1, MODEL])
        v.cls32 = sbuf(nc, ctx, "cls32", [32, MODEL])
        v.wqk = sbuf(nc, ctx, "wqk", [P, KT, 512])
        v.wv = sbuf(nc, ctx, "wv", [P, KT, 1024])
        v.wkv_bd = sbuf(nc, ctx, "wkv_bd", [P, 2 * P])
        v.wq_bd = sbuf(nc, ctx, "wq_bd", [P, P])
        v.outw = sbuf(nc, ctx, "outw", [P, 2, MODEL])
        v.wout = sbuf(nc, ctx, "wout", [P, PAIRS, MODEL])
        v.wq2 = sbuf(nc, ctx, "wq2", [P, KT, MODEL])
        v.wdkv = sbuf(nc, ctx, "wdkv", [P, KT, P])
        v.wukv = sbuf(nc, ctx, "wukv", [P, 2 * MODEL])
        v.wo = sbuf(nc, ctx, "wo", [P, KT, MODEL])
        v.g_ln = sbuf(nc, ctx, "g_ln", [P, MODEL])
        v.b_ln = sbuf(nc, ctx, "b_ln", [P, MODEL])
        v.g1 = sbuf(nc, ctx, "g1b", [P, MODEL])
        v.inv_root = sbuf(nc, ctx, "inv_root", [P, 1])
        v.root = sbuf(nc, ctx, "root", [P, 1])
        v.nbq = sbuf(nc, ctx, "nbq", [P, 1])
        v.biasr = sbuf(nc, ctx, "biasr", [P, 768], BF16)
        v.ones_bf = sbuf(nc, ctx, "ones_bf", [P, P], BF16)
        v.ident = sbuf(nc, ctx, "ident", [P, P])
        v.ident_r = sbuf(nc, ctx, "ident_r", [P, P], F32R)
        v.ident_bf = sbuf(nc, ctx, "ident_bf", [P, P], BF16)
        v.causal = sbuf(nc, ctx, "causal", [P, P + 2], BF16)
        v.half1 = sbuf(nc, ctx, "half1", [P, P])
        v.bmask = sbuf(nc, ctx, "bmask", [HEADS, HEADS, DV])
        v.ewT = sbuf(nc, ctx, "ewT", [P, LT, L])
        v.kcls_bd = sbuf(nc, ctx, "kcls_bd", [P, PAIRS, HEADS], F32R)
        v.vcls_bd = sbuf(nc, ctx, "vcls_bd", [HEADS, 1024])
        v.QT = sbuf(nc, ctx, "QT", [P, PAIRS, QCOLS], F32R)
        v.oclsT = sbuf(nc, ctx, "oclsT", [P, PAIRS, nb])
        v.kclsT = sbuf(nc, ctx, "kclsT", [P, PAIRS, nb], F32R)
        load_constants(nc, v, a)
        mixer_and_attention(nc, v, a, nb)
        class_tokens(nc, v, a, nb)
        latent_attention(nc, v, a, nb)
    with ExitStack() as ctx:
        v.identd = sbuf(nc, ctx, "identd", [P, P])
        v.lower = sbuf(nc, ctx, "lower", [TOKW, TOKT, NEXP, NEXP])
        v.inv_root_d = sbuf(nc, ctx, "inv_root_d", [P, 1])
        v.g2 = sbuf(nc, ctx, "g2b", [TOKW, MODEL])
        v.gateh = sbuf(nc, ctx, "gateh", [P, KT, NEXP], F32R)
        v.gatel = sbuf(nc, ctx, "gatel", [P, KT, NEXP], F32R)
        v.w1h, v.w1l, v.w2h, v.w2l = [sbuf(nc, ctx, n, [P, NEXP, KT * HID], F32R)
                                      for n in ("w1h", "w1l", "w2h", "w2l")]
        load_experts(nc, v, a)
        experts(nc, v, a, out, a.xs.shape[0] // CHUNK)


def kernel(**inputs):
    import concourse.bacc as bacc
    from concourse.bass_utils import run_bass_kernel_spmd as run

    g = {n: np.asarray(x) for n, x in inputs.items()}
    wkv = g["L0_attn_Wkv"].reshape(MODEL, HEADS, DK + DV)
    wk, wv = wkv[:, :, :DK].reshape(MODEL, HEADS * DK), wkv[:, :, DK:].reshape(MODEL, HEADS * DV)
    arrays = {
        "x": g["x"], "cls_tok": g["cls_tok"].reshape(1, MODEL),
        "wqT": g["L0_tok_Wq_w"].T, "wkT": g["L0_tok_Wk_w"].T, "wvT": g["L0_tok_Wv_w"].T,
        "bq": g["L0_tok_Wq_b"].reshape(F, 1), "bk": g["L0_tok_Wk_b"].reshape(1, F),
        "bv": g["L0_tok_Wv_b"].reshape(1, F),
        "w_bias": g["L0_tok_w_bias"], "local_mask": g["L0_tok_local_mask"],
        "out_w": g["L0_tok_out_w"], "out_b": g["L0_tok_out_b"].reshape(1, MODEL),
        "ln_g": g["L0_tok_ln_g"].reshape(1, MODEL), "ln_b": g["L0_tok_ln_b"].reshape(1, MODEL),
        "wqk": np.concatenate([g["L0_attn_Wq"], wk], axis=1), "wv": wv, "wout": g["L0_attn_Wout"],
        "g1": g["L0_ffn_g1"].reshape(1, MODEL), "ffn_wq": g["L0_ffn_Wq"], "wdkv": g["L0_ffn_Wdkv"],
        "wukv": np.concatenate([g["L0_ffn_Wuk"], g["L0_ffn_Wuv"]], axis=1), "wo": g["L0_ffn_Wo"],
        "g2": g["L0_ffn_g2"].reshape(1, MODEL), "gate_w": g["L0_ffn_gate_w"], "w1": g["L0_ffn_w1"],
        "w2": g["L0_ffn_w2"],
    }
    nb = g["x"].shape[0]
    rows = -(-nb * SEQ // CHUNK) * CHUNK
    nc = bacc.Bacc("TRN2", target_bir_lowering=False, num_devices=1)
    args, launched = {}, {}
    for name, x in arrays.items():
        x = np.ascontiguousarray(x)
        launched["in_" + name] = x
        args[name] = nc.dram_tensor("in_" + name, x.shape, mybir.dt.from_np(x.dtype), kind="ExternalInput").ap()
    a = Names()
    a.x = args["x"]
    a.cls_tok = args["cls_tok"]
    a.wqT = args["wqT"]
    a.wkT = args["wkT"]
    a.wvT = args["wvT"]
    a.bq = args["bq"]
    a.bk = args["bk"]
    a.bv = args["bv"]
    a.w_bias = args["w_bias"]
    a.local_mask = args["local_mask"]
    a.out_w = args["out_w"]
    a.out_b = args["out_b"]
    a.ln_g = args["ln_g"]
    a.ln_b = args["ln_b"]
    a.wqk = args["wqk"]
    a.wv = args["wv"]
    a.wout = args["wout"]
    a.g1 = args["g1"]
    a.ffn_wq = args["ffn_wq"]
    a.wdkv = args["wdkv"]
    a.wukv = args["wukv"]
    a.wo = args["wo"]
    a.g2 = args["g2"]
    a.gate_w = args["gate_w"]
    a.w1 = args["w1"]
    a.w2 = args["w2"]
    a.xs = nc.dram_tensor("xs", (rows, MODEL), F32, kind="Internal").ap()
    a.bs = nc.dram_tensor("bs", (rows, MODEL), F32, kind="Internal").ap()
    a.hs = nc.dram_tensor("hs", (nb, P, LT * MODEL), F32, kind="Internal").ap()
    a.vcls_attn = nc.dram_tensor("vcls_attn", (1, HEADS * DV), F32, kind="Internal").ap()
    a.vcls_mla = nc.dram_tensor("vcls_mla", (nb, MODEL), F32, kind="Internal").ap()
    out = nc.dram_tensor("out_rows", (rows, MODEL), F32, kind="ExternalOutput").ap()
    build(nc, a, out)
    r = run(nc, [launched], core_ids=[0])
    return r.results[0]["out_rows"][:nb * SEQ].reshape(nb, SEQ, MODEL)
```

```python
from contextlib import ExitStack

import numpy as np
import concourse.bass as bass
from concourse import mybir


class Names:
    pass

F32 = mybir.dt.float32
F32R = mybir.dt.float32r
BF16 = mybir.dt.bfloat16
U8 = mybir.dt.uint8
I32 = mybir.dt.int32
ALU = mybir.AluOpType
ACT = mybir.ActivationFunctionType
AX = mybir.AxisListType

P = 128
F, L, H = 64, 256, 4
MODEL = F * H
KT = MODEL // P
LT = L // P
SEQ = L + 1
HEADS, DK, DV = 16, 16, 64
PAIRS = HEADS // 2
GROUPS = HEADS // 4
QCOLS = L + 2
NEXP, HID = 8, 512
MT = HID // P
TOKT, TOKW = 4, 121
CHUNK = TOKT * TOKW
LN_EPS, RMS_EPS, L2_EPS = 1e-5, 1e-6, 1e-12
MASKED = -1e30
ROOT_GUESS = 0x5F3759DF
ROOT_STEPS = 12
TINY = 1e-36


def sbuf(nc, ctx, name, shape, dt=F32):
    return ctx.enter_context(nc.sbuf_tensor(name, shape, dt))


def release(nc, held):
    nc.clear_and_free_semaphores(held)
    nc.all_engine_barrier()


def sems(nc, ctx, *names):
    held = [nc.alloc_semaphore(n) for n in names]
    ctx.callback(release, nc, held)
    return held


def power(pool, out, x, exponent):
    e = exponent[0:out.shape[0], :]
    while len(e.shape) < len(out.shape):
        e = e.unsqueeze(len(e.shape))
    return pool.tensor_tensor(out, x, e.to_broadcast(list(out.shape)), ALU.pow)


def inverse_root(dve, y, x, work, stepped, before):
    bits, minus_half, square = work[0].bitcast(I32), work[1], work[0]
    dve.tensor_scalar(bits, x.bitcast(I32), 1, None, ALU.logical_shift_right).then_inc(stepped, 1)
    dve.tensor_scalar(minus_half, x, -0.5, None, ALU.mult).then_inc(stepped, 1)
    dve.wait_ge(stepped, before + 2)
    dve.tensor_scalar(y.bitcast(I32), bits, -1, ROOT_GUESS, ALU.mult, ALU.add).then_inc(stepped, 1)
    for n in range(3):
        dve.wait_ge(stepped, before + 3 + 3 * n)
        dve.tensor_tensor(square, y, y, ALU.mult).then_inc(stepped, 1)
        dve.wait_ge(stepped, before + 4 + 3 * n)
        dve.tensor_tensor(square, square, minus_half, ALU.mult).then_inc(stepped, 1)
        dve.wait_ge(stepped, before + 5 + 3 * n)
        dve.scalar_tensor_tensor(y, square, 1.5, y, ALU.add, ALU.mult).then_inc(stepped, 1)


def load_constants(nc, v, a):
    with ExitStack() as ctx:
        wb = sbuf(nc, ctx, "wb", [P, LT, L])
        mask8 = sbuf(nc, ctx, "mask8", [P, LT, L], U8)
        maskf = sbuf(nc, ctx, "maskf", [P, LT, L])
        brow = sbuf(nc, ctx, "brow", [P, 768])
        bpart = sbuf(nc, ctx, "bpart", [P, 3, 768], BF16)
        brest = sbuf(nc, ctx, "brest", [P, 2, 768])
        bq = sbuf(nc, ctx, "bq", [P, 1])
        stats = sbuf(nc, ctx, "c_stats", [1, 6])
        mv = sbuf(nc, ctx, "c_mv", [1, 2])
        rstd = sbuf(nc, ctx, "c_rstd", [1, 2])
        cn = sbuf(nc, ctx, "cn", [1, MODEL])
        cnT = sbuf(nc, ctx, "cnT", [P, KT])
        sq = sbuf(nc, ctx, "c_sq", [1, 1536])
        ss = sbuf(nc, ctx, "c_ss", [1, 48])
        rn = sbuf(nc, ctx, "c_rn", [1, 48])
        qkn = sbuf(nc, ctx, "c_qkn", [1, 512])
        vn = sbuf(nc, ctx, "c_vn", [1, 1024])
        hl = sbuf(nc, ctx, "c_hl", [1, 2 * HEADS, 4, DK], F32R)
        kcol = sbuf(nc, ctx, "kcol", [P, PAIRS])
        vb = sbuf(nc, ctx, "c_vb", [HEADS, 1024])
        ps = ctx.enter_context(nc.psum_tensor("ps0", [P, 8, 512], F32))
        (zeroed, tables, ld_bd, ld_w, ld_mask, ld_bias, ld_cls, ld_vcls, st_vcls, mask_f, wb_ready, wbT, bias_split,
         cls_stats, cls_norm, cls_T, cls_Tc, cls_proj, cls_sq, cls_ss, cls_rn, cls_unit, cls_hl, cls_hlT,
         cls_col, identr, cls_lift, cls_rstd, powers) = sems(
            nc, ctx, "zeroed", "tables", "ld_bd", "ld_w", "ld_mask", "ld_bias", "ld_cls", "ld_vcls", "st_vcls",
            "mask_f", "wb_ready", "wbT", "bias_split", "cls_stats", "cls_norm", "cls_T", "cls_Tc", "cls_proj",
            "cls_sq", "cls_ss", "cls_rn", "cls_unit", "cls_hl", "cls_hlT", "cls_col", "identr", "cls_lift", "cls_rstd", "powers")
        block = ctx.enter_context(nc.Block())

        @block.sync
        def _(sp):
            sp.dma_start(v.cls_row[:], a.cls_tok).then_inc(ld_cls, 16)
            sp.dma_start(v.wqk[:], a.wqk.rearrange("(k p) n -> p k n", p=P)).then_inc(ld_cls, 16)
            sp.dma_start(v.wv[:], a.wv.rearrange("(k p) n -> p k n", p=P)).then_inc(ld_cls, 16)
            sp.dma_start(wb[:], a.w_bias.rearrange("(t p) s -> p t s", p=P)).then_inc(ld_mask, 16)
            sp.dma_start(mask8[:], a.local_mask.rearrange("(t p) s -> p t s", p=P)).then_inc(ld_mask, 16)
            for n, b in enumerate((a.bk, a.bk, a.bv, a.bv, a.bk, a.bk, a.bv, a.bv)):
                sp.dma_start(brow[:, n * F:(n + 1) * F], b.partition_broadcast(P)).then_inc(ld_bias, 16)
            sp.dma_start(brow[:, 512:768], a.out_b.partition_broadcast(P)).then_inc(ld_bias, 16)
            for hh in range(2):
                sp.dma_start(bq[hh * F:(hh + 1) * F, :], a.bq).then_inc(ld_bias, 16)
            sp.wait_ge(zeroed, 8)
            for hh in range(2):
                rows = slice(hh * F, (hh + 1) * F)
                sp.dma_start(v.wkv_bd[rows, hh * F:(hh + 1) * F], a.wkT).then_inc(ld_bd, 16)
                sp.dma_start(v.wkv_bd[rows, P + hh * F:P + (hh + 1) * F], a.wvT).then_inc(ld_bd, 16)
                sp.dma_start(v.wq_bd[rows, hh * F:(hh + 1) * F], a.wqT).then_inc(ld_bd, 16)
            sp.wait_ge(ld_bd, 96)
            for dst, src in ((v.g_ln, a.ln_g), (v.b_ln, a.ln_b), (v.g1, a.g1)):
                sp.dma_start(dst[:], src.partition_broadcast(P)).then_inc(ld_w, 16)
            sp.dma_start(v.cls32[:], a.cls_tok.partition_broadcast(32)).then_inc(ld_w, 16)
            sp.dma_start(v.outw[:], a.out_w.rearrange("(k p) n -> p k n", p=P)).then_inc(ld_w, 16)
            sp.dma_start(v.wout[:], a.wout.rearrange("(k p) n -> p k n", p=P)).then_inc(ld_w, 16)
            sp.dma_start(v.wq2[:], a.ffn_wq.rearrange("(k p) n -> p k n", p=P)).then_inc(ld_w, 16)
            sp.dma_start(v.wdkv[:], a.wdkv.rearrange("(k p) n -> p k n", p=P)).then_inc(ld_w, 16)
            sp.dma_start(v.wukv[:], a.wukv).then_inc(ld_w, 16)
            sp.dma_start(v.wo[:], a.wo.rearrange("(k p) n -> p k n", p=P)).then_inc(ld_w, 16)
            wo_rows = a.wo.rearrange("(g q d) n -> q d g n", q=4, d=DK)
            for q in range(4):
                sp.dma_start(v.wo_pad[32 * q:32 * q + DK], wo_rows[q]).then_inc(ld_w, 16)
            sp.wait_ge(cls_unit, 2)
            sp.dma_start(a.vcls_attn, vn[:]).then_inc(st_vcls, 16)
            sp.wait_ge(st_vcls, 16)
            sp.dma_start(vb[:], a.vcls_attn.partition_broadcast(HEADS)).then_inc(ld_vcls, 16)
            sp.wait_ge(ld_w, 224)

        @block.gpsimd
        def _(pool):
            pool.memset(v.inv_root[:], -0.5).then_inc(powers, 1)
            pool.memset(v.root[:], 0.5).then_inc(powers, 1)
            pool.memset(v.ident[:], 0.0).then_inc(zeroed, 1)
            pool.memset(v.wkv_bd[:], 0.0).then_inc(zeroed, 1)
            pool.memset(v.wq_bd[:], 0.0).then_inc(zeroed, 1)
            pool.memset(v.kmask[:], 0.0).then_inc(zeroed, 1)
            pool.memset(v.biasr[:], 0.0).then_inc(zeroed, 1)
            pool.memset(v.bmask[:], 1.0).then_inc(zeroed, 1)
            pool.memset(v.wo_pad[:], 0.0).then_inc(zeroed, 1)
            pool.memset(v.zero_bf[:], 0.0).then_inc(zeroed, 1)
            pool.memset(v.causal[:], 0.0).then_inc(zeroed, 1)
            pool.memset(v.half1[:], 0.0).then_inc(zeroed, 1)
            pool.memset(v.ones_bf[:], 1.0).then_inc(zeroed, 1)
            pool.memset(v.QT[:].bitcast(F32), 0.0).then_inc(zeroed, 1)
            pool.wait_ge(zeroed, 12)
            pool.affine_select(out=v.ident[:], in_=v.ident[:], compare_op=ALU.not_equal, fill=1.0, base=0,
                               pattern=[[-1, P]], channel_multiplier=1).then_inc(tables, 1)
            for hh in range(2):
                rows = slice(64 * hh, 64 * hh + 64)
                pool.wait_ge(tables, 1 + hh)
                pool.affine_select(out=v.kmask[rows], in_=v.kmask[rows], compare_op=ALU.not_equal, fill=1.0, base=hh,
                                   pattern=[[2, PAIRS], [-1, HEADS]], channel_multiplier=0).then_inc(tables, 1)
            pool.wait_ge(tables, 3)
            pool.affine_select(out=v.bmask[:], in_=v.bmask[:], compare_op=ALU.is_equal, fill=0.0, base=0,
                               pattern=[[1, HEADS], [0, DV]], channel_multiplier=-1).then_inc(tables, 1)
            pool.wait_ge(tables, 4)
            pool.affine_select(out=v.causal[:], in_=v.causal[:], compare_op=ALU.is_ge, fill=MASKED, base=1,
                               pattern=[[-1, P + 2]], channel_multiplier=1).then_inc(tables, 1)
            for hh in range(2):
                rows = slice(64 * hh, 64 * hh + 64)
                pool.wait_ge(tables, 5 + hh)
                pool.memset(v.half1[rows, 64 * hh:64 * hh + 64], 1.0).then_inc(tables, 1)
            pool.wait_ge(tables, 7)
            pool.tensor_copy(v.ident_r[:], v.ident[:]).then_inc(identr, 1)
            pool.tensor_copy(v.ident_bf[:], v.ident[:]).then_inc(identr, 1)
            pool.tensor_copy(v.sel[:], v.bmask[:, :, 0:32]).then_inc(identr, 1)
            pool.tensor_copy(v.bmask_r[:], v.bmask[0:8, 0:8, :].rearrange("p h d -> p (h d)")).then_inc(identr, 1)
            pool.wait_ge(powers, 2)
            pool.wait_ge(identr, 4)
            pool.wait_ge(cls_stats, 3)
            power(pool, rstd[:, 0:1], rstd[:, 1:2], v.inv_root).then_inc(cls_rstd, 1)
            pool.wait_ge(cls_rstd, 1)
            pool.wait_ge(cls_lift, 1)
            power(pool, rn[:], ss[:], v.inv_root).then_inc(cls_rn, 1)
            pool.wait_ge(cls_rn, 1)
            pool.wait_ge(ld_vcls, 16)
            pool.tensor_tensor(v.vcls_bd[:], vb[:], v.bmask[:].rearrange("p h d -> p (h d)"),
                               ALU.mult).then_inc(identr, 1)

        @block.scalar
        def _(act):
            act.wait_ge(wbT, 1)
            for s in range(LT):
                act.activation(v.ewT[:, s, :], ps[:, s, 0:L], ACT.Exp)
            act.wait_ge(cls_proj, 1)
            act.activation(sq[:, 0:512], ps[0:1, 3, :], ACT.Square).then_inc(cls_sq, 1)
            act.activation(sq[:, 512:1536], ps[0:1, 4:6, :].rearrange("p a n -> p (a n)"),
                           ACT.Square).then_inc(cls_sq, 1)

        @block.vector
        def _(dve):
            dve.wait_ge(ld_cls, 48)
            dve.bn_stats(stats[:], v.cls_row[:]).then_inc(cls_stats, 1)
            dve.wait_ge(cls_stats, 1)
            dve.bn_aggr(mv[:], stats[:]).then_inc(cls_stats, 1)
            dve.wait_ge(cls_stats, 2)
            dve.tensor_scalar(rstd[:, 1:2], mv[:, 1:2], LN_EPS, None, ALU.add).then_inc(cls_stats, 1)
            dve.wait_ge(cls_rstd, 1)
            dve.tensor_scalar(cn[:], v.cls_row[:], mv[:, 0:1], rstd[:, 0:1], ALU.subtract,
                              ALU.mult).then_inc(cls_norm, 1)
            dve.wait_ge(ld_mask, 32)
            dve.tensor_copy(maskf[:], mask8[:]).then_inc(mask_f, 1)
            dve.wait_ge(mask_f, 1)
            dve.tensor_tensor(wb[:], wb[:], maskf[:], ALU.mult).then_inc(wb_ready, 1)
            dve.wait_ge(ld_bias, 176)
            dve.tensor_copy(bpart[:, 0, :], brow[:]).then_inc(bias_split, 1)
            dve.wait_ge(bias_split, 1)
            dve.tensor_tensor(brest[:, 0, :], brow[:], bpart[:, 0, :], ALU.subtract).then_inc(bias_split, 1)
            dve.wait_ge(bias_split, 2)
            dve.tensor_copy(bpart[:, 1, :], brest[:, 0, :]).then_inc(bias_split, 1)
            dve.wait_ge(bias_split, 3)
            dve.tensor_tensor(brest[:, 1, :], brest[:, 0, :], bpart[:, 1, :], ALU.subtract).then_inc(bias_split, 1)
            dve.wait_ge(bias_split, 4)
            dve.tensor_copy(bpart[:, 2, :], brest[:, 1, :]).then_inc(bias_split, 1)
            dve.wait_ge(bias_split, 5)
            dve.wait_ge(zeroed, 11)
            for n in range(3):
                dve.tensor_copy(v.biasr[32 * n:32 * n + 1, :], bpart[32 * n:32 * n + 1, n, :])
            dve.tensor_scalar(v.nbq[:], bq[:], -1.0, None, ALU.mult)
            dve.wait_ge(ld_w, 224)
            dve.tensor_scalar(v.wq2[:], v.wq2[:], DK ** -0.5, None, ALU.mult)
            dve.wait_ge(cls_T, 1)
            dve.tensor_copy(cnT[:], ps[:, 2, 0:KT]).then_inc(cls_Tc, 1)
            dve.wait_ge(cls_sq, 2)
            dve.tensor_reduce(ss[:, 0:32], sq[:, 0:512].rearrange("p (g d) -> p g d", d=DK), AX.X,
                              ALU.add).then_inc(cls_ss, 1)
            dve.tensor_reduce(ss[:, 32:48], sq[:, 512:1536].rearrange("p (g d) -> p g d", d=DV), AX.X,
                              ALU.add).then_inc(cls_ss, 1)
            dve.wait_ge(cls_ss, 2)
            dve.tensor_scalar(ss[:], ss[:], L2_EPS ** 2, None, ALU.max).then_inc(cls_lift, 1)
            dve.wait_ge(cls_rn, 1)
            dve.tensor_tensor(qkn[:].rearrange("p (g d) -> p g d", d=DK),
                              ps[0:1, 3, :].rearrange("p (g d) -> p g d", d=DK),
                              rn[:, 0:32].unsqueeze(2).to_broadcast([1, 32, DK]), ALU.mult).then_inc(cls_unit, 1)
            dve.tensor_tensor(vn[:].rearrange("p (g d) -> p g d", d=DV),
                              ps[0:1, 4:6, :].rearrange("p a (g d) -> p (a g) d", d=DV),
                              rn[:, 32:48].unsqueeze(2).to_broadcast([1, 16, DV]), ALU.mult).then_inc(cls_unit, 1)
            dve.wait_ge(cls_unit, 2)
            g = qkn[:].rearrange("p (g d) -> p g d", d=DK)
            for q in range(2):
                heads = slice(q * HEADS, (q + 1) * HEADS)
                dve.tensor_copy(blocks(hl[:, heads], q, 0), twice(g[:, heads])).then_inc(cls_hl, 1)
            dve.wait_ge(cls_hl, 2)
            for q in range(2):
                heads = slice(q * HEADS, (q + 1) * HEADS)
                dve.tensor_tensor(blocks(hl[:, heads], q, 1), twice(g[:, heads]),
                                  blocks(hl[:, heads], q, 0).bitcast(F32), ALU.subtract).then_inc(cls_hl, 1)
            dve.wait_ge(cls_hlT, 1)
            dve.wait_ge(zeroed, 12)
            dve.tensor_copy(v.QT[:, :, L], ps[:, 6, 0:PAIRS]).then_inc(cls_col, 1)
            dve.tensor_copy(kcol[:], ps[:, 6, PAIRS:2 * PAIRS]).then_inc(cls_col, 1)
            dve.wait_ge(cls_col, 2)
            dve.wait_ge(tables, 3)
            dve.tensor_tensor(v.kcls_bd[:], v.kmask[:], kcol[:].unsqueeze(2).to_broadcast([P, PAIRS, HEADS]), ALU.mult)

        @block.tensor
        def _(pe):
            pe.wait_ge(tables, 7)
            pe.wait_ge(wb_ready, 1)
            for s in range(LT):
                for t in range(LT):
                    last = pe.transpose(ps[:, s, t * P:(t + 1) * P], wb[:, t, s * P:(s + 1) * P], v.ident[:])
            last.then_inc(wbT, 1)
            pe.wait_ge(cls_norm, 1)
            for k in range(KT):
                last = pe.transpose(ps[:, 2, k:k + 1], cn[:, k * P:(k + 1) * P], v.ident[0:1, 0:1])
            last.then_inc(cls_T, 1)
            pe.wait_ge(cls_Tc, 1)
            for k in range(KT):
                pe.matmul(ps[0:1, 3, :], cnT[:, k:k + 1], v.wqk[:, k, :], start=k == 0, stop=k == KT - 1)
            for n in range(2):
                for k in range(KT):
                    last = pe.matmul(ps[0:1, 4 + n, :], cnT[:, k:k + 1], v.wv[:, k, n * 512:(n + 1) * 512],
                                     start=k == 0, stop=k == KT - 1)
            last.then_inc(cls_proj, 1)
            pe.wait_ge(cls_hl, 4)
            pe.wait_ge(identr, 1)
            hf = hl[:].bitcast(F32)
            for q in range(2):
                for pr in range(PAIRS):
                    g0 = q * HEADS + 2 * pr
                    last = pe.transpose(ps[:, 6, q * PAIRS + pr:q * PAIRS + pr + 1],
                                        hf[:, g0:g0 + 2].rearrange("p g a d -> p (g a d)"), v.ident[0:1, 0:1])
            last.then_inc(cls_hlT, 1)


def blocks(hl, is_key, low):
    if is_key:
        return hl.rearrange("p g (a b) d -> p g a b d", b=2)[:, :, :, int(low), :]
    return hl[:, :, 2 * low:2 * low + 2, :]


def twice(x):
    r, g, d = x.shape
    return x.unsqueeze(2).to_broadcast([r, g, 2, d])


def mixer_and_attention(nc, v, a, nb):
    with ExitStack() as ctx:
        idle = sbuf(nc, ctx, "idle", [1, 1])
        xraw = sbuf(nc, ctx, "xraw", [P, L * H + 8])
        x2 = sbuf(nc, ctx, "x2", [P, 2, L])
        ekv = sbuf(nc, ctx, "ekv", [P, LT, 2, 2, P])
        eq = sbuf(nc, ctx, "eq", [P, 2, L])
        den = sbuf(nc, ctx, "den", [P, 2, L])
        rden = sbuf(nc, ctx, "rden", [P, 2, L])
        yT = sbuf(nc, ctx, "yT", [P, 2, L])
        stats = sbuf(nc, ctx, "stats", [P, LT, 6])
        mv = sbuf(nc, ctx, "mv", [P, LT, 2])
        rstd = sbuf(nc, ctx, "rstd", [P, 2, LT])
        ln = sbuf(nc, ctx, "ln", [P, LT, MODEL])
        h1 = sbuf(nc, ctx, "h1", [P, LT, MODEL])
        stats2 = sbuf(nc, ctx, "stats2", [P, LT, 6])
        mv2 = sbuf(nc, ctx, "mv2", [P, LT, 2])
        rstd2 = sbuf(nc, ctx, "rstd2", [P, 2, LT])
        xn = sbuf(nc, ctx, "xn", [P, LT, MODEL])
        xT = sbuf(nc, ctx, "xT", [P, KT, L])
        sq = sbuf(nc, ctx, "sq", [P, LT, 1536])
        ss = sbuf(nc, ctx, "ss", [P, LT, 32])
        vss = sbuf(nc, ctx, "vss", [P, LT, HEADS])
        ssm = sbuf(nc, ctx, "ssm", [P, LT, 32])
        vssm = sbuf(nc, ctx, "vssm", [P, LT, HEADS])
        rn = sbuf(nc, ctx, "rn", [P, LT, 32])
        vrn = sbuf(nc, ctx, "vrn", [P, LT, HEADS])
        qkn = sbuf(nc, ctx, "qkn", [P, LT, 512])
        hl = sbuf(nc, ctx, "hl", [P, LT, 2 * HEADS, 4, DK], F32R)
        V = sbuf(nc, ctx, "V", [P, LT, HEADS * DV])
        KTr = sbuf(nc, ctx, "KTr", [P, PAIRS, L], F32R)
        R = sbuf(nc, ctx, "R", [P, 2, LT, QCOLS])
        PR = sbuf(nc, ctx, "PR", [P, 3, LT, QCOLS])
        rcl = sbuf(nc, ctx, "rcl", [HEADS, QCOLS])
        pcl = sbuf(nc, ctx, "pcl", [HEADS, QCOLS])
        oTs = sbuf(nc, ctx, "oTs", [P, PAIRS, QCOLS])
        osq = sbuf(nc, ctx, "osq", [P, 2, L])
        osm = sbuf(nc, ctx, "osm", [P, 2, LT * 8])
        orr = sbuf(nc, ctx, "orr", [P, 2, LT * 8])
        orn = sbuf(nc, ctx, "orn", [P, 2, LT * 8])
        nwork = sbuf(nc, ctx, "nwork", [P, 2, LT * 32])
        onm = sbuf(nc, ctx, "onm", [P, 2, LT * 8])
        oth = sbuf(nc, ctx, "oth", [P, 2, LT * 8])
        osc = sbuf(nc, ctx, "osc", [P, 2, LT * 8])
        sc_hi = sbuf(nc, ctx, "sc_hi", [8, 2, L], F32R)
        sc_lo = sbuf(nc, ctx, "sc_lo", [8, 2, L], F32R)
        OT = sbuf(nc, ctx, "OT", [P, PAIRS, L])
        h2 = sbuf(nc, ctx, "h2", [P, LT * MODEL])
        ps = ctx.enter_context(nc.psum_tensor("psA", [P, 8, 512], F32))
        (qkT_copied, v_ss, v_lift, v_rn, x_loaded, x2_ready, kvq_done, ek_done, eq_done, ev_done, den_done, num_done, den_t, den_r, y_done, hpre_done,
         ln_stats, ln_done, h1_done, ln2_stats, xn_done, xn_T, xT_done, qk_done, v_done, qk_sq, v_sq, qk_ss,
         qk_rn, qk_unit, v_unit, qk_hi, qk_lo, qkT_done, pcl_sim, pcl_relu, pcl_done, sim_done, relu_done,
         prob_done, av_done, o_copied, o_sq, o_ss, o_norms, o_tanh, o_scale, sc_turned, sc_split, sc_spread,
         ocl_copied, oT_done,
         out_done, h2_done, h2_stored, ln_rooted, ln2_rooted, qk_lift, o_lift, o_rooted) = sems(
            nc, ctx, "qkT_copied", "v_ss", "v_lift", "v_rn", "x_loaded", "x2_ready", "kvq_done", "ek_done", "eq_done", "ev_done", "den_done", "num_done", "den_t",
            "den_r", "y_done", "hpre_done", "ln_stats", "ln_done", "h1_done", "ln2_stats", "xn_done",
            "xn_T", "xT_done", "qk_done", "v_done", "qk_sq", "v_sq", "qk_ss", "qk_rn", "qk_unit", "v_unit", "qk_hi",
            "qk_lo", "qkT_done", "pcl_sim", "pcl_relu", "pcl_done", "sim_done", "relu_done",
            "prob_done", "av_done", "o_copied", "o_sq", "o_ss", "o_norms", "o_tanh", "o_scale", "sc_turned",
            "sc_split", "sc_spread", "ocl_copied", "oT_done", "out_done", "h2_done", "h2_stored", "ln_rooted", "ln2_rooted",
            "qk_lift", "o_lift", "o_rooted")
        block = ctx.enter_context(nc.Block())
        x_flat = a.x.rearrange("n c l h -> n c (l h)")
        TURN_BANKS = (0, 1, 6, 7)

        def load_x(sp, i):
            src = x_flat[bass.ds(i, 1)].rearrange("n c m -> c (n m)")
            sp.dma_start(xraw[0:F, 4:4 + L * H], src).then_inc(x_loaded, 16)
            sp.dma_start(xraw[F:P, 3:3 + L * H], src).then_inc(x_loaded, 16)

        def low_parts(eng, i, t):
            for q in range(2):
                eng.wait_ge(qk_hi, 4 * i + 2 * t + q + 1)
                src = qkn[:, t, q * 256:(q + 1) * 256].rearrange("p (g d) -> p g d", d=DK)
                heads = slice(q * HEADS, (q + 1) * HEADS)
                eng.tensor_tensor(blocks(hl[:, t, heads], q, 1), twice(src),
                                  blocks(hl[:, t, heads], q, 0).bitcast(F32), ALU.subtract).then_inc(qk_lo, 1)

        @block.sync
        def _(sp):
            load_x(sp, 0)
            with sp.Fori(1, nb) as i:
                at, prev = sp.snap(i), sp.snap(i - 1)
                sp.wait_ge(x2_ready, i)
                load_x(sp, at)
                sp.wait_ge(h2_done, i)
                sp.dma_start(a.hs[bass.ds(prev, 1)].rearrange("n p m -> p (n m)"), h2[:]).then_inc(h2_stored, 16)
            sp.wait_ge(h2_done, nb)
            sp.dma_start(a.hs[nb - 1], h2[:]).then_inc(h2_stored, 16)
            sp.wait_ge(h2_stored, 16 * nb + 1)

        @block.gpsimd
        def _(pool):
            with pool.Fori(0, nb) as i:
                pool.wait_ge(ln_stats, 5 * i + 5)
                power(pool, rstd[:, 1], rstd[:, 0], v.inv_root).then_inc(ln_rooted, 1)
                pool.wait_ge(ln2_stats, 5 * i + 5)
                power(pool, rstd2[:, 1], rstd2[:, 0], v.inv_root).then_inc(ln2_rooted, 1)
                low_parts(pool, i, 0)

        @block.scalar
        def _(act):
            with act.Fori(0, nb) as i:
                act.wait_ge(kvq_done, i + 1)
                for t in range(LT):
                    act.activation(ekv[:, t, 0], ps[:, t, :].rearrange("p (a n) -> p a n", a=2)[:, :, 0:P],
                                   ACT.Exp).then_inc(ek_done, 1)
                act.activation(eq[:], ps[:, 2, :].rearrange("p (a n) -> p a n", a=2), ACT.Exp, bias=v.nbq[:],
                               scale=-1.0).then_inc(eq_done, 1)
                act.wait_ge(xn_T, i + 1)
                act.activation(xT[:], ps[:, 7, :].rearrange("p (k n) -> p k n", k=KT), ACT.Copy).then_inc(xT_done, 1)
                act.wait_ge(qk_done, i + 1)
                act.activation(sq[:, :, 0:512], ps[:, 0:2, :], ACT.Square).then_inc(qk_sq, 1)

                def value_squares(t):
                    act.wait_ge(v_done, LT * i + t + 1)
                    act.activation(sq[:, t, 512:1536].rearrange("p (a n) -> p a n", a=2),
                                   ps[:, 2 + 2 * t:4 + 2 * t, :], ACT.Square).then_inc(v_sq, 1)

                value_squares(0)
                act.wait_ge(qk_unit, i + 1)
                for t in range(LT):
                    for q in range(2):
                        src = qkn[:, t, q * 256:(q + 1) * 256].rearrange("p (g d) -> p g d", d=DK)
                        act.activation(blocks(hl[:, t, q * HEADS:(q + 1) * HEADS], q, 0), twice(src),
                                       ACT.Copy).then_inc(qk_hi, 1)
                value_squares(1)
                for n in range(8):
                    act.wait_ge(qkT_done, 8 * i + n + 1)
                    dst = (v.QT if n < 4 else KTr)[:, 2 * (n % 4):2 * (n % 4) + 2, 0:L]
                    act.activation(dst, ps[:, TURN_BANKS[n % 4], :].rearrange("p (a n) -> p a n", a=2),
                                   ACT.Copy).then_inc(qkT_copied, 1)
                act.wait_ge(pcl_sim, i + 1)
                act.activation(rcl[:], ps[0:HEADS, 7, 0:QCOLS], ACT.Relu).then_inc(pcl_relu, 1)

                def relu(h):
                    act.wait_ge(sim_done, HEADS * i + h + 1)
                    act.wait_ge(prob_done, HEADS * i + h + 1)
                    b = 2 * (h % 2)
                    act.activation(R[:, h % 2], ps[:, b:b + 2, 0:QCOLS], ACT.Relu).then_inc(relu_done, 1)

                def take_outputs(pr):
                    act.wait_ge(av_done, PAIRS * i + pr + 1)
                    act.activation(oTs[:, pr], ps[:, 4 + pr % 2, 0:QCOLS], ACT.Copy).then_inc(o_copied, 1)
                    if pr >= 2:
                        act.wait_ge(o_ss, PAIRS * i + pr - 1)
                    act.activation(osq[:, pr % 2], ps[:, 4 + pr % 2, 0:L], ACT.Square).then_inc(o_sq, 1)

                def norm_tanh(g):
                    act.wait_ge(o_norms, 4 * i + 2 * g + 2)
                    act.activation(oth[:, g], onm[:, g], ACT.Tanh).then_inc(o_tanh, 1)

                relu(0)
                for pr in range(PAIRS):
                    relu(2 * pr + 1)
                    if pr >= 1:
                        take_outputs(pr - 1)
                    if pr == 6:
                        norm_tanh(0)
                    if pr < PAIRS - 1:
                        relu(2 * pr + 2)
                take_outputs(PAIRS - 1)
                norm_tanh(1)

        @block.vector
        def _(dve):
            dve.memset(PR[:], 0.0).then_inc(prob_done, 1)
            dve.memset(R[:], 0.0).then_inc(prob_done, 1)
            dve.sem_inc(h2_stored, 1)

            def layer_norm_stats(i, src, st, mvt, rs, sem):
                for t in range(LT):
                    dve.bn_stats(st[:, t], src[t]).then_inc(sem, 1)
                dve.wait_ge(sem, 5 * i + 2)
                dve.memset(idle[:], 0.0)
                for t in range(LT):
                    dve.bn_aggr(mvt[:, t], st[:, t]).then_inc(sem, 1)
                dve.wait_ge(sem, 5 * i + 4)
                dve.tensor_scalar(rs[:, 0], mvt[:, :, 1], LN_EPS, None, ALU.add).then_inc(sem, 1)

            with dve.Fori(0, nb) as i:
                dve.wait_ge(x_loaded, 32 * i + 32)
                raw = xraw[:, 4:4 + L * H].rearrange("p (l a b) -> p a l b", a=2, b=2)[:, :, :, 0]
                dve.tensor_copy(x2[:], raw).then_inc(x2_ready, 1)
                for t in range(LT):
                    dve.wait_ge(ek_done, LT * i + t + 1)
                    dve.tensor_tensor(ekv[:, t, 1], ps[:, t, :].rearrange("p (a n) -> p a n", a=2)[:, :, P:2 * P],
                                      ekv[:, t, 0], ALU.mult).then_inc(ev_done, 1)
                dve.wait_ge(den_done, i + 1)
                dve.wait_ge(eq_done, i + 1)
                dve.scalar_tensor_tensor(den[:], eq[:], 1.0, ps[:, 4, :].rearrange("p (a n) -> p a n", a=2),
                                         ALU.add, ALU.mult).then_inc(den_t, 1)
                dve.wait_ge(den_t, i + 1)
                dve.reciprocal(rden[:], den[:]).then_inc(den_r, 1)
                dve.wait_ge(den_r, i + 1)
                dve.wait_ge(num_done, i + 1)
                dve.tensor_tensor(yT[:], ps[:, 3, :].rearrange("p (a n) -> p a n", a=2), rden[:],
                                  ALU.mult).then_inc(y_done, 1)
                dve.wait_ge(hpre_done, i + 1)
                mixed = [ps[:, 5, t * MODEL:(t + 1) * MODEL] for t in range(LT)]
                layer_norm_stats(i, mixed, stats, mv, rstd, ln_stats)
                for t in range(LT):
                    dve.scalar_tensor_tensor(ln[:, t], mixed[t], mv[:, t, 0:1], v.g_ln[:], ALU.subtract,
                                             ALU.mult).then_inc(ln_done, 1)
                dve.wait_ge(ln_rooted, i + 1)
                dve.wait_ge(ln_done, LT * i + LT)
                for t in range(LT):
                    dve.scalar_tensor_tensor(h1[:, t], ln[:, t], rstd[:, 1, t:t + 1], v.b_ln[:], ALU.mult,
                                             ALU.add).then_inc(h1_done, 1)
                dve.wait_ge(h1_done, LT * i + LT)
                layer_norm_stats(i, [h1[:, t] for t in range(LT)], stats2, mv2, rstd2, ln2_stats)
                dve.wait_ge(ln2_rooted, i + 1)
                for t in range(LT):
                    dve.tensor_scalar(xn[:, t], h1[:, t], mv2[:, t, 0:1], rstd2[:, 1, t:t + 1], ALU.subtract,
                                      ALU.mult).then_inc(xn_done, 1)
                dve.wait_ge(qk_sq, i + 1)
                dve.tensor_reduce(ss[:], sq[:, :, 0:512].rearrange("p t (g d) -> p t g d", d=DK), AX.X,
                                  ALU.add).then_inc(qk_ss, 1)
                dve.wait_ge(qk_ss, i + 1)
                dve.tensor_scalar(ssm[:], ss[:], L2_EPS ** 2, None, ALU.max).then_inc(qk_lift, 1)
                dve.wait_ge(qk_lift, i + 1)
                inverse_root(dve, rn[:].rearrange("p t g -> p (t g)"), ssm[:].rearrange("p t g -> p (t g)"),
                             [nwork[:, n] for n in range(2)], qk_rn, ROOT_STEPS * i)
                dve.wait_ge(qk_rn, ROOT_STEPS * (i + 1))
                dve.tensor_tensor(qkn[:].rearrange("p t (g d) -> p t g d", d=DK),
                                  ps[:, 0:2, :].rearrange("p t (g d) -> p t g d", d=DK),
                                  rn[:].unsqueeze(3).to_broadcast([P, LT, 32, DK]), ALU.mult).then_inc(qk_unit, 1)

                def value_sums(t):
                    dve.wait_ge(v_sq, LT * i + t + 1)
                    dve.tensor_reduce(vss[:, t], sq[:, t, 512:1536].rearrange("p (g d) -> p g d", d=DV), AX.X,
                                      ALU.add).then_inc(v_ss, 1)

                value_sums(0)
                low_parts(dve, i, 1)
                value_sums(1)

                def value_norms():
                    dve.wait_ge(v_ss, LT * i + LT)
                    dve.tensor_scalar(vssm[:], vss[:], L2_EPS ** 2, None, ALU.max).then_inc(v_lift, 1)
                    dve.wait_ge(v_lift, i + 1)
                    inverse_root(dve, vrn[:].rearrange("p t g -> p (t g)"), vssm[:].rearrange("p t g -> p (t g)"),
                                 [nwork[:, n, 0:LT * HEADS] for n in range(2)], v_rn, ROOT_STEPS * i)
                    dve.wait_ge(v_rn, ROOT_STEPS * (i + 1))
                    for t in range(LT):
                        dve.tensor_tensor(V[:, t].rearrange("p (g d) -> p g d", d=DV),
                                          ps[:, 2 + 2 * t:4 + 2 * t, :].rearrange("p a (g d) -> p (a g) d", d=DV),
                                          vrn[:, t].unsqueeze(2).to_broadcast([P, HEADS, DV]),
                                          ALU.mult).then_inc(v_unit, 1)

                value_norms()
                dve.wait_ge(pcl_relu, i + 1)
                dve.tensor_tensor(pcl[:], ps[0:HEADS, 7, 0:QCOLS], rcl[:], ALU.mult).then_inc(pcl_done, 1)

                def prob(h):
                    dve.wait_ge(relu_done, HEADS * i + h + 1)
                    b = 2 * (h % 2)
                    dve.tensor_tensor(PR[:, h % 3], ps[:, b:b + 2, 0:QCOLS], R[:, h % 2],
                                      ALU.mult).then_inc(prob_done, 1)

                def norms(g):
                    sums = ps[:, 6 + g, 0:LT * 8]
                    dve.wait_ge(o_ss, PAIRS * i + 4 * g + 4)
                    dve.tensor_scalar(osm[:, g], sums, TINY, None, ALU.max).then_inc(o_lift, 1)
                    dve.wait_ge(o_lift, 2 * i + g + 1)
                    inverse_root(dve, orr[:, g], osm[:, g], [nwork[:, n, 0:LT * 8] for n in range(2)], o_rooted,
                                 ROOT_STEPS * (2 * i + g))
                    dve.wait_ge(o_rooted, ROOT_STEPS * (2 * i + g + 1))
                    dve.tensor_tensor(onm[:, g], sums, orr[:, g], ALU.mult).then_inc(o_norms, 1)
                    dve.tensor_scalar(orn[:, g], orr[:, g], 1 / L2_EPS, None, ALU.min).then_inc(o_norms, 1)

                def scale(g):
                    dve.wait_ge(o_norms, 4 * i + 2 * g + 2)
                    dve.wait_ge(o_tanh, 2 * i + g + 1)
                    dve.tensor_tensor(osc[:, g], oth[:, g], orn[:, g], ALU.mult).then_inc(o_scale, 1)

                def split_scale(g):
                    turned = ps[0:8, 6 + g, P:P + L]
                    dve.wait_ge(sc_turned, 2 * i + g + 1)
                    dve.tensor_copy(sc_hi[:, g], turned).then_inc(sc_split, 1)
                    dve.wait_ge(sc_split, 4 * i + 2 * g + 1)
                    dve.tensor_tensor(sc_lo[:, g], turned, sc_hi[:, g].bitcast(F32), ALU.subtract)\
                        .then_inc(sc_split, 1)

                def scale_outputs(g):
                    for pr in range(4 * g, 4 * g + 4):
                        dve.wait_ge(sc_spread, PAIRS * i + pr + 1)
                        dve.tensor_tensor(OT[:, pr], ps[:, pr % 4, 0:L], oTs[:, pr, 0:L], ALU.mult)\
                            .then_inc(oT_done, 1)

                for h in range(12):
                    prob(h)
                norms(0)
                prob(12)
                scale(0)
                prob(13)
                prob(14)
                split_scale(0)
                prob(15)
                dve.wait_ge(o_copied, PAIRS * i + PAIRS)
                dve.tensor_copy(v.oclsT[:, :, bass.ds(i, 1)].rearrange("p a b -> p (a b)"), oTs[:, :, L])\
                    .then_inc(ocl_copied, 1)
                scale_outputs(0)
                norms(1)
                scale(1)
                split_scale(1)
                scale_outputs(1)
                dve.wait_ge(out_done, i + 1)
                dve.wait_ge(h2_stored, 16 * i + 1)
                dve.tensor_tensor(h2[:], ps[:, 5, :], h1[:].rearrange("p t n -> p (t n)"), ALU.add).then_inc(h2_done, 1)

        @block.tensor
        def _(pe):
            with pe.Fori(0, nb) as i:
                pe.wait_ge(x2_ready, i + 1)
                for t in range(LT):
                    pe.matmul(ps[:, t, :], v.ones_bf[0:96, :], v.biasr[0:96, 0:512], start=True, stop=False,
                              skip_group_check=True)
                    for hp in range(2):
                        pe.matmul(ps[:, t, hp * 256:hp * 256 + 256], x2[:, hp, t * P:(t + 1) * P], v.wkv_bd[:],
                                  start=False, stop=True, skip_group_check=True)
                for hp in range(2):
                    last = pe.matmul(ps[:, 2, hp * 256:hp * 256 + 256], v.wq_bd[:], x2[:, hp, :], start=True,
                                     stop=True)
                last.then_inc(kvq_done, 1)
                for bank, kv, ready, done in ((4, 0, ek_done, den_done), (3, 1, ev_done, num_done)):
                    pe.wait_ge(ready, LT * i + LT)
                    for hp in range(2):
                        for t in range(LT):
                            last = pe.matmul(ps[:, bank, hp * L:(hp + 1) * L], ekv[:, t, kv, hp, :], v.ewT[:, t, :],
                                             start=t == 0, stop=t == LT - 1)
                    last.then_inc(done, 1)
                for t in range(LT):
                    pe.matmul(ps[:, 5, t * MODEL:(t + 1) * MODEL], v.ones_bf[0:96, :], v.biasr[0:96, 512:768],
                              start=t == 0, stop=False, skip_group_check=True)
                for t in range(LT):
                    for hp in range(2):
                        pe.matmul(ps[:, 5, t * MODEL + hp * P:t * MODEL + hp * P + P], x2[:, hp, t * P:(t + 1) * P],
                                  v.ident[:], start=False, stop=False, skip_group_check=True)
                pe.wait_ge(y_done, i + 1)
                for t in range(LT):
                    for hp in range(2):
                        last = pe.matmul(ps[:, 5, t * MODEL:(t + 1) * MODEL], yT[:, hp, t * P:(t + 1) * P],
                                         v.outw[:, hp, :], start=False, stop=True, skip_group_check=True)
                last.then_inc(hpre_done, 1)
                pe.wait_ge(xn_done, LT * i + LT)
                for k in range(KT):
                    for t in range(LT):
                        last = pe.transpose(ps[:, 7, k * L + t * P:k * L + (t + 1) * P],
                                            xn[:, t, k * P:(k + 1) * P], v.ident[:])
                last.then_inc(xn_T, 1)
                pe.wait_ge(xT_done, i + 1)
                for t in range(LT):
                    for k in range(KT):
                        last = pe.matmul(ps[:, t, :], xT[:, k, t * P:(t + 1) * P], v.wqk[:, k, :], start=k == 0,
                                         stop=k == KT - 1)
                last.then_inc(qk_done, 1)
                for t in range(LT):
                    for n in range(2):
                        for k in range(KT):
                            last = pe.matmul(ps[:, 2 + 2 * t + n, :], xT[:, k, t * P:(t + 1) * P],
                                             v.wv[:, k, n * 512:(n + 1) * 512], start=k == 0, stop=k == KT - 1)
                    last.then_inc(v_done, 1)
                pe.wait_ge(qk_lo, 4 * i + 4)
                for n in range(8):
                    if n >= 4:
                        pe.wait_ge(qkT_copied, 8 * i + n - 3)
                    for j in range(2):
                        for t in range(LT):
                            g0 = HEADS * (n // 4) + 2 * (2 * (n % 4) + j)
                            last = pe.transpose(ps[:, TURN_BANKS[n % 4], j * L + t * P:j * L + (t + 1) * P].bitcast(F32R),
                                                hl[:, t, g0:g0 + 2].rearrange("p g a d -> p (g a d)"),
                                                v.ident_r[:])
                    last.then_inc(qkT_done, 1)
                pe.wait_ge(qkT_copied, 8 * i + 8)
                for pr in range(PAIRS):
                    last = pe.matmul(ps[0:HEADS, 7, 0:QCOLS], v.kcls_bd[:, pr, :], v.QT[:, pr, :], start=pr == 0,
                                     stop=pr == PAIRS - 1)
                last.then_inc(pcl_sim, 1)

                def sim(h):
                    rows = slice(64 * (h % 2), 64 * (h % 2) + 64)
                    if h >= 2:
                        pe.wait_ge(prob_done, HEADS * i + h + 1)
                    for t in range(LT):
                        last = pe.matmul(ps[:, 2 * (h % 2) + t, 0:QCOLS], KTr[rows, h // 2, t * P:(t + 1) * P],
                                         v.QT[rows, h // 2, :], start=True, stop=True)
                    last.then_inc(sim_done, 1)

                def values(h):
                    pe.wait_ge(prob_done, HEADS * i + h + 3)
                    rows = slice(64 * (h % 2), 64 * (h % 2) + 64)
                    for jt in range(LT):
                        last = pe.matmul(ps[rows, 4 + h // 2 % 2, 0:QCOLS], V[:, jt, h * DV:(h + 1) * DV],
                                         PR[:, h % 3, jt, :], start=False, stop=True, skip_group_check=True)
                    return last

                def square_sums(pr):
                    pe.wait_ge(o_sq, PAIRS * i + pr + 1)
                    for t in range(LT):
                        last = pe.matmul(ps[:, 6 + pr // 4, t * 8:t * 8 + 8], osq[:, pr % 2, t * P:(t + 1) * P],
                                         v.kmask[:, pr % 4, 0:8], start=pr % 4 == 0 and t == 0, stop=True,
                                         skip_group_check=True)
                    last.then_inc(o_ss, 1)

                def turn_scale(g):
                    pe.wait_ge(o_scale, 2 * i + g + 1)
                    for t in range(LT):
                        last = pe.transpose(ps[0:8, 6 + g, P + t * P:P + (t + 1) * P], osc[:, g, t * 8:t * 8 + 8],
                                            v.ident[:])
                    last.then_inc(sc_turned, 1)

                def spread_scale(g):
                    pe.wait_ge(sc_split, 4 * i + 2 * g + 2)
                    for pr in range(4):
                        if g == 1:
                            pe.wait_ge(oT_done, PAIRS * i + pr + 1)
                        ind = v.bmask_r[:, pr * P:(pr + 1) * P]
                        pe.matmul(ps[:, pr, 0:L], ind, sc_hi[:, g], start=True, stop=False)
                        pe.matmul(ps[:, pr, 0:L], ind, sc_lo[:, g], start=False, stop=True).then_inc(sc_spread, 1)

                def project(g):
                    for pr in range(4 * g, 4 * g + 4):
                        pe.wait_ge(oT_done, PAIRS * i + pr + 1)
                        for t in range(LT):
                            last = pe.matmul(ps[:, 5, t * MODEL:(t + 1) * MODEL], OT[:, pr, t * P:(t + 1) * P],
                                             v.wout[:, pr, :], start=pr == 0 and t == 0, stop=pr == PAIRS - 1,
                                             skip_group_check=True)
                    return last

                sim(0)
                pe.wait_ge(v_unit, LT * i + LT)
                sim(1)
                pe.wait_ge(pcl_done, i + 1)
                for pr in range(PAIRS):
                    if pr >= 2:
                        pe.wait_ge(o_copied, PAIRS * i + pr - 1)
                        pe.wait_ge(o_sq, PAIRS * i + pr - 1)
                    pe.matmul(ps[:, 4 + pr % 2, 0:QCOLS], v.vcls_bd[:, pr * P:(pr + 1) * P], pcl[:], start=True,
                              stop=False, skip_group_check=True)
                    for h in (2 * pr, 2 * pr + 1):
                        last = values(h)
                        if h % 2:
                            last.then_inc(av_done, 1)
                        if h + 2 < HEADS:
                            sim(h + 2)
                    if pr >= 1:
                        square_sums(pr - 1)
                    if pr == 6:
                        turn_scale(0)
                pe.wait_ge(prob_done, HEADS * i + HEADS + 2)
                spread_scale(0)
                square_sums(PAIRS - 1)
                project(0)
                turn_scale(1)
                spread_scale(1)
                project(1).then_inc(out_done, 1)


def class_tokens(nc, v, a, nb):
    NP = PAIRS * nb
    with ExitStack() as ctx:
        sq = sbuf(nc, ctx, "b_sq", [P, NP])
        ssum = sbuf(nc, ctx, "b_ssum", [P, NP])
        ssm = sbuf(nc, ctx, "b_ssm", [P, NP])
        nrm = sbuf(nc, ctx, "b_nrm", [P, NP])
        rnm = sbuf(nc, ctx, "b_rnm", [P, NP])
        th = sbuf(nc, ctx, "b_th", [P, NP])
        sc = sbuf(nc, ctx, "b_sc", [P, NP])
        on = sbuf(nc, ctx, "b_on", [P, PAIRS, nb])
        h2c = sbuf(nc, ctx, "b_h2", [nb, MODEL])
        stats = sbuf(nc, ctx, "b_stats", [nb, 6])
        mv = sbuf(nc, ctx, "b_mv", [nb, 2])
        rstd = sbuf(nc, ctx, "b_rstd", [nb, 5])
        y = sbuf(nc, ctx, "b_y", [nb, MODEL])
        ysq = sbuf(nc, ctx, "b_ysq", [nb, MODEL])
        hn = sbuf(nc, ctx, "b_hn", [nb, MODEL])
        hT = sbuf(nc, ctx, "b_hT", [P, KT, nb])
        cT = sbuf(nc, ctx, "b_cT", [P, nb])
        hl = sbuf(nc, ctx, "b_hl", [nb, HEADS, 4, DK], F32R)
        vrow = sbuf(nc, ctx, "b_v", [nb, MODEL])
        vT = sbuf(nc, ctx, "b_vT", [P, KT, nb])
        x = sbuf(nc, ctx, "b_x", [nb, MODEL])
        base = sbuf(nc, ctx, "b_base", [nb, MODEL])
        ps = ctx.enter_context(nc.psum_tensor("psB", [P, 8, 512], F32))
        (squared, norms_sum, norms, tanhed, scaled, unit, attn_out, h2_done, stat, y_done, ysq_done, rms, hn_done,
         hn_T, hT_done, c_done, cT_done, kv_done, k_hi, k_lo, v_copied, kT_done, k_copied, vT_done, v_turned,
         o_done, x_done, stored, lifted, rooted) = sems(
            nc, ctx, "b_squared", "b_norms_sum", "b_norms", "b_tanhed", "b_scaled", "b_unit", "b_attn_out",
            "b_h2_done", "b_stat", "b_y_done", "b_ysq_done", "b_rms", "b_hn_done", "b_hn_T", "b_hT_done", "b_c_done",
            "b_cT_done", "b_kv_done", "b_k_hi", "b_k_lo", "b_v_copied", "b_kT_done", "b_k_copied", "b_vT_done",
            "b_v_turned", "b_o_done", "b_x_done", "b_stored",
            "b_lifted", "b_rooted")
        block = ctx.enter_context(nc.Block())
        oc = v.oclsT[:].rearrange("p a b -> p (a b)")

        @block.sync
        def _(sp):
            sp.wait_ge(v_copied, 1)
            sp.dma_start(a.vcls_mla[0:nb], vrow[:]).then_inc(stored, 16)
            sp.wait_ge(x_done, 2)
            rows = a.xs[0:nb * SEQ].rearrange("(n s) d -> n s d", s=SEQ)[:, 0, :]
            sp.dma_start(rows, x[:]).then_inc(stored, 16)
            rows = a.bs[0:nb * SEQ].rearrange("(n s) d -> n s d", s=SEQ)[:, 0, :]
            sp.dma_start(rows, base[:]).then_inc(stored, 16)
            sp.wait_ge(stored, 48)

        @block.gpsimd
        def _(pool):
            pool.wait_ge(lifted, 2)
            power(pool, nrm[:], ssum[:], v.root).then_inc(norms, 1)
            power(pool, rnm[:], ssm[:], v.inv_root).then_inc(norms, 1)
            pool.wait_ge(stat, 3)
            power(pool, rstd[:, 0:1], rstd[:, 4:5], v.inv_root).then_inc(rooted, 1)
            pool.wait_ge(rms, 2)
            power(pool, rstd[:, 3:4], rstd[:, 2:3], v.inv_root).then_inc(rooted, 1)

        @block.scalar
        def _(act):
            act.activation(sq[:], oc, ACT.Square).then_inc(squared, 1)
            act.wait_ge(norms, 1)
            act.activation(th[:], nrm[:], ACT.Tanh).then_inc(tanhed, 1)
            act.wait_ge(y_done, 1)
            act.activation(ysq[:], y[:], ACT.Square).then_inc(ysq_done, 1)

        @block.vector
        def _(dve):
            dve.wait_ge(norms_sum, 1)
            dve.tensor_copy(ssum[:], ps[:, 0, 0:NP]).then_inc(lifted, 1)
            dve.tensor_scalar(ssm[:], ps[:, 0, 0:NP], L2_EPS ** 2, None, ALU.max).then_inc(lifted, 1)
            dve.wait_ge(tanhed, 1)
            dve.wait_ge(norms, 2)
            dve.tensor_tensor(sc[:], th[:], rnm[:], ALU.mult).then_inc(scaled, 1)
            dve.wait_ge(scaled, 1)
            dve.tensor_tensor(on[:].rearrange("p a b -> p (a b)"), oc, sc[:], ALU.mult).then_inc(unit, 1)
            dve.wait_ge(attn_out, 1)
            dve.tensor_tensor(h2c[:], ps[0:nb, 1, 0:MODEL], v.cls32[0:nb, :], ALU.add).then_inc(h2_done, 1)
            dve.wait_ge(h2_done, 1)
            dve.bn_stats(stats[:], h2c[:]).then_inc(stat, 1)
            dve.wait_ge(stat, 1)
            dve.bn_aggr(mv[:], stats[:]).then_inc(stat, 1)
            dve.wait_ge(stat, 2)
            dve.tensor_scalar(rstd[:, 4:5], mv[:, 1:2], LN_EPS, None, ALU.add).then_inc(stat, 1)
            dve.wait_ge(rooted, 1)
            dve.tensor_scalar(y[:], h2c[:], mv[:, 0:1], rstd[:, 0:1], ALU.subtract, ALU.mult).then_inc(y_done, 1)
            dve.wait_ge(ysq_done, 1)
            dve.tensor_reduce(rstd[:, 1:2], ysq[:], AX.X, ALU.add).then_inc(rms, 1)
            dve.wait_ge(rms, 1)
            dve.tensor_scalar(rstd[:, 2:3], rstd[:, 1:2], 1.0 / MODEL, RMS_EPS, ALU.mult, ALU.add).then_inc(rms, 1)
            dve.wait_ge(rms, 2)
            dve.wait_ge(rooted, 2)
            dve.scalar_tensor_tensor(hn[:], y[:], rstd[:, 3:4], v.g1[0:nb, :], ALU.mult, ALU.mult).then_inc(hn_done, 1)
            dve.wait_ge(hn_T, 1)
            dve.tensor_copy(hT[:], ps[:, 2, 0:KT * nb].rearrange("p (k n) -> p k n", k=KT)).then_inc(hT_done, 1)
            dve.wait_ge(c_done, 1)
            dve.tensor_copy(cT[:], ps[:, 3, 0:nb]).then_inc(cT_done, 1)
            dve.wait_ge(kv_done, 1)
            k = ps[0:nb, 4, 0:MODEL].rearrange("p (g d) -> p g d", d=DK)
            dve.tensor_copy(blocks(hl[:], 1, 0), twice(k)).then_inc(k_hi, 1)
            dve.tensor_copy(vrow[:], ps[0:nb, 4, MODEL:2 * MODEL]).then_inc(v_copied, 1)
            dve.wait_ge(k_hi, 1)
            dve.tensor_tensor(blocks(hl[:], 1, 1), twice(k), blocks(hl[:], 1, 0).bitcast(F32),
                              ALU.subtract).then_inc(k_lo, 1)
            dve.wait_ge(vT_done, 1)
            dve.tensor_copy(vT[:], ps[:, 5, 0:KT * nb].rearrange("p (k n) -> p k n", k=KT)).then_inc(v_turned, 1)
            dve.wait_ge(kT_done, 1)
            dve.tensor_copy(v.kclsT[:], ps[:, 6, 0:NP].rearrange("p (a b) -> p a b", a=PAIRS)).then_inc(k_copied, 1)
            dve.wait_ge(o_done, 1)
            dve.tensor_tensor(x[:], ps[0:nb, 7, 0:MODEL], y[:], ALU.add).then_inc(x_done, 1)
            dve.wait_ge(x_done, 1)
            dve.tensor_tensor(base[:], x[:], h2c[:], ALU.add).then_inc(x_done, 1)

        @block.tensor
        def _(pe):
            pe.wait_ge(squared, 1)
            pe.matmul(ps[:, 0, 0:NP], v.half1[:], sq[:], start=True, stop=True).then_inc(norms_sum, 1)
            pe.wait_ge(unit, 1)
            for pr in range(PAIRS):
                last = pe.matmul(ps[0:nb, 1, 0:MODEL], on[:, pr, :], v.wout[:, pr, :], start=pr == 0,
                                 stop=pr == PAIRS - 1)
            last.then_inc(attn_out, 1)
            pe.wait_ge(hn_done, 1)
            for k in range(KT):
                last = pe.transpose(ps[:, 2, k * nb:(k + 1) * nb], hn[:, k * P:(k + 1) * P], v.ident[0:nb, 0:nb])
            last.then_inc(hn_T, 1)
            pe.wait_ge(hT_done, 1)
            for k in range(KT):
                last = pe.matmul(ps[:, 3, 0:nb], v.wdkv[:, k, :], hT[:, k, :], start=k == 0, stop=k == KT - 1)
            last.then_inc(c_done, 1)
            pe.wait_ge(cT_done, 1)
            pe.matmul(ps[0:nb, 4, :], cT[:], v.wukv[:], start=True, stop=True).then_inc(kv_done, 1)
            pe.wait_ge(v_copied, 1)
            for k in range(KT):
                last = pe.transpose(ps[:, 5, k * nb:(k + 1) * nb], vrow[:, k * P:(k + 1) * P], v.ident[0:nb, 0:nb])
            last.then_inc(vT_done, 1)
            pe.wait_ge(k_lo, 1)
            hf = hl[:].bitcast(F32)
            for pr in range(PAIRS):
                last = pe.transpose(ps[:, 6, pr * nb:(pr + 1) * nb], hf[:, 2 * pr:2 * pr + 2].rearrange("p g a d -> p (g a d)"),
                                    v.ident[0:nb, 0:nb])
            last.then_inc(kT_done, 1)
            pe.wait_ge(v_turned, 1)
            for k in range(KT):
                last = pe.matmul(ps[0:nb, 7, 0:MODEL], vT[:, k, :], v.wo[:, k, :], start=k == 0, stop=k == KT - 1)
            last.then_inc(o_done, 1)


def latent_attention(nc, v, a, nb):
    with ExitStack() as ctx:
        stats = sbuf(nc, ctx, "m_stats", [P, LT, 6])
        idle = sbuf(nc, ctx, "m_idle", [1, 1])
        h2 = sbuf(nc, ctx, "m_h2", [P, LT, MODEL])
        hy = sbuf(nc, ctx, "m_hy", [P, LT, MODEL])
        y_kept = sbuf(nc, ctx, "m_y_kept", [P, LT, MODEL])
        mv = sbuf(nc, ctx, "m_mv", [P, LT, 2])
        rstd = sbuf(nc, ctx, "m_rstd", [P, 2, LT])
        y = sbuf(nc, ctx, "m_y", [P, LT, MODEL])
        ysq = sbuf(nc, ctx, "m_ysq", [P, LT, MODEL])
        ms = sbuf(nc, ctx, "m_ms", [P, 3, LT])
        hn = sbuf(nc, ctx, "m_hn", [P, LT, MODEL])
        hT = sbuf(nc, ctx, "m_hT", [P, KT, L])
        cT = sbuf(nc, ctx, "m_cT", [P, L])
        hl = sbuf(nc, ctx, "m_hl", [P, LT, 2 * HEADS, 4, DK], F32R)
        V = sbuf(nc, ctx, "m_V", [P, LT, MODEL])
        KTr = sbuf(nc, ctx, "m_KT", [P, PAIRS, QCOLS], F32R)
        nmax = sbuf(nc, ctx, "m_nmax", [P, LT, HEADS])
        esum = sbuf(nc, ctx, "m_esum", [P, LT, HEADS])
        PM = sbuf(nc, ctx, "m_P", [P, 2, 2, QCOLS])
        pc = sbuf(nc, ctx, "m_pc", [P, LT, HEADS])
        pcT = sbuf(nc, ctx, "m_pcT", [HEADS, L])
        PT = sbuf(nc, ctx, "m_PT", [P, 2, 512])
        vb = sbuf(nc, ctx, "m_vb", [HEADS, MODEL])
        vcb = sbuf(nc, ctx, "m_vcb", [HEADS, HEADS, 32])
        resum = sbuf(nc, ctx, "m_resum", [P, LT, HEADS])
        rs_hi = sbuf(nc, ctx, "m_rs_hi", [HEADS, L], F32R)
        rs_lo = sbuf(nc, ctx, "m_rs_lo", [HEADS, L], F32R)
        rsb = sbuf(nc, ctx, "m_rsb", [P, GROUPS, L])
        oT = sbuf(nc, ctx, "m_oT", [P, GROUPS, L])
        x = sbuf(nc, ctx, "m_x", [P, LT, MODEL])
        base = sbuf(nc, ctx, "m_base", [P, LT, MODEL])
        pad = a.xs.shape[0] - nb * SEQ
        zparts = max(n for n in range(1, P + 1) if pad % n == 0)
        zrow = sbuf(nc, ctx, "m_zrow", [zparts, pad // zparts * MODEL])
        ps = ctx.enter_context(nc.psum_tensor("psC", [P, 8, 512], F32))
        (v_loaded, vcb_done, ln_stats, y_done, ysq_done, rms, hn_done, hn_T, hT_done, cq_done, cT_done, kv_done,
         qk_hi, qk_lo, v_copied, qkT_done, qT_act, qT_dve, kcls_done, s_done, max_done, exp_done, pc_done, pT_done,
         pT_copied, o_done, pcT_done, pcT_copied, resum_done, rs_turned, rs_split, rs_spread,
         rs_copied, oT_done, wo_done, x_done,
         base_done, stored, pad_done, rooted, h2_loaded, hy_done, y_copied) = sems(
            nc, ctx, "m_v_loaded", "m_vcb_done", "m_ln_stats", "m_y_done", "m_ysq_done", "m_rms", "m_hn_done",
            "m_hn_T", "m_hT_done", "m_cq_done", "m_cT_done", "m_kv_done", "m_qk_hi", "m_qk_lo", "m_v_copied",
            "m_qkT_done", "m_qT_act", "m_qT_dve", "m_kcls_done", "m_s_done", "m_max_done", "m_exp_done", "m_pc_done",
            "m_pT_done", "m_pT_copied", "m_o_done", "m_pcT_done", "m_pcT_copied", "m_resum_done", "m_rs_turned",
            "m_rs_split", "m_rs_spread", "m_rs_copied", "m_oT_done", "m_wo_done", "m_x_done", "m_base_done", "m_stored", "m_pad_done", "m_rooted",
            "m_h2_loaded", "m_hy_done", "m_y_copied")
        block = ctx.enter_context(nc.Block())
        UNITS = [(hp, t) for hp in range(PAIRS) for t in range(LT)]
        KEYS = [P + 2, QCOLS]
        NU = len(UNITS)

        def q_psum(t):
            return ps[:, 0, t * MODEL:(t + 1) * MODEL].rearrange("p (g d) -> p g d", d=DK)

        def k_psum(t):
            return ps[:, 1 + t, 0:MODEL].rearrange("p (g d) -> p g d", d=DK)

        xs_rows = a.xs[0:nb * SEQ].rearrange("(n s) d -> n s d", s=SEQ)[:, 1:SEQ, :]
        bs_rows = a.bs[0:nb * SEQ].rearrange("(n s) d -> n s d", s=SEQ)[:, 1:SEQ, :]

        @block.sync
        def _(sp):
            sp.wait_ge(pad_done, 2)
            sp.dma_start(a.xs[nb * SEQ:nb * SEQ + pad].rearrange("(p r) d -> p (r d)", p=zparts), zrow[:]).then_inc(stored, 16)
            sp.dma_start(a.bs[nb * SEQ:nb * SEQ + pad].rearrange("(p r) d -> p (r d)", p=zparts), zrow[:]).then_inc(stored, 16)
            sp.dma_start(h2[:].rearrange("p t n -> p (t n)"), a.hs[0]).then_inc(h2_loaded, 16)

            def value_and_results(i):
                sp.wait_ge(vcb_done, i + 1)
                sp.dma_start(vb[:], a.vcls_mla[bass.ds(i, 1)].partition_broadcast(HEADS)).then_inc(v_loaded, 16)
                out_x = xs_rows[bass.ds(i, 1)].rearrange("n (t p) d -> p (n t) d", p=P)
                out_b = bs_rows[bass.ds(i, 1)].rearrange("n (t p) d -> p (n t) d", p=P)
                sp.wait_ge(x_done, i + 1)
                sp.dma_start(out_x, x[:]).then_inc(stored, 16)
                sp.wait_ge(base_done, i + 2)
                sp.dma_start(out_b, base[:]).then_inc(stored, 16)

            with sp.Fori(0, nb - 1) as i:
                at, nxt = sp.snap(i), sp.snap(i + 1)
                sp.wait_ge(hy_done, i + 1)
                sp.dma_start(h2[:].rearrange("p t n -> p (t n)"),
                             a.hs[bass.ds(nxt, 1)].rearrange("n p m -> p (n m)")).then_inc(h2_loaded, 16)
                value_and_results(at)
            value_and_results(nb - 1)
            sp.wait_ge(h2_loaded, 16 * nb)
            sp.wait_ge(stored, 32 * nb + 32)

        @block.gpsimd
        def _(pool):
            pool.memset(KTr[:].bitcast(F32), 0.0).then_inc(pad_done, 1)
            pool.memset(zrow[:], 0.0).then_inc(pad_done, 1)
            pool.memset(vcb[:], 0.0).then_inc(vcb_done, 1)
            pool.sem_inc(base_done, 1)

            def roots(j):
                pool.wait_ge(ln_stats, 5 * j + 5)
                power(pool, rstd[:, 1], rstd[:, 0], v.inv_root).then_inc(rooted, 1)
                pool.wait_ge(rms, j + 1)
                power(pool, ms[:, 2], ms[:, 1], v.inv_root).then_inc(rooted, 1)

            def keep(i):
                pool.wait_ge(y_done, LT * i + LT)
                pool.wait_ge(base_done, i + 1)
                pool.tensor_tensor(hy[:], h2[:], y[:], ALU.add).then_inc(hy_done, 1)
                pool.tensor_copy(y_kept[:], y[:]).then_inc(y_copied, 1)
                pool.wait_ge(kv_done, i + 1)
                pool.wait_ge(v_loaded, 16 * i + 16)
                pool.tensor_tensor(vcb[:, :, 0:DK],
                                   vb[:].rearrange("p (h d) -> p h d", d=DK), v.bmask[:, :, 0:DK],
                                   ALU.mult).then_inc(vcb_done, 1)

            roots(0)
            with pool.Fori(0, nb - 1) as i:
                keep(i)
                roots(i + 1)
            keep(nb - 1)

        @block.scalar
        def _(act):
            def squares(j):
                for t in range(LT):
                    act.wait_ge(y_done, LT * j + t + 1)
                    act.activation(ysq[:, t], y[:, t], ACT.Square, accum_out=ms[:, 0, t:t + 1]).then_inc(ysq_done, 1)

            def sample(i, more):
                act.wait_ge(hn_T, i + 1)
                act.activation(hT[:], ps[:, 6, :].rearrange("p (k n) -> p k n", k=KT), ACT.Copy).then_inc(hT_done, 1)
                act.wait_ge(cq_done, i + 1)
                act.activation(cT[:], ps[:, 7, 0:L], ACT.Copy).then_inc(cT_done, 1)
                for t in range(LT):
                    act.activation(blocks(hl[:, t, 0:HEADS], 0, 0), twice(q_psum(t)),
                                   ACT.Copy).then_inc(qk_hi, 1)
                act.wait_ge(kv_done, i + 1)
                for t in range(LT):
                    act.activation(blocks(hl[:, t, HEADS:2 * HEADS], 1, 0), twice(k_psum(t)),
                                   ACT.Copy).then_inc(qk_hi, 1)
                act.activation(V[:], ps[:, 1:3, MODEL:2 * MODEL], ACT.Copy).then_inc(v_copied, 1)
                for n in range(0, 8, 2):
                    act.wait_ge(qkT_done, 8 * i + n + 1)
                    j = 2 * (n % 4)
                    dst = v.QT[:, j:j + 2, 0:L] if n < 4 else KTr[:, j:j + 2, 1:1 + L]
                    act.activation(dst, ps[:, n % 4, :].rearrange("p (a n) -> p a n", a=2),
                                   ACT.Copy).then_inc(qT_act, 1)
                for u, (hp, t) in enumerate(UNITS):
                    act.wait_ge(max_done, NU * i + u + 1)
                    act.wait_ge(pT_done, NU * i + u + 1)
                    if u >= 2:
                        act.wait_ge(pc_done, NU * i + u - 1)
                    N = KEYS[t]
                    b = 2 * (u % 2)
                    for hh in range(2):
                        h = 2 * hp + hh
                        act.activation(PM[:, u % 2, hh, 0:N - 1], ps[:, b + hh, 0:N - 1], ACT.Exp,
                                       bias=nmax[:, t, h:h + 1], accum_out=esum[:, t, h:h + 1]).then_inc(exp_done, 1)
                    if more and u == 8:
                        squares(i + 1)
                act.wait_ge(pcT_done, i + 1)
                act.activation(pcT[:], ps[0:HEADS, 4, 0:L], ACT.Copy).then_inc(pcT_copied, 1)
                for g in range(GROUPS):
                    act.wait_ge(rs_spread, GROUPS * i + g + 1)
                    act.activation(rsb[:, g], ps[:, g, 0:L], ACT.Copy).then_inc(rs_copied, 1)

            squares(0)
            with act.Fori(0, nb - 1) as i:
                sample(i, True)
            sample(nb - 1, False)

        @block.vector
        def _(dve):
            def norm_stats(j):
                dve.wait_ge(h2_loaded, 16 * j + 16)
                for t in range(LT):
                    dve.bn_stats(stats[:, t], h2[:, t]).then_inc(ln_stats, 1)
                dve.wait_ge(ln_stats, 5 * j + 2)
                dve.memset(idle[:], 0.0)
                for t in range(LT):
                    dve.bn_aggr(mv[:, t], stats[:, t]).then_inc(ln_stats, 1)
                dve.wait_ge(ln_stats, 5 * j + 4)
                dve.tensor_scalar(rstd[:, 0], mv[:, :, 1], LN_EPS, None, ALU.add).then_inc(ln_stats, 1)

            def normalise(j, first=False):
                dve.wait_ge(rooted, 2 * j + 1)
                if not first:
                    dve.wait_ge(hy_done, j)
                    dve.wait_ge(y_copied, j)
                for t in range(LT):
                    dve.tensor_scalar(y[:, t], h2[:, t], mv[:, t, 0:1], rstd[:, 1, t:t + 1], ALU.subtract,
                                      ALU.mult).then_inc(y_done, 1)

            def mean_square(j):
                dve.wait_ge(ysq_done, LT * j + LT)
                dve.tensor_scalar(ms[:, 1], ms[:, 0], 1.0 / MODEL, RMS_EPS, ALU.mult, ALU.add).then_inc(rms, 1)

            def rms_norm(j, first=False):
                dve.wait_ge(rooted, 2 * j + 2)
                if not first:
                    dve.wait_ge(hn_T, j)
                for t in range(LT):
                    dve.scalar_tensor_tensor(hn[:, t], y[:, t], ms[:, 2, t:t + 1], v.g1[:], ALU.mult,
                                             ALU.mult).then_inc(hn_done, 1)

            def sample(i, more):
                dve.wait_ge(qk_hi, 4 * i + LT)
                for t in range(LT):
                    dve.tensor_tensor(blocks(hl[:, t, 0:HEADS], 0, 1), twice(q_psum(t)),
                                      blocks(hl[:, t, 0:HEADS], 0, 0).bitcast(F32), ALU.subtract).then_inc(qk_lo, 1)
                dve.wait_ge(v_copied, i + 1)
                for t in range(LT):
                    dve.tensor_tensor(blocks(hl[:, t, HEADS:2 * HEADS], 1, 1), twice(k_psum(t)),
                                      blocks(hl[:, t, HEADS:2 * HEADS], 1, 0).bitcast(F32),
                                      ALU.subtract).then_inc(qk_lo, 1)
                dve.tensor_copy(KTr[:, :, 0], v.kclsT[:, :, bass.ds(i, 1)].rearrange("p a b -> p (a b)"))\
                    .then_inc(kcls_done, 1)
                for n in range(1, 8, 2):
                    dve.wait_ge(qkT_done, 8 * i + n + 1)
                    j = 2 * (n % 4)
                    dst = v.QT[:, j:j + 2, 0:L] if n < 4 else KTr[:, j:j + 2, 1:1 + L]
                    dve.tensor_copy(dst, ps[:, n % 4, :].rearrange("p (a n) -> p a n", a=2)).then_inc(qT_dve, 1)

                def copy_back(u):
                    t = UNITS[u][1]
                    dve.wait_ge(pT_done, NU * i + u + 3)
                    n = 256 * (t + 1)
                    dve.tensor_copy(PT[:, u % 2, 0:n], ps[:, 4 + u % 2, 0:n]).then_inc(pT_copied, 1)
                    dve.tensor_copy(pc[:, t, 2 * UNITS[u][0]:2 * UNITS[u][0] + 2],
                                    PM[:, u % 2, :, 0]).then_inc(pc_done, 1)

                for u, (hp, t) in enumerate(UNITS):
                    dve.wait_ge(s_done, NU * i + u + 1)
                    b = 2 * (u % 2)
                    dve.tensor_reduce(nmax[:, t, 2 * hp:2 * hp + 2], ps[:, b:b + 2, 0:KEYS[t] - 1], AX.X, ALU.max,
                                      negate=True).then_inc(max_done, 1)
                    if u:
                        copy_back(u - 1)
                    if more:
                        if u == 4:
                            norm_stats(i + 1)
                        elif u == 6:
                            normalise(i + 1)
                        elif u == 10:
                            mean_square(i + 1)
                        elif u == 12:
                            rms_norm(i + 1)
                copy_back(NU - 1)
                dve.wait_ge(exp_done, 2 * NU * (i + 1))
                dve.reciprocal(resum[:], esum[:]).then_inc(resum_done, 1)
                dve.wait_ge(rs_turned, i + 1)
                dve.tensor_copy(rs_hi[:], ps[0:HEADS, 5, 0:L]).then_inc(rs_split, 1)
                dve.wait_ge(rs_split, 2 * i + 1)
                dve.tensor_tensor(rs_lo[:], ps[0:HEADS, 5, 0:L], rs_hi[:].bitcast(F32),
                                  ALU.subtract).then_inc(rs_split, 1)
                dve.wait_ge(o_done, i + 1)
                for g in range(GROUPS):
                    dve.wait_ge(rs_copied, GROUPS * i + g + 1)
                    dve.tensor_tensor(oT[:, g], ps[:, 6 + g // 2, g % 2 * L:(g % 2 + 1) * L], rsb[:, g],
                                      ALU.mult).then_inc(oT_done, 1)
                dve.wait_ge(wo_done, i + 1)
                dve.wait_ge(stored, 32 * i + 32)
                dve.wait_ge(y_copied, i + 1)
                dve.tensor_tensor(x[:], ps[:, 5, :].rearrange("p (t n) -> p t n", t=LT), y_kept[:],
                                  ALU.add).then_inc(x_done, 1)
                dve.wait_ge(hy_done, i + 1)
                dve.tensor_tensor(base[:], ps[:, 5, :].rearrange("p (t n) -> p t n", t=LT), hy[:],
                                  ALU.add).then_inc(base_done, 1)

            norm_stats(0)
            normalise(0, first=True)
            mean_square(0)
            rms_norm(0, first=True)
            with dve.Fori(0, nb - 1) as i:
                sample(i, True)
            sample(nb - 1, False)

        @block.tensor
        def _(pe):
            pe.sem_inc(pT_done, 2)
            with pe.Fori(0, nb) as i:
                pe.wait_ge(hn_done, LT * i + LT)
                for k in range(KT):
                    for t in range(LT):
                        last = pe.transpose(ps[:, 6, k * L + t * P:k * L + (t + 1) * P],
                                            hn[:, t, k * P:(k + 1) * P], v.ident[:])
                last.then_inc(hn_T, 1)
                pe.wait_ge(hT_done, i + 1)
                for k in range(KT):
                    pe.matmul(ps[:, 7, 0:L], v.wdkv[:, k, :], hT[:, k, :], start=k == 0, stop=k == KT - 1)
                for t in range(LT):
                    for k in range(KT):
                        last = pe.matmul(ps[:, 0, t * MODEL:(t + 1) * MODEL], hT[:, k, t * P:(t + 1) * P],
                                         v.wq2[:, k, :], start=k == 0, stop=k == KT - 1)
                last.then_inc(cq_done, 1)
                pe.wait_ge(cT_done, i + 1)
                for t in range(LT):
                    last = pe.matmul(ps[:, 1 + t, :], cT[:, t * P:(t + 1) * P], v.wukv[:], start=True, stop=True)
                last.then_inc(kv_done, 1)
                pe.wait_ge(v_copied, i + 1)
                pe.wait_ge(qk_lo, 4 * i + 4)
                for n in range(8):
                    if n >= 4:
                        pe.wait_ge(qT_dve if n % 2 else qT_act, 4 * i + n // 2 - 1)
                    for j in range(2):
                        for t in range(LT):
                            g0 = HEADS * (n // 4) + 2 * (2 * (n % 4) + j)
                            last = pe.transpose(ps[:, n % 4, j * L + t * P:j * L + (t + 1) * P].bitcast(F32R),
                                                hl[:, t, g0:g0 + 2].rearrange("p g a d -> p (g a d)"),
                                                v.ident_r[:])
                    last.then_inc(qkT_done, 1)
                pe.wait_ge(qT_act, 4 * i + 4)
                pe.wait_ge(qT_dve, 4 * i + 4)
                pe.wait_ge(kcls_done, i + 1)

                def scores(u):
                    hp, t = UNITS[u]
                    if u >= 2:
                        pe.wait_ge(exp_done, 2 * NU * i + 2 * (u - 1))
                    for hh in range(2):
                        b = 2 * (u % 2) + hh
                        rows = slice(64 * hh, 64 * hh + 64)
                        pe.matmul(ps[:, b, 0:KEYS[t]], v.QT[rows, hp, t * P:(t + 1) * P], KTr[rows, hp, 0:KEYS[t]],
                                  start=True, stop=False, skip_group_check=True)
                        last = pe.matmul(ps[:, b, t * P:t * P + P + 2], v.ident_bf[:], v.causal[:], start=False,
                                         stop=True, skip_group_check=True)
                    last.then_inc(s_done, 1)

                def turn(u):
                    hp, t = UNITS[u]
                    pe.wait_ge(exp_done, 2 * NU * i + 2 * (u + 1))
                    if u >= 2:
                        pe.wait_ge(pT_copied, NU * i + u - 1)
                    for hh in range(2):
                        for jt in range(t + 1):
                            c = (hh * (t + 1) + jt) * P
                            last = pe.transpose(ps[:, 4 + u % 2, c:c + P],
                                                PM[:, u % 2, hh, 1 + jt * P:1 + (jt + 1) * P], v.ident[:])
                    last.then_inc(pT_done, 1)

                def values(u):
                    hp, t = UNITS[u]
                    pe.wait_ge(pT_copied, NU * i + u + 1)
                    for hh in range(2):
                        h = 2 * hp + hh
                        g, rows = h // 4, slice(32 * (h % 4), 32 * (h % 4) + DK)
                        out = ps[rows, 6 + g // 2, g % 2 * L + t * P:g % 2 * L + (t + 1) * P]
                        for jt in range(t + 1):
                            c = (hh * (t + 1) + jt) * P
                            pe.matmul(out, V[:, jt, h * DK:(h + 1) * DK], PT[:, u % 2, c:c + P], start=False,
                                      stop=True, skip_group_check=True)

                for b in (6, 7):
                    pe.matmul(ps[:, b, :], v.ones_bf[0:1, :], v.zero_bf[:], start=True, stop=False,
                              skip_group_check=True)
                scores(0)
                scores(1)
                for u in range(NU):
                    turn(u)
                    if u + 2 < NU:
                        scores(u + 2)
                    if u:
                        values(u - 1)
                values(NU - 1)
                pe.wait_ge(pc_done, NU * (i + 1))
                for t in range(LT):
                    last = pe.transpose(ps[0:HEADS, 4, t * P:(t + 1) * P], pc[:, t, :], v.ident[:])
                last.then_inc(pcT_done, 1)
                pe.wait_ge(resum_done, i + 1)
                for t in range(LT):
                    last = pe.transpose(ps[0:HEADS, 5, t * P:(t + 1) * P], resum[:, t, :], v.ident[:])
                last.then_inc(rs_turned, 1)
                pe.wait_ge(pcT_copied, i + 1)
                pe.wait_ge(vcb_done, i + 2)
                for g in range(GROUPS):
                    last = pe.matmul(ps[:, 6 + g // 2, g % 2 * L:(g % 2 + 1) * L],
                                     vcb[:, 4 * g:4 * g + 4, :].rearrange("p h d -> p (h d)"), pcT[:], start=False,
                                     stop=True, skip_group_check=True)
                last.then_inc(o_done, 1)
                pe.wait_ge(rs_split, 2 * i + 2)
                for g in range(GROUPS):
                    sel = v.sel[:, 4 * g:4 * g + 4, :].rearrange("p h d -> p (h d)")
                    pe.matmul(ps[:, g, 0:L], sel, rs_hi[:], start=True, stop=False)
                    pe.matmul(ps[:, g, 0:L], sel, rs_lo[:], start=False, stop=True).then_inc(rs_spread, 1)
                for g in range(GROUPS):
                    pe.wait_ge(oT_done, GROUPS * i + g + 1)
                    for t in range(LT):
                        last = pe.matmul(ps[:, 5, t * MODEL:(t + 1) * MODEL], oT[:, g, t * P:(t + 1) * P],
                                         v.wo_pad[:, g, :], start=g == 0 and t == 0, stop=g == GROUPS - 1,
                                         skip_group_check=True)
                last.then_inc(wo_done, 1)


def load_experts(nc, v, a):
    with ExitStack() as ctx:
        NST = 4
        stage = sbuf(nc, ctx, "w_stage", [P, NST, KT * HID])
        gstage = sbuf(nc, ctx, "g_stage", [P, KT, NEXP])
        w_loaded = sems(nc, ctx, *[f"w_loaded{n}" for n in range(NST)])
        hi_done, lo_done, g_loaded, g_hi, misc = sems(nc, ctx, "w_hi", "w_lo", "g_loaded", "g_hi", "d_misc")
        block = ctx.enter_context(nc.Block())
        parts = [(v.w1h, v.w1l, e) for e in range(NEXP)] + [(v.w2h, v.w2l, e) for e in range(NEXP)]

        @block.sync
        def _(sp):
            sp.dma_start(v.g2[:], a.g2.partition_broadcast(TOKW)).then_inc(g_loaded, 16)
            sp.dma_start(gstage[:], a.gate_w.rearrange("(k p) e -> p k e", p=P)).then_inc(g_loaded, 16)
            for n, (h, _, e) in enumerate(parts):
                if n >= NST:
                    sp.wait_ge(lo_done, n - NST + 1)
                if h is v.w1h:
                    src = a.w1[e].rearrange("(k p) n -> p k n", p=P)
                    dst = stage[:, n % NST].rearrange("p (k n) -> p k n", k=KT)
                else:
                    src = a.w2[e].rearrange("(m p) d -> p m d", p=P)
                    dst = stage[:, n % NST].rearrange("p (m d) -> p m d", m=MT)
                sp.dma_start(dst, src).then_inc(w_loaded[n % NST], 16)
            sp.wait_ge(g_loaded, 32)

        @block.scalar
        def _(act):
            for n, (h, _, e) in enumerate(parts):
                act.wait_ge(w_loaded[n % NST], 16 * (n // NST + 1))
                act.activation(h[:, e], stage[:, n % NST], ACT.Copy).then_inc(hi_done, 1)

        @block.gpsimd
        def _(pool):
            pool.memset(v.lower[:], 1.0).then_inc(misc, 1)
            pool.memset(v.inv_root_d[:], -0.5)
            pool.memset(v.identd[:], 0.0).then_inc(misc, 1)
            pool.wait_ge(misc, 2)
            for t in range(TOKT):
                pool.affine_select(out=v.lower[:, t], in_=v.lower[:, t], compare_op=ALU.is_gt, fill=0.0, base=0,
                                   pattern=[[1, NEXP], [-1, NEXP]], channel_multiplier=0)
            pool.affine_select(out=v.identd[:], in_=v.identd[:], compare_op=ALU.not_equal, fill=1.0, base=0,
                               pattern=[[-1, P]], channel_multiplier=1)

        @block.vector
        def _(dve):
            dve.wait_ge(g_loaded, 32)
            dve.tensor_copy(v.gateh[:], gstage[:]).then_inc(g_hi, 1)
            dve.wait_ge(g_hi, 1)
            dve.tensor_tensor(v.gatel[:], gstage[:], v.gateh[:].bitcast(F32), ALU.subtract)
            for n, (h, l, e) in enumerate(parts):
                dve.wait_ge(hi_done, n + 1)
                dve.tensor_tensor(l[:, e], stage[:, n % NST], h[:, e].bitcast(F32), ALU.subtract).then_inc(lo_done, 1)


def experts(nc, v, a, out, chunks):
    with ExitStack() as ctx:
        x = sbuf(nc, ctx, "d_x", [TOKW, TOKT, MODEL])
        acc = sbuf(nc, ctx, "d_acc", [TOKW, TOKT, MODEL])
        xsq = sbuf(nc, ctx, "d_xsq", [TOKW, TOKT, MODEL])
        ms = sbuf(nc, ctx, "d_ms", [TOKW, 3, TOKT])
        tn = sbuf(nc, ctx, "d_tn", [TOKW, TOKT, MODEL])
        tTh = sbuf(nc, ctx, "d_tTh", [P, KT, CHUNK], F32R)
        tTl = sbuf(nc, ctx, "d_tTl", [P, KT, CHUNK], F32R)
        lg = sbuf(nc, ctx, "d_lg", [TOKW, TOKT, NEXP])
        gt = sbuf(nc, ctx, "d_gt", [TOKW, TOKT, NEXP, NEXP])
        eqm = sbuf(nc, ctx, "d_eqm", [TOKW, TOKT, NEXP, NEXP])
        rank = sbuf(nc, ctx, "d_rank", [TOKW, TOKT, NEXP])
        sel = sbuf(nc, ctx, "d_sel", [TOKW, TOKT, NEXP])
        mx = sbuf(nc, ctx, "d_mx", [TOKW, TOKT])
        ex = sbuf(nc, ctx, "d_ex", [TOKW, TOKT, NEXP])
        exs = sbuf(nc, ctx, "d_exs", [TOKW, TOKT, NEXP])
        es = sbuf(nc, ctx, "d_es", [TOKW, 2, TOKT])
        cg = sbuf(nc, ctx, "d_cg", [TOKW, TOKT, NEXP])
        S = sbuf(nc, ctx, "d_S", [P, 3, CHUNK])
        Sh = sbuf(nc, ctx, "d_Sh", [P, 3, CHUNK], F32R)
        Sl = sbuf(nc, ctx, "d_Sl", [P, 3, CHUNK], F32R)
        ps = ctx.enter_context(nc.psum_tensor("psD", [P, 8, 512], F32))
        (x_loaded, b_loaded, x_sq, rms, tn_done, t_T, t_hi, t_lo, lg_done, gate, ex_done, hid_done, silu_done,
         s_hi, s_lo, y_done, acc_done, stored, rooted) = sems(
            nc, ctx, "d_x_loaded", "d_b_loaded", "d_x_sq", "d_rms", "d_tn_done", "d_t_T", "d_t_hi", "d_t_lo",
            "d_lg_done", "d_gate", "d_ex_done", "d_hid_done", "d_silu_done", "d_s_hi", "d_s_lo", "d_y_done",
            "d_acc_done", "d_stored", "d_rooted")
        block = ctx.enter_context(nc.Block())
        NB = NEXP * MT
        xs = a.xs.rearrange("(c t p) d -> c p t d", t=TOKT, p=TOKW)
        bs = a.bs.rearrange("(c t p) d -> c p t d", t=TOKT, p=TOKW)
        outc = out.rearrange("(c t p) d -> c p t d", t=TOKT, p=TOKW)

        def one(view, i):
            return view[bass.ds(i, 1)].rearrange("c p t d -> p (c t) d")

        @block.sync
        def _(sp):
            sp.dma_start(x[:], one(xs, 0)).then_inc(x_loaded, 16)
            sp.dma_start(acc[:], one(bs, 0)).then_inc(b_loaded, 16)
            with sp.Fori(1, chunks) as i:
                at = sp.snap(i)
                prev = sp.snap(i - 1)
                nx, nb_, no = one(xs, at), one(bs, at), one(outc, prev)
                sp.wait_ge(tn_done, TOKT * i)
                sp.dma_start(x[:], nx).then_inc(x_loaded, 16)
                sp.wait_ge(acc_done, NEXP * TOKT * i)
                sp.dma_start(no, acc[:]).then_inc(stored, 16)
                sp.wait_ge(stored, 16 * i)
                sp.dma_start(acc[:], nb_).then_inc(b_loaded, 16)
            sp.wait_ge(acc_done, NEXP * TOKT * chunks)
            sp.dma_start(one(outc, chunks - 1), acc[:]).then_inc(stored, 16)
            sp.wait_ge(stored, 16 * chunks)

        @block.gpsimd
        def _(pool):
            def root(j):
                pool.wait_ge(rms, j + 1)
                power(pool, ms[:, 2], ms[:, 1], v.inv_root_d).then_inc(rooted, 1)

            def chunk(i, more):
                for b in range(NB):
                    pool.wait_ge(s_hi, NB * i + b + 1)
                    pool.tensor_tensor(Sl[:, b % 3], S[:, b % 3], Sh[:, b % 3].bitcast(F32),
                                       ALU.subtract).then_inc(s_lo, 1)
                    if more and b == 17:
                        root(i + 1)

            root(0)
            with pool.Fori(0, chunks - 1) as i:
                chunk(i, True)
            chunk(chunks - 1, False)

        @block.scalar
        def _(act):
            def squares(j):
                act.wait_ge(x_loaded, 16 * j + 16)
                for t in range(TOKT):
                    act.activation(xsq[:, t], x[:, t], ACT.Square, accum_out=ms[:, 0, t:t + 1]).then_inc(x_sq, 1)

            def chunk(i, more):
                act.wait_ge(t_T, i + 1)
                act.activation(tTh[:], ps[:, 0:2, 0:CHUNK], ACT.Copy).then_inc(t_hi, 1)
                act.wait_ge(gate, GATE_STEPS * i + 4)
                act.activation(ex[:], exs[:], ACT.Exp).then_inc(ex_done, 1)
                for b in range(NB):
                    act.wait_ge(hid_done, NB * i + b + 1)
                    act.activation(S[:, b % 3], ps[:, b % 3, 0:CHUNK], ACT.Silu).then_inc(silu_done, 1)
                    if more and b == 12:
                        squares(i + 1)

            squares(0)
            with act.Fori(0, chunks - 1) as i:
                chunk(i, True)
            chunk(chunks - 1, False)

        @block.vector
        def _(dve):
            def mean_square(j):
                dve.wait_ge(x_sq, TOKT * j + TOKT)
                dve.tensor_scalar(ms[:, 1], ms[:, 0], 1.0 / MODEL, RMS_EPS, ALU.mult, ALU.add).then_inc(rms, 1)

            def rms_norm(j, first=False):
                dve.wait_ge(rooted, j + 1)
                if not first:
                    dve.wait_ge(t_T, j)
                for t in range(TOKT):
                    dve.scalar_tensor_tensor(tn[:, t], x[:, t], ms[:, 2, t:t + 1], v.g2[:], ALU.mult,
                                             ALU.mult).then_inc(tn_done, 1)

            def chunk(i, more):
                dve.wait_ge(t_hi, i + 1)
                dve.tensor_tensor(tTl[:], ps[:, 0:2, 0:CHUNK], tTh[:].bitcast(F32), ALU.subtract).then_inc(t_lo, 1)
                g = GATE_STEPS * i
                dve.wait_ge(lg_done, i + 1)
                dve.tensor_copy(lg[:], ps[0:TOKW, 2, 0:TOKT * NEXP].rearrange("p (t e) -> p t e", t=TOKT))\
                    .then_inc(gate, 1)
                dve.wait_ge(gate, g + 1)
                one_e = lg[:].unsqueeze(3).to_broadcast([TOKW, TOKT, NEXP, NEXP])
                other = lg[:].unsqueeze(2).to_broadcast([TOKW, TOKT, NEXP, NEXP])
                dve.tensor_reduce(mx[:], lg[:], AX.X, ALU.max).then_inc(gate, 1)
                dve.tensor_tensor(gt[:], other, one_e, ALU.is_gt).then_inc(gate, 1)
                dve.wait_ge(gate, g + 2)
                dve.tensor_tensor(exs[:], lg[:], mx[:].unsqueeze(2).to_broadcast([TOKW, TOKT, NEXP]),
                                  ALU.subtract).then_inc(gate, 1)
                dve.tensor_tensor(eqm[:], other, one_e, ALU.is_equal).then_inc(gate, 1)
                dve.wait_ge(gate, g + 5)
                dve.tensor_tensor(eqm[:], eqm[:], v.lower[:], ALU.mult).then_inc(gate, 1)
                dve.wait_ge(gate, g + 6)
                dve.tensor_tensor(gt[:], gt[:], eqm[:], ALU.add).then_inc(gate, 1)
                dve.wait_ge(gate, g + 7)
                dve.tensor_reduce(rank[:], gt[:], AX.X, ALU.add).then_inc(gate, 1)
                dve.wait_ge(gate, g + 8)
                dve.tensor_scalar(sel[:], rank[:], 2.0, None, ALU.is_lt).then_inc(gate, 1)
                dve.wait_ge(gate, g + 9)
                dve.wait_ge(ex_done, i + 1)
                dve.tensor_tensor(exs[:], ex[:], sel[:], ALU.mult).then_inc(gate, 1)
                dve.wait_ge(gate, g + 10)
                dve.tensor_reduce(es[:, 0], exs[:], AX.X, ALU.add).then_inc(gate, 1)
                dve.wait_ge(gate, g + 11)
                dve.reciprocal(es[:, 1], es[:, 0]).then_inc(gate, 1)
                dve.wait_ge(gate, g + 12)
                dve.tensor_tensor(cg[:], exs[:], es[:, 1].unsqueeze(2).to_broadcast([TOKW, TOKT, NEXP]),
                                  ALU.mult).then_inc(gate, 1)

                def add_expert(e):
                    dve.wait_ge(y_done, NEXP * i + e + 1)
                    if e:
                        dve.wait_ge(acc_done, NEXP * TOKT * i + TOKT * e)
                    for t in range(TOKT):
                        bank = 4 + 2 * (e % 2) + t // 2
                        dve.scalar_tensor_tensor(acc[:, t], ps[0:TOKW, bank, (t % 2) * MODEL:(t % 2 + 1) * MODEL],
                                                 cg[:, t, e:e + 1], acc[:, t], ALU.mult, ALU.add).then_inc(acc_done, 1)

                dve.wait_ge(gate, g + 13)
                dve.wait_ge(b_loaded, 16 * i + 16)
                for b in range(NB):
                    dve.wait_ge(silu_done, NB * i + b + 1)
                    dve.tensor_copy(Sh[:, b % 3], S[:, b % 3]).then_inc(s_hi, 1)
                    if b % MT == 1 and b >= MT:
                        add_expert(b // MT - 1)
                    if more and b == 16:
                        mean_square(i + 1)
                    if more and b == 20:
                        rms_norm(i + 1)
                add_expert(NEXP - 1)

            mean_square(0)
            rms_norm(0, first=True)
            with dve.Fori(0, chunks - 1) as i:
                chunk(i, True)
            chunk(chunks - 1, False)

        @block.tensor
        def _(pe):
            def mm3(out, lh, ll, rh, rl, start, stop, lone=True):
                pe.matmul(out, lh, rh, start=start, stop=False, skip_group_check=not lone)
                pe.matmul(out, ll, rh, start=False, stop=False, skip_group_check=not lone)
                return pe.matmul(out, lh, rl, start=False, stop=stop, skip_group_check=not lone)

            with pe.Fori(0, chunks) as i:
                pe.wait_ge(tn_done, TOKT * i + TOKT)
                for k in range(KT):
                    for t in range(TOKT):
                        last = pe.transpose(ps[:, k, t * TOKW:(t + 1) * TOKW], tn[:, t, k * P:(k + 1) * P],
                                            v.identd[0:TOKW, 0:TOKW])
                last.then_inc(t_T, 1)
                pe.wait_ge(t_lo, i + 1)
                for t in range(TOKT):
                    c = slice(t * TOKW, (t + 1) * TOKW)
                    for k in range(KT):
                        last = mm3(ps[0:TOKW, 2, t * NEXP:(t + 1) * NEXP], tTh[:, k, c], tTl[:, k, c],
                                   v.gateh[:, k, :], v.gatel[:, k, :], k == 0, k == KT - 1)
                last.then_inc(lg_done, 1)
                pe.wait_ge(gate, GATE_STEPS * i + 1)

                def hidden(b):
                    e, m = divmod(b, MT)
                    if b >= 3:
                        pe.wait_ge(silu_done, NB * i + b - 2)
                    for k in range(KT):
                        c = slice(k * HID + m * P, k * HID + (m + 1) * P)
                        last = mm3(ps[:, b % 3, 0:CHUNK], v.w1h[:, e, c], v.w1l[:, e, c], tTh[:, k, :], tTl[:, k, :],
                                   k == 0, k == KT - 1)
                    last.then_inc(hid_done, 1)

                def output(b):
                    e, m = divmod(b, MT)
                    pe.wait_ge(s_lo, NB * i + b + 1)
                    if m == 0 and e >= 2:
                        pe.wait_ge(acc_done, NEXP * TOKT * i + TOKT * (e - 1))
                    w = slice(m * MODEL, (m + 1) * MODEL)
                    for t in range(TOKT):
                        c = slice(t * TOKW, (t + 1) * TOKW)
                        bank = 4 + 2 * (e % 2) + t // 2
                        last = mm3(ps[0:TOKW, bank, (t % 2) * MODEL:(t % 2 + 1) * MODEL], Sh[:, b % 3, c],
                                   Sl[:, b % 3, c], v.w2h[:, e, w], v.w2l[:, e, w], m == 0 and t % 2 == 0,
                                   m == MT - 1, lone=False)
                    if m == MT - 1:
                        last.then_inc(y_done, 1)

                hidden(0)
                hidden(1)
                for b in range(NB):
                    if b + 2 < NB:
                        hidden(b + 2)
                    output(b)


GATE_STEPS = 13


def build(nc, a, out):
    nb = a.x.shape[0]
    v = Names()
    with ExitStack() as ctx:
        v.cls_row = sbuf(nc, ctx, "cls_row", [1, MODEL])
        v.cls32 = sbuf(nc, ctx, "cls32", [32, MODEL])
        v.wqk = sbuf(nc, ctx, "wqk", [P, KT, 512])
        v.wv = sbuf(nc, ctx, "wv", [P, KT, 1024])
        v.wkv_bd = sbuf(nc, ctx, "wkv_bd", [P, 2 * P])
        v.wq_bd = sbuf(nc, ctx, "wq_bd", [P, P])
        v.outw = sbuf(nc, ctx, "outw", [P, 2, MODEL])
        v.wout = sbuf(nc, ctx, "wout", [P, PAIRS, MODEL])
        v.wq2 = sbuf(nc, ctx, "wq2", [P, KT, MODEL])
        v.wdkv = sbuf(nc, ctx, "wdkv", [P, KT, P])
        v.wukv = sbuf(nc, ctx, "wukv", [P, 2 * MODEL])
        v.wo = sbuf(nc, ctx, "wo", [P, KT, MODEL])
        v.g_ln = sbuf(nc, ctx, "g_ln", [P, MODEL])
        v.b_ln = sbuf(nc, ctx, "b_ln", [P, MODEL])
        v.g1 = sbuf(nc, ctx, "g1b", [P, MODEL])
        v.inv_root = sbuf(nc, ctx, "inv_root", [P, 1])
        v.root = sbuf(nc, ctx, "root", [P, 1])
        v.nbq = sbuf(nc, ctx, "nbq", [P, 1])
        v.biasr = sbuf(nc, ctx, "biasr", [P, 768], BF16)
        v.ones_bf = sbuf(nc, ctx, "ones_bf", [P, P], BF16)
        v.ident = sbuf(nc, ctx, "ident", [P, P])
        v.ident_r = sbuf(nc, ctx, "ident_r", [P, P], F32R)
        v.ident_bf = sbuf(nc, ctx, "ident_bf", [P, P], BF16)
        v.causal = sbuf(nc, ctx, "causal", [P, P + 2], BF16)
        v.half1 = sbuf(nc, ctx, "half1", [P, P])
        v.bmask = sbuf(nc, ctx, "bmask", [HEADS, HEADS, DV])
        v.sel = sbuf(nc, ctx, "sel", [HEADS, HEADS, 32], F32R)
        v.wo_pad = sbuf(nc, ctx, "wo_pad", [P, GROUPS, MODEL])
        v.zero_bf = sbuf(nc, ctx, "zero_bf", [1, 512], BF16)
        v.bmask_r = sbuf(nc, ctx, "bmask_r", [8, 8 * DV], F32R)
        v.kmask = sbuf(nc, ctx, "kmask", [P, PAIRS, HEADS])
        v.ewT = sbuf(nc, ctx, "ewT", [P, LT, L])
        v.kcls_bd = sbuf(nc, ctx, "kcls_bd", [P, PAIRS, HEADS], F32R)
        v.vcls_bd = sbuf(nc, ctx, "vcls_bd", [HEADS, 1024])
        v.QT = sbuf(nc, ctx, "QT", [P, PAIRS, QCOLS], F32R)
        v.oclsT = sbuf(nc, ctx, "oclsT", [P, PAIRS, nb])
        v.kclsT = sbuf(nc, ctx, "kclsT", [P, PAIRS, nb], F32R)
        load_constants(nc, v, a)
        mixer_and_attention(nc, v, a, nb)
        class_tokens(nc, v, a, nb)
        latent_attention(nc, v, a, nb)
    with ExitStack() as ctx:
        v.identd = sbuf(nc, ctx, "identd", [P, P])
        v.lower = sbuf(nc, ctx, "lower", [TOKW, TOKT, NEXP, NEXP])
        v.inv_root_d = sbuf(nc, ctx, "inv_root_d", [P, 1])
        v.g2 = sbuf(nc, ctx, "g2b", [TOKW, MODEL])
        v.gateh = sbuf(nc, ctx, "gateh", [P, KT, NEXP], F32R)
        v.gatel = sbuf(nc, ctx, "gatel", [P, KT, NEXP], F32R)
        v.w1h, v.w1l, v.w2h, v.w2l = [sbuf(nc, ctx, n, [P, NEXP, KT * HID], F32R)
                                      for n in ("w1h", "w1l", "w2h", "w2l")]
        load_experts(nc, v, a)
        experts(nc, v, a, out, a.xs.shape[0] // CHUNK)


def kernel(**inputs):
    import concourse.bacc as bacc
    from concourse.bass_utils import run_bass_kernel_spmd as run

    g = {n: np.asarray(x) for n, x in inputs.items()}
    wkv = g["L0_attn_Wkv"].reshape(MODEL, HEADS, DK + DV)
    wk, wv = wkv[:, :, :DK].reshape(MODEL, HEADS * DK), wkv[:, :, DK:].reshape(MODEL, HEADS * DV)
    arrays = {
        "x": g["x"], "cls_tok": g["cls_tok"].reshape(1, MODEL),
        "wqT": g["L0_tok_Wq_w"].T, "wkT": g["L0_tok_Wk_w"].T, "wvT": g["L0_tok_Wv_w"].T,
        "bq": g["L0_tok_Wq_b"].reshape(F, 1), "bk": g["L0_tok_Wk_b"].reshape(1, F),
        "bv": g["L0_tok_Wv_b"].reshape(1, F),
        "w_bias": g["L0_tok_w_bias"], "local_mask": g["L0_tok_local_mask"],
        "out_w": g["L0_tok_out_w"], "out_b": g["L0_tok_out_b"].reshape(1, MODEL),
        "ln_g": g["L0_tok_ln_g"].reshape(1, MODEL), "ln_b": g["L0_tok_ln_b"].reshape(1, MODEL),
        "wqk": np.concatenate([g["L0_attn_Wq"], wk], axis=1), "wv": wv, "wout": g["L0_attn_Wout"],
        "g1": g["L0_ffn_g1"].reshape(1, MODEL), "ffn_wq": g["L0_ffn_Wq"], "wdkv": g["L0_ffn_Wdkv"],
        "wukv": np.concatenate([g["L0_ffn_Wuk"], g["L0_ffn_Wuv"]], axis=1), "wo": g["L0_ffn_Wo"],
        "g2": g["L0_ffn_g2"].reshape(1, MODEL), "gate_w": g["L0_ffn_gate_w"], "w1": g["L0_ffn_w1"],
        "w2": g["L0_ffn_w2"],
    }
    nb = g["x"].shape[0]
    rows = -(-nb * SEQ // CHUNK) * CHUNK
    nc = bacc.Bacc("TRN2", target_bir_lowering=False, num_devices=1)
    args, launched = {}, {}
    for name, x in arrays.items():
        x = np.ascontiguousarray(x)
        launched["in_" + name] = x
        args[name] = nc.dram_tensor("in_" + name, x.shape, mybir.dt.from_np(x.dtype), kind="ExternalInput").ap()
    a = Names()
    a.x = args["x"]
    a.cls_tok = args["cls_tok"]
    a.wqT = args["wqT"]
    a.wkT = args["wkT"]
    a.wvT = args["wvT"]
    a.bq = args["bq"]
    a.bk = args["bk"]
    a.bv = args["bv"]
    a.w_bias = args["w_bias"]
    a.local_mask = args["local_mask"]
    a.out_w = args["out_w"]
    a.out_b = args["out_b"]
    a.ln_g = args["ln_g"]
    a.ln_b = args["ln_b"]
    a.wqk = args["wqk"]
    a.wv = args["wv"]
    a.wout = args["wout"]
    a.g1 = args["g1"]
    a.ffn_wq = args["ffn_wq"]
    a.wdkv = args["wdkv"]
    a.wukv = args["wukv"]
    a.wo = args["wo"]
    a.g2 = args["g2"]
    a.gate_w = args["gate_w"]
    a.w1 = args["w1"]
    a.w2 = args["w2"]
    a.xs = nc.dram_tensor("xs", (rows, MODEL), F32, kind="Internal").ap()
    a.bs = nc.dram_tensor("bs", (rows, MODEL), F32, kind="Internal").ap()
    a.hs = nc.dram_tensor("hs", (nb, P, LT * MODEL), F32, kind="Internal").ap()
    a.vcls_attn = nc.dram_tensor("vcls_attn", (1, HEADS * DV), F32, kind="Internal").ap()
    a.vcls_mla = nc.dram_tensor("vcls_mla", (nb, MODEL), F32, kind="Internal").ap()
    out = nc.dram_tensor("out_rows", (rows, MODEL), F32, kind="ExternalOutput").ap()
    build(nc, a, out)
    r = run(nc, [launched], core_ids=[0])
    return r.results[0]["out_rows"][:nb * SEQ].reshape(nb, SEQ, MODEL)
```
